# Optimizing a Trainium2 kernel written in Bass

```python
import numpy as np
import jax
import jax.numpy as jnp

def _softmax(x, axis=-1):
    return jax.nn.softmax(x, axis=axis)

def _gelu(x):
    return jax.nn.gelu(x, approximate=True)

def _silu(x):
    return jax.nn.silu(x)

def _sigmoid(x):
    return jax.nn.sigmoid(x)

def _layernorm(x, axis=-1, eps=1e-05):
    m = jnp.mean(x, axis=axis, keepdims=True)
    v = jnp.var(x, axis=axis, keepdims=True)
    return (x - m) / jnp.sqrt(v + eps)

def _scatter_add(tgt, idx, src, axis=0):
    return tgt.at[idx].add(src)

def _segment_sum(src, seg, n):
    return jax.ops.segment_sum(src, seg, n)
kernel_name = 'mk_adj_ffn_d2_adj_r2_7bce83'

def setup_inputs(seed: int=0):
    np.random.seed(seed)
    _w = jnp.asarray

    def _rec_inputs():
        import jax
        import jax.numpy as jnp
        _gk = jax.random.key(seed)
        x = 7.22e-05 + 1 * jax.random.normal(jax.random.fold_in(_gk, 1), (128, 64, 256), jnp.float32)
        _w = (1.0 + jnp.arange(64, dtype=jnp.float32)) ** (-0.5)
        _w = _w / _w.mean()
        _pij = jnp.clip(0.0625 * _w[:, None] * _w[None, :], 0.0, 1.0)
        _a = jax.random.uniform(jax.random.fold_in(_gk, 2), (128, 64, 64)) < _pij
        _a = jnp.logical_or(_a, jnp.eye(64, dtype=bool))
        _af = _a.astype(jnp.float32)
        _af = _af * jax.random.uniform(jax.random.fold_in(_gk, 3), (128, 64, 64), jnp.float32, 0.05, 1)
        adj = _af
        _nm = jnp.ones((128, 64), dtype=bool)
        nodemask = jnp.where(_nm, 1.0, 0.0).astype(jnp.float32)
        return (x, adj, nodemask)
    x, adj, nodemask = _rec_inputs()

    def _L0_gnn_setup():
        import jax, jax.numpy as jnp
        import numpy as np
        B, N, IN_DIM, ATT_DIM = (2, 4096, 256, 256)
        key = jax.random.key(seed)
        k1, k2, k3, k4 = jax.random.split(key, 4)
        X = jax.random.normal(k1, (B, N, IN_DIM), dtype=jnp.float32)
        adj = jax.random.uniform(k2, (B, N, N), dtype=jnp.float32)
        mask = jnp.ones((B, N), dtype=jnp.float32)
        Wqk = jax.random.normal(k3, (IN_DIM, 2 * ATT_DIM), dtype=jnp.float32) / np.sqrt(IN_DIM)
        Wv = jax.random.normal(k4, (IN_DIM, IN_DIM), dtype=jnp.float32) / np.sqrt(IN_DIM)
        return {'X': X, 'adj': adj, 'mask': mask, 'Wqk': Wqk, 'Wv': Wv}
    _L0_gnn_all = _L0_gnn_setup()
    _L0_gnn_in = {k: v for k, v in _L0_gnn_all.items() if k in ('Wqk', 'Wv')}
    del _L0_gnn_all

    def _L0_ffn_setup():
        import jax, jax.numpy as jnp
        import numpy as np
        ROUTER_JITTER = 0.01
        NEG_INF = -jnp.inf

        def _sparsemixer_eval(scores, num_experts):
            eids = jnp.arange(num_experts)
            max1 = jnp.max(scores, axis=-1, keepdims=True)
            sel1 = jnp.argmax(scores, axis=-1)
            factor1 = jnp.maximum(jnp.abs(scores), max1)
            mask1 = (max1 - scores) / factor1 > 2.0 * ROUTER_JITTER
            mg1 = jnp.where(mask1, NEG_INF, scores)
            p1 = jax.nn.softmax(mg1, axis=-1)
            mult1 = jnp.take_along_axis(p1, sel1[:, None], axis=-1)[:, 0]
            oh1 = sel1[:, None] == eids[None, :]
            masked_scores = jnp.where(oh1, NEG_INF, scores)
            max2 = jnp.max(masked_scores, axis=-1, keepdims=True)
            sel2 = jnp.argmax(masked_scores, axis=-1)
            factor2 = jnp.maximum(jnp.abs(scores), max2)
            mask2 = (max2 - scores) / factor2 > 2.0 * ROUTER_JITTER
            mg2 = jnp.where(mask2, NEG_INF, masked_scores)
            p2 = jax.nn.softmax(mg2, axis=-1)
            mult2 = jnp.take_along_axis(p2, sel2[:, None], axis=-1)[:, 0]
            weights = jnp.stack([mult1, mult2], axis=-1)
            experts = jnp.stack([sel1, sel2], axis=-1)
            return (weights, experts)
        B, S, H, F, E = (2, 1024, 256, 512, 8)
        key = jax.random.key(seed)
        ks = jax.random.split(key, 6)
        scale_h = 1.0 / np.sqrt(H)
        scale_f = 1.0 / np.sqrt(F)
        return {'x': jax.random.normal(ks[0], (B, S, H), dtype=jnp.float32), 'wg': jax.random.normal(ks[1], (H, E), dtype=jnp.float32) * scale_h, 'bg': jax.random.normal(ks[2], (E,), dtype=jnp.float32) * 0.01, 'w1': jax.random.normal(ks[3], (E, H, F), dtype=jnp.float32) * scale_h, 'w3': jax.random.normal(ks[4], (E, H, F), dtype=jnp.float32) * scale_h, 'w2': jax.random.normal(ks[5], (E, F, H), dtype=jnp.float32) * scale_f}
    _L0_ffn_all = _L0_ffn_setup()
    _L0_ffn_in = {k: v for k, v in _L0_ffn_all.items() if k in ('wg', 'bg', 'w1', 'w3', 'w2')}
    del _L0_ffn_all

    def _L1_gnn_setup():
        import jax, jax.numpy as jnp
        import numpy as np
        B, N, F_IN, F_HID, F_OUT = (32, 512, 256, 256, 256)

        def _gcn_layer(x, adj, W, b):
            support = jnp.einsum('bnf,fh->bnh', x, W)
            return jnp.einsum('bnm,bmh->bnh', adj, support) + b
        key = jax.random.key(seed)
        ks = jax.random.split(key, 8)

        def xavier(k, fan_in, fan_out):
            bound = float(np.sqrt(6.0 / (fan_in + fan_out)))
            return jax.random.uniform(k, (fan_in, fan_out), jnp.float32, -bound, bound)
        return {'batch_graph': jax.random.normal(ks[0], (B, N, F_IN), jnp.float32), 'adj': jax.random.uniform(ks[1], (B, N, N), jnp.float32), 'W1': xavier(ks[2], F_IN, F_HID), 'b1': jnp.zeros((F_HID,), jnp.float32), 'W2': xavier(ks[3], F_HID, F_HID), 'b2': jnp.zeros((F_HID,), jnp.float32), 'W3': xavier(ks[4], F_HID, F_OUT), 'b3': jnp.zeros((F_OUT,), jnp.float32)}
    _L1_gnn_all = _L1_gnn_setup()
    _L1_gnn_in = {k: v for k, v in _L1_gnn_all.items() if k in ('W1', 'b1', 'W2', 'b2', 'W3', 'b3')}
    del _L1_gnn_all

    def _L1_ffn_setup():
        import jax, jax.numpy as jnp
        import numpy as np
        B, S, D, E, O = (512, 128, 256, 16, 256)
        key = jax.random.key(seed)
        k_x, k_wg, k_bg, k_we, k_be = jax.random.split(key, 5)
        scale_g = 1.0 / np.sqrt(D)
        scale_e = 1.0 / np.sqrt(D)
        return {'x': jax.random.normal(k_x, (B, S, D), dtype=jnp.float32), 'Wg': jax.random.uniform(k_wg, (D, E), jnp.float32, -scale_g, scale_g), 'bg': jax.random.uniform(k_bg, (E,), jnp.float32, -scale_g, scale_g), 'We': jax.random.uniform(k_we, (E, D, O), jnp.float32, -scale_e, scale_e), 'be': jax.random.uniform(k_be, (E, O), jnp.float32, -scale_e, scale_e)}
    _L1_ffn_all = _L1_ffn_setup()
    _L1_ffn_in = {k: v for k, v in _L1_ffn_all.items() if k in ('Wg', 'bg', 'We', 'be')}
    del _L1_ffn_all
    return {'x': x, 'adj': adj, 'nodemask': nodemask, 'L0_gnn_Wqk': _L0_gnn_in['Wqk'], 'L0_gnn_Wv': _L0_gnn_in['Wv'], 'L0_ffn_wg': _L0_ffn_in['wg'], 'L0_ffn_bg': _L0_ffn_in['bg'], 'L0_ffn_w1': _L0_ffn_in['w1'], 'L0_ffn_w3': _L0_ffn_in['w3'], 'L0_ffn_w2': _L0_ffn_in['w2'], 'L1_gnn_W1': _L1_gnn_in['W1'], 'L1_gnn_b1': _L1_gnn_in['b1'], 'L1_gnn_W2': _L1_gnn_in['W2'], 'L1_gnn_b2': _L1_gnn_in['b2'], 'L1_gnn_W3': _L1_gnn_in['W3'], 'L1_gnn_b3': _L1_gnn_in['b3'], 'L1_ffn_Wg': _L1_ffn_in['Wg'], 'L1_ffn_bg': _L1_ffn_in['bg'], 'L1_ffn_We': _L1_ffn_in['We'], 'L1_ffn_be': _L1_ffn_in['be']}

def reference(x, adj, nodemask, L0_gnn_Wqk, L0_gnn_Wv, L0_ffn_wg, L0_ffn_bg, L0_ffn_w1, L0_ffn_w3, L0_ffn_w2, L1_gnn_W1, L1_gnn_b1, L1_gnn_W2, L1_gnn_b2, L1_gnn_W3, L1_gnn_b3, L1_ffn_Wg, L1_ffn_bg, L1_ffn_We, L1_ffn_be):
    import jax
    import jax.numpy as jnp

    def _L0_gnn_ref(X, adj, mask, Wqk, Wv):
        import jax, jax.numpy as jnp
        import numpy as np
        B, N, IN_DIM, ATT_DIM = (2, 4096, 256, 256)
        qk = X @ Wqk
        q, k = jnp.split(qk, 2, axis=-1)
        v = X @ Wv
        att_dim = q.shape[-1]
        inv_scale = 1.0 / jnp.sqrt(jnp.float32(att_dim))
        k_m = k * mask[:, :, None]
        agg = jnp.einsum('bij,bjd->bid', adj, k_m)
        w = inv_scale * mask * jnp.einsum('bid,bid->bi', q, agg)
        L = jax.nn.softmax(w, axis=1)[:, :, None] * v
        return L

    def _L0_ffn_ref(x, wg, bg, w1, w3, w2):
        import jax, jax.numpy as jnp
        import numpy as np
        ROUTER_JITTER = 0.01
        NEG_INF = -jnp.inf

        def _sparsemixer_eval(scores, num_experts):
            eids = jnp.arange(num_experts)
            max1 = jnp.max(scores, axis=-1, keepdims=True)
            sel1 = jnp.argmax(scores, axis=-1)
            factor1 = jnp.maximum(jnp.abs(scores), max1)
            mask1 = (max1 - scores) / factor1 > 2.0 * ROUTER_JITTER
            mg1 = jnp.where(mask1, NEG_INF, scores)
            p1 = jax.nn.softmax(mg1, axis=-1)
            mult1 = jnp.take_along_axis(p1, sel1[:, None], axis=-1)[:, 0]
            oh1 = sel1[:, None] == eids[None, :]
            masked_scores = jnp.where(oh1, NEG_INF, scores)
            max2 = jnp.max(masked_scores, axis=-1, keepdims=True)
            sel2 = jnp.argmax(masked_scores, axis=-1)
            factor2 = jnp.maximum(jnp.abs(scores), max2)
            mask2 = (max2 - scores) / factor2 > 2.0 * ROUTER_JITTER
            mg2 = jnp.where(mask2, NEG_INF, masked_scores)
            p2 = jax.nn.softmax(mg2, axis=-1)
            mult2 = jnp.take_along_axis(p2, sel2[:, None], axis=-1)[:, 0]
            weights = jnp.stack([mult1, mult2], axis=-1)
            experts = jnp.stack([sel1, sel2], axis=-1)
            return (weights, experts)
        B, S, H = x.shape
        E = w1.shape[0]
        xt = x.reshape(-1, H)
        scores = jax.nn.softmax(xt @ wg + bg, axis=-1)
        routing_weights, selected_experts = _sparsemixer_eval(scores, E)
        eids = jnp.arange(E)
        comb = jnp.sum(routing_weights[:, :, None] * (selected_experts[:, :, None] == eids[None, None, :]).astype(xt.dtype), axis=1)
        out = jnp.zeros_like(xt)
        for e in range(E):
            h = jax.nn.gelu(xt @ w1[e], approximate=False) * (xt @ w3[e])
            out = out + comb[:, e:e + 1] * (h @ w2[e])
        return out.reshape(B, S, H)

    def _L1_gnn_ref(batch_graph, adj, W1, b1, W2, b2, W3, b3):
        import jax, jax.numpy as jnp
        import numpy as np
        B, N, F_IN, F_HID, F_OUT = (32, 512, 256, 256, 256)

        def _gcn_layer(x, adj, W, b):
            support = jnp.einsum('bnf,fh->bnh', x, W)
            return jnp.einsum('bnm,bmh->bnh', adj, support) + b
        x = jax.nn.relu(_gcn_layer(batch_graph, adj, W1, b1))
        x = jax.nn.relu(_gcn_layer(x, adj, W2, b2))
        out = _gcn_layer(x, adj, W3, b3)
        return out

    def _L1_ffn_ref(x, Wg, bg, We, be):
        import jax, jax.numpy as jnp
        import numpy as np
        B, S, D, E, O = (512, 128, 256, 16, 256)
        scores = jax.nn.softmax(jnp.mean(x, axis=1) @ Wg + bg, axis=-1)
        idx = jnp.argmax(scores, axis=-1)
        gate = jnp.take_along_axis(scores, idx[:, None], axis=-1)
        W_sel = We[idx]
        b_sel = be[idx]
        y = jnp.einsum('bsd,bdo->bso', x, W_sel) + b_sel[:, None, :]
        return gate[:, :, None] * y
    x = x + _L0_gnn_ref(_layernorm(x, axis=-1), adj, nodemask, L0_gnn_Wqk, L0_gnn_Wv)
    x = x + _L0_ffn_ref(_layernorm(x, axis=-1), L0_ffn_wg, L0_ffn_bg, L0_ffn_w1, L0_ffn_w3, L0_ffn_w2)
    x = x + _L1_gnn_ref(_layernorm(x, axis=-1), adj, L1_gnn_W1, L1_gnn_b1, L1_gnn_W2, L1_gnn_b2, L1_gnn_W3, L1_gnn_b3)
    x = x + _L1_ffn_ref(_layernorm(x, axis=-1), L1_ffn_Wg, L1_ffn_bg, L1_ffn_We, L1_ffn_be)
    return x

_drawn_inputs = setup_inputs


def setup_inputs(seed=0):
    import zlib

    import numpy as np

    out = dict(_drawn_inputs(seed))
    spreads = {'L1_gnn_b1': (0.0, 0.1), 'L1_gnn_b2': (0.0, 0.1), 'L1_gnn_b3': (0.0, 0.392)}
    factors = {'L1_ffn_Wg': 3.998, 'L1_ffn_bg': 29.384, 'L1_ffn_We': 3.917, 'L1_ffn_be': 8.0}
    for name, (base, spread) in spreads.items():
        noise = np.random.default_rng([zlib.crc32(name.encode()), seed]).standard_normal(out[name].shape)
        drawn = base * np.exp(spread * noise) if base else spread * noise
        out[name] = jnp.asarray(drawn.astype(out[name].dtype))
    for name, factor in factors.items():
        out[name] = (out[name] * factor).astype(out[name].dtype)
    return out
```

```python
from contextlib import ExitStack

import concourse.bass as bass
from concourse import mybir
from concourse.bass import IndirectOffsetOnAxis, ds

F32 = mybir.dt.float32
I32 = mybir.dt.int32
U32 = mybir.dt.uint32
ALU = mybir.AluOpType
ACT = mybir.ActivationFunctionType
AX = mybir.AxisListType

P = 128
GRAPHS, NODES, D = 128, 64, 256
TOKENS = GRAPHS * NODES
TILES = TOKENS // P
GT = 4
GROUPS = TILES // GT
KD = D // P
E0, F0 = 8, 512
KF = F0 // P
E1 = 16
HALVES = 2
HT = TILES // HALVES
HG = GROUPS // HALVES
ROUTED = (2 * HT * P + E0 * (P - 1)) // P
ITEMS = HALVES * ROUTED
EPS = 1e-5
JITTER2 = 2.0 * 0.01
ATT_SCALE = 1.0 / float(D) ** 0.5

CONST = {}
_at = 0
for _name, _n in (("ident", P), ("before", P), ("ones", P), ("half_of", P), ("own_tile", GT),
                  ("rev0", E0), ("rev1", E1), ("restart", E0 * HT), ("tile_start", ROUTED),
                  ("eps", GT), ("minus_half", GT)):
    CONST[_name] = (_n, _at)
    _at += _n
CONST_COLS = _at


def wait(eng, sem, value):
    if isinstance(value, int) and value <= 0:
        return
    eng.wait_ge(sem, value)


class At:

    def __init__(self, h, parity, shift=0):
        self.n = 2 * h + parity + shift
        self.slot = (parity + shift) % 2
        self.used = h + (parity + shift) // 2


def straight(first, last, body):
    for k in range(first, last):
        body(k // 2, k % 2)


def looped(eng, first, last, body):
    with eng.Fori(first // 2, last // 2, 1) as h:
        body(h, 0)
        body(h, 1)


def program(nc, x, adjT, maskT, wqkT, wv, wg0, bg0, w1, w3, w2, gw, gb, wg1, bg1, we, be, const, out):
    ctx = ExitStack()
    with ctx:
        def sb(name, shape, dt=F32):
            return ctx.enter_context(nc.sbuf_tensor(name, shape, dt))

        def sem(name):
            return ctx.enter_context(nc.semaphore(name))

        def dram(name, rows):
            return nc.dram_tensor(name, [rows, D], F32, kind="Internal").ap()

        x1_dram = dram("x1_dram", TOKENS)
        n1_dram = dram("n1_dram", TOKENS)
        xs_dram = dram("xs_dram", ITEMS * P)
        ys_dram = dram("ys_dram", ITEMS * P)

        big = sb("big", [P, E0 * (2 * KD * F0 + KF * D)])
        mid = sb("mid", [P, 14336])
        cst = sb("cst", [P, CONST_COLS])
        mask = sb("mask", [P, TILES])
        mp = sb("mp", [P, KD, D])
        wv_sb = sb("wv_sb", [P, KD, D])
        wg0_sb = sb("wg0_sb", [P, KD, E0])
        bg0_sb = sb("bg0_sb", [P, E0])
        gw_sb = sb("gw_sb", [P, 3, KD, D])
        gb_sb = sb("gb_sb", [P, 3, D])
        wg1_sb = sb("wg1_sb", [P, KD, E1])
        bg1_sb = sb("bg1_sb", [2 * GT, E1])
        zero = sb("zero", [P, D])

        def const_of(name, rows=P):
            n, at = CONST[name]
            return cst[0:rows, at:at + n]

        ident = const_of("ident")

        class Carve:

            def __init__(self, buf):
                self.buf, self.at = buf, 0

            def __call__(self, n, pattern=None, **sizes):
                part = self.buf[:, self.at:self.at + n]
                self.at += n
                return part.rearrange(pattern, **sizes) if pattern else part

        c = Carve(mid)
        adj_sb = c(2 * GT * P, "p (s j n) -> p s j n", s=2, j=GT)
        xin = c(2 * GT * D, "p (s j n) -> p s j n", s=2, j=GT)
        xn = c(2 * GT * D, "p (s j n) -> p s j n", s=2, j=GT)
        tt = c(GT * 2 * D, "p (j a k n) -> p j a k n", j=GT, a=2, k=KD)
        v_sb = c(2 * GT * D, "p (s j n) -> p s j n", s=2, j=GT)
        x1 = c(2 * GT * D, "p (s j n) -> p s j n", s=2, j=GT)
        n1 = c(2 * GT * D, "p (s j n) -> p s j n", s=2, j=GT)
        n1T = c(GT * D, "p (j k n) -> p j k n", j=GT, k=KD)
        assert c.at <= 14336, c.at
        wqk_stage = tt.rearrange("p j a k n -> p (j a k n)")[:, 0:4 * D]\
            .rearrange("p (h k n) -> p h k n", h=2, k=KD)
        c = Carve(big)
        w13_sb = [c(E0 * KD * F0) for _ in range(2)]
        w2_sb = c(E0 * KF * D)
        c = Carve(mid)
        c(2 * GT * P)
        x1c = c(2 * GT * D, "p (s j n) -> p s j n", s=2, j=GT)
        yg = c(2 * GT * 2 * D, "p (s j c n) -> p s j c n", s=2, j=GT, c=2)
        x2 = c(2 * GT * D, "p (s j n) -> p s j n", s=2, j=GT)
        n2 = c(2 * GT * D, "p (s j n) -> p s j n", s=2, j=GT)
        hT = c(GT * D, "p (j k n) -> p j k n", j=GT, k=KD)
        hsum = c(GT * D, "p (j n) -> p j n", j=GT)
        assert c.at <= 14336, c.at
        c = Carve(mid)
        c(9216)
        g_sb = c(2 * F0, "p (s n) -> p s n", s=2)
        h_sb = c(2 * F0, "p (s n) -> p s n", s=2)
        hsT = c(2 * F0, "p (s k n) -> p s k n", s=2, k=KF)
        y_sb = c(2 * D, "p (s n) -> p s n", s=2)
        xs = c(2 * D, "p (s n) -> p s n", s=2)
        xsT = c(2 * D, "p (s k n) -> p s k n", s=2, k=KD)
        assert c.at <= 14336, c.at
        c = Carve(big)
        we_sb = c(E1 * KD * D)
        hrelu = c(GT * D, "p (j n) -> p j n", j=GT)
        x3 = c(2 * GT * D, "p (s j n) -> p s j n", s=2, j=GT)
        n3 = c(GT * D, "p (j n) -> p j n", j=GT)
        n3z = c(GT * KD * 2 * P, "p (j k g n) -> p j k g n", j=GT, k=KD, g=2)
        beg = c(2 * GT * D, "p (s j n) -> p s j n", s=2, j=GT)
        ysum = c(GT * D, "p (j n) -> p j n", j=GT)
        outc = c(2 * GT * D, "p (s j n) -> p s j n", s=2, j=GT)
        assert c.at <= 24576, c.at

        st1 = sb("st1", [P, GT, 6])
        mv1 = sb("mv1", [P, GT, 2])
        ve1 = sb("ve1", [P, GT])
        rstd1 = sb("rstd1", [P, GT])
        st2 = sb("st2", [P, GT, 6])
        mv2 = sb("mv2", [P, GT, 2])
        ve2 = sb("ve2", [P, GT])
        rstd2 = sb("rstd2", [P, GT])
        w_col = sb("w_col", [P, 2, GT])
        w_masked = sb("w_masked", [P, GT])
        w_max = sb("w_max", [GT, 2])
        w_sub = sb("w_sub", [GT, 2, NODES])
        w_exp = sb("w_exp", [GT, 2, NODES])
        w_sum = sb("w_sum", [GT, 2])
        w_rcp = sb("w_rcp", [GT, 2])
        w_prob = sb("w_prob", [GT, 2, NODES])
        p_col = sb("p_col", [P, GT])
        logit = sb("logit", [P, TILES, E0])
        r_a = sb("r_a", [P, HT, E0])
        r_b = sb("r_b", [P, HT, E0])
        r_c = sb("r_c", [P, HT, E0])
        r_p = sb("r_p", [P, HT, E0])
        pick = sb("pick", [P, 2, HT, E0])
        both = sb("both", [P, HT, E0])
        top = sb("top", [P, 2, HT])
        r_k = sb("r_k", [P, HT])
        weight = sb("weight", [P, TILES, 2])
        slot_f = sb("slot_f", [P, HT])
        slot_i = sb("slot_i", [P, TILES, 2], I32)
        n_f = sb("n_f", [P, E0])
        n_i = sb("n_i", [P, E0], I32)
        n_end = sb("n_end", [P, E0])
        n_base = sb("n_base", [P, E0])
        tile_e = sb("tile_e", [1, ROUTED, E0])
        tile_ef = sb("tile_ef", [1, ROUTED])
        expert_of = sb("expert_of", [1, ITEMS], I32)
        xg = sb("xg", [P, 2, GT, D])
        slot_now = sb("slot_now", [P, 2, GT * 2], I32)
        m_T = sb("m_T", [P, KD, GT, 2])
        lg = sb("lg", [2 * GT, E1])
        lg_e = sb("lg_e", [2 * GT, E1])
        lg_k = sb("lg_k", [2 * GT, E1])
        lg_s = sb("lg_s", [2 * GT, 4])
        spread = sb("spread", [2 * GT, 2, GT])
        gate = sb("gate", [P, 2, GT])
        expert = sb("expert", [P, 2, GT], I32)

        bank = [ctx.enter_context(nc.psum_tensor(f"bank{i}", [P, 512], F32)) for i in range(8)]

        consts_in = sem("consts_in")
        wqk_in = sem("wqk_in")
        zeroed = sem("zeroed")
        mp_mm = sem("mp_mm")
        mp_ready = sem("mp_ready")
        experts_in = sem("experts_in")
        rows_zeroed = sem("rows_zeroed")
        xin_in = [sem(f"xin_in{s}") for s in range(2)]
        adj_in = [sem(f"adj_in{s}") for s in range(2)]
        x1_out = [sem(f"x1_out{s}") for s in range(2)]
        n1_out = [sem(f"n1_out{s}") for s in range(2)]
        st1_done = sem("st1_done")
        mv1_done = sem("mv1_done")
        ve1_done = sem("ve1_done")
        rstd1_done = sem("rstd1_done")
        xn_done = sem("xn_done")
        st2_done = sem("st2_done")
        mv2_done = sem("mv2_done")
        ve2_done = sem("ve2_done")
        rstd2_done = sem("rstd2_done")
        n1_done = sem("n1_done")
        adj_masked = sem("adj_masked")
        tt_mm = sem("tt_mm")
        tt_ready = sem("tt_ready")
        uv_mm = sem("uv_mm")
        v_ready = sem("v_ready")
        w_dot = sem("w_dot")
        w_masked_done = sem("w_masked_done")
        w_row = sem("w_row")
        w_max_done = sem("w_max_done")
        w_sub_done = sem("w_sub_done")
        w_exp_done = sem("w_exp_done")
        w_sum_done = sem("w_sum_done")
        w_rcp_done = sem("w_rcp_done")
        w_prob_done = sem("w_prob_done")
        p_mm = sem("p_mm")
        p_col_done = sem("p_col_done")
        x1_done = sem("x1_done")
        n1T_mm = sem("n1T_mm")
        n1T_ready = sem("n1T_ready")
        logit_mm = sem("logit_mm")
        logit_ready = sem("logit_ready")
        route_step = sem("route_step")
        route_exp = sem("route_exp")
        counts_mm = sem("counts_mm")
        routed = sem("routed")
        xg_in = [sem(f"xg_in{s}") for s in range(2)]
        slots_copied = sem("slots_copied")
        scattered = [sem(f"scattered{s}") for s in range(2)]
        xs_in = [sem(f"xs_in{s}") for s in range(2)]
        xsT_mm = sem("xsT_mm")
        xsT_ready = sem("xsT_ready")
        w1_mm = sem("w1_mm")
        w3_mm = sem("w3_mm")
        gelu_done = sem("gelu_done")
        h_done = sem("h_done")
        hsT_mm = sem("hsT_mm")
        hsT_ready = sem("hsT_ready")
        y_mm = sem("y_mm")
        y_ready = sem("y_ready")
        ys_out = [sem(f"ys_out{s}") for s in range(2)]
        we_in = sem("we_in")
        x1c_in = [sem(f"x1c_in{s}") for s in range(2)]
        adjc_in = [sem(f"adjc_in{s}") for s in range(2)]
        yg_in = [sem(f"yg_in{s}") for s in range(2)]
        beg_in = [sem(f"beg_in{s}") for s in range(2)]
        out_out = [sem(f"out_out{s}") for s in range(2)]
        half_sum = sem("half_sum")
        x2_done = sem("x2_done")
        st3_done = sem("st3_done")
        mv3_done = sem("mv3_done")
        ve3_done = sem("ve3_done")
        rstd3_done = sem("rstd3_done")
        n2_done = sem("n2_done")
        a_mm = [sem(f"a_mm{i}") for i in range(3)]
        a_ready = [sem(f"a_ready{i}") for i in range(3)]
        b_mm = [sem(f"b_mm{i}") for i in range(3)]
        b_added = [sem(f"b_added{i}") for i in range(3)]
        relu_done = [sem(f"relu_done{i}") for i in range(2)]
        x3_done = sem("x3_done")
        st4_done = sem("st4_done")
        mv4_done = sem("mv4_done")
        ve4_done = sem("ve4_done")
        rstd4_done = sem("rstd4_done")
        n3_done = sem("n3_done")
        n3T_mm = sem("n3T_mm")
        n3z_ready = sem("n3z_ready")
        m_done = sem("m_done")
        lg_mm = sem("lg_mm")
        gate_step = sem("gate_step")
        lg_exp = sem("lg_exp")
        spread_done = sem("spread_done")
        spread_mm = sem("spread_mm")
        expert_ready = sem("expert_ready")
        out_mm = sem("out_mm")
        ysum_done = sem("ysum_done")
        ygate_done = sem("ygate_done")
        out_done = sem("out_done")
        pe_held = sem("pe_held")
        act_held = sem("act_held")
        dve_held = sem("dve_held")
        pool_held = sem("pool_held")

        CONSTS = 13
        GATE_STEPS, EXP_AFTER = 10, 3
        blk = ctx.enter_context(nc.Block())

        def tokens4(t, g):
            return t[ds(g * (GT * P), GT * P), :].rearrange("(j p) n -> p j n", p=P)

        @blk.sync
        def _(sp):
            for dst, src in (
                (cst[:, :], const), (mask[:, :], maskT), (wv_sb[:, :, :], wv.rearrange("(k p) n -> p k n", p=P)),
                (wg0_sb[:, :, :], wg0.rearrange("(k p) n -> p k n", p=P)),
                (bg0_sb[:, :], bg0.partition_broadcast(P)),
                (gw_sb[:, 0], gw[0].rearrange("(k p) n -> p k n", p=P)),
                (gw_sb[:, 1], gw[1].rearrange("(k p) n -> p k n", p=P)),
                (gw_sb[:, 2], gw[2].rearrange("(k p) n -> p k n", p=P)),
                (gb_sb[:, 0], gb[0].partition_broadcast(P)), (gb_sb[:, 1], gb[1].partition_broadcast(P)),
                (gb_sb[:, 2], gb[2].partition_broadcast(P)),
                (wg1_sb[:, :, :], wg1.rearrange("(k p) n -> p k n", p=P)),
                (bg1_sb[:, :], bg1.partition_broadcast(2 * GT)),
            ):
                sp.dma_start(dst, src).then_inc(consts_in, 16)
            sp.dma_start(wqk_stage, wqkT.rearrange("(h k p) n -> p h k n", h=2, p=P)).then_inc(wqk_in, 16)
            sp.wait_ge(zeroed, 2)

            def load_adj(g, sems, free_sem, free_at):
                wait(sp, free_sem, free_at)
                for b in range(2):
                    rows = slice(b * NODES, (b + 1) * NODES)
                    sp.dma_start(adj_sb[rows, g.slot, :, rows],
                                 adjT[ds(g.n * (GT * 2), GT * 2), :, :]
                                 .rearrange("(j b) p n -> b p j n", b=2)[b]).then_inc(sems[g.slot], 16)

            def load_x(g):
                wait(sp, x1_done, g.n - 1)
                sp.dma_start(xin[:, g.slot], tokens4(x, g.n)).then_inc(xin_in[g.slot], 16)

            def store_x1(g):
                sp.wait_ge(x1_done, g.n + 1)
                sp.dma_start(tokens4(x1_dram, g.n), x1[:, g.slot]).then_inc(x1_out[g.slot], 16)

            def store_n1(g):
                sp.wait_ge(n1_done, g.n + 1)
                sp.dma_start(tokens4(n1_dram, g.n), n1[:, g.slot]).then_inc(n1_out[g.slot], 16)

            def stage_a(nxt, prev):
                def body(h, par):
                    g1, g0 = At(h, par, 1), At(h, par, -1)
                    if nxt:
                        load_adj(g1, adj_in, tt_mm, GT * (g1.n - 1))
                        load_x(g1)
                    if prev:
                        store_x1(g0)
                        store_n1(g0)
                return body

            g = At(0, 0)
            load_adj(g, adj_in, tt_mm, 0)
            load_x(g)
            stage_a(True, False)(0, 0)
            sp.dma_start(w13_sb[0].rearrange("p (e k n) -> p e k n", e=E0, k=KD),
                         w1.rearrange("e (k p) n -> p e k n", p=P)).then_inc(experts_in, 16)
            sp.dma_start(w13_sb[1].rearrange("p (e k n) -> p e k n", e=E0, k=KD),
                         w3.rearrange("e (k p) n -> p e k n", p=P)).then_inc(experts_in, 16)
            sp.dma_start(w2_sb.rearrange("p (e k n) -> p e k n", e=E0, k=KF),
                         w2.rearrange("e (k p) n -> p e k n", p=P)).then_inc(experts_in, 16)
            straight(1, 4, stage_a(True, True))
            sp.dma_start(xs_dram.rearrange("(i p) n -> p i n", p=P),
                         zero[:, :].unsqueeze(1).to_broadcast([P, ITEMS, D])).then_inc(rows_zeroed, 16)
            looped(sp, 4, GROUPS - 2, stage_a(True, True))
            straight(GROUPS - 2, GROUPS - 1, stage_a(True, True))
            straight(GROUPS - 1, GROUPS + 1, stage_a(False, True))

            def load_rows(i):
                wait(sp, xsT_mm, i.n - 1)
                sp.dma_start(xs[:, i.slot], xs_dram[ds(i.n * P, P), :]).then_inc(xs_in[i.slot], 16)

            def store_rows(i):
                sp.wait_ge(y_ready, i.n + 1)
                sp.dma_start(ys_dram[ds(i.n * P, P), :], y_sb[:, i.slot]).then_inc(ys_out[i.slot], 16)

            def stage_f(h, par):
                load_rows(At(h, par))
                store_rows(At(h, par, -4))

            def half_scattered(half):
                for s in range(2):
                    sp.wait_ge(scattered[s], (half + 1) * (HG // 2) * GT * 2 * 16)

            for s in range(2):
                sp.wait_ge(x1_out[s], 16 * GROUPS // 2)
                sp.wait_ge(n1_out[s], 16 * GROUPS // 2)
            sp.wait_ge(n1T_mm, 2 * GROUPS)
            half_scattered(0)
            straight(0, 4, lambda h, par: load_rows(At(h, par)))
            straight(4, 6, stage_f)
            looped(sp, 6, ROUTED - 1, stage_f)
            straight(ROUTED - 1, ROUTED, stage_f)
            half_scattered(1)
            straight(ROUTED, ROUTED + 1, stage_f)
            looped(sp, ROUTED + 1, ITEMS, stage_f)

            def load_c(g):
                wait(sp, x2_done, g.n - 1)
                sp.dma_start(x1c[:, g.slot], tokens4(x1_dram, g.n)).then_inc(x1c_in[g.slot], 16)

            def load_adj_c(g):
                load_adj(g, adjc_in, a_mm[2], 2 * (g.n - 1))

            for s in range(2):
                sp.wait_ge(x1_out[s], 16 * GROUPS // 2)
            load_c(At(0, 0))
            load_adj_c(At(0, 0))
            straight(ITEMS, ITEMS + 4, lambda h, par: store_rows(At(h, par, -4)))
            sp.wait_ge(y_mm, ITEMS)
            sp.dma_start(we_sb.rearrange("p (e k n) -> p e k n", e=E1, k=KD),
                         we.rearrange("e (k p) n -> p e k n", p=P)).then_inc(we_in, 16)

            def store_out(g):
                sp.wait_ge(out_done, g.n + 1)
                sp.dma_start(tokens4(out, g.n), outc[:, g.slot]).then_inc(out_out[g.slot], 16)

            def stage_c(nxt, prev):
                def body(h, par):
                    if nxt:
                        load_c(At(h, par, 1))
                        load_adj_c(At(h, par, 1))
                    if prev:
                        store_out(At(h, par, -1))
                return body

            straight(0, 1, stage_c(True, False))
            straight(1, 4, stage_c(True, True))
            looped(sp, 4, GROUPS - 2, stage_c(True, True))
            straight(GROUPS - 2, GROUPS - 1, stage_c(True, True))
            straight(GROUPS - 1, GROUPS + 1, stage_c(False, True))
            for s in range(2):
                sp.wait_ge(out_out[s], 16 * GROUPS // 2)
                sp.wait_ge(n1_out[s], 16 * GROUPS // 2)
                sp.wait_ge(ys_out[s], 16 * ITEMS // 2)

        @blk.gpsimd
        def _(pool):
            pool.memset(adj_sb, 0.0).then_inc(zeroed, 1)
            pool.memset(zero[:, :], 0.0).then_inc(zeroed, 1)
            pool.wait_ge(consts_in, 16 * CONSTS)

            def rsqrt(g, mv, mv_sem, ve, ve_sem, rstd, rstd_sem):
                pool.wait_ge(mv_sem, g.n + 1)
                pool.tensor_tensor(ve[:, :], mv[:, :, 1], const_of("eps"), ALU.add).then_inc(ve_sem, 1)
                pool.wait_ge(ve_sem, g.n + 1)
                pool.tensor_tensor(rstd[:, :], ve[:, :], const_of("minus_half"), ALU.pow).then_inc(rstd_sem, 1)

            def load_for_scatter(q):
                wait(pool, scattered[q.slot], 2 * GT * 16 * q.used)
                pool.wait_ge(n1_out[q.slot], 16 * (q.used + 1))
                pool.sem_inc(pool_held, 1)
                pool.dma_start(xg[:, q.slot], tokens4(n1_dram, q.n)).then_inc(xg_in[q.slot], 16)

            def copy_slots(q):
                pool.tensor_copy(slot_now[:, q.slot],
                                 slot_i[:, ds(q.n * GT, GT), :].rearrange("p j c -> p (j c)")
                                 ).then_inc(slots_copied, 1)

            def scatter(q, part):
                if part == 0:
                    copy_slots(q)
                    pool.wait_ge(slots_copied, q.n + 1)
                    pool.wait_ge(xg_in[q.slot], 16 * (q.used + 1))
                    pool.sem_inc(pool_held, 1)
                for j in range(2 * part, 2 * part + 2):
                    for c in range(2):
                        at = slot_now[:, q.slot, 2 * j + c:2 * j + c + 1].bitcast(U32)
                        pool.indirect_dma_start(xs_dram, IndirectOffsetOnAxis(ap=at, axis=0),
                                                xg[:, q.slot, j], None).then_inc(scattered[q.slot], 16)

            def stage_a(nxt, prev, scat):
                def body(h, par):
                    if scat:
                        q = At(h - HG // 2 - 1, par)
                        load_for_scatter(At(h - HG // 2 - 1, par, 1)) if scat == 1 else None
                        scatter(q, 0)
                    if prev:
                        rsqrt(At(h, par, -1), mv2, mv2_done, ve2, ve2_done, rstd2, rstd2_done)
                    if nxt:
                        rsqrt(At(h, par, 1), mv1, mv1_done, ve1, ve1_done, rstd1, rstd1_done)
                    if scat:
                        scatter(q, 1)
                return body

            straight(-1, 0, stage_a(True, False, 0))
            straight(0, 1, stage_a(True, False, 0))
            straight(1, 4, stage_a(True, True, 0))
            looped(pool, 4, HG + 2, stage_a(True, True, 0))
            pool.wait_ge(routed, 1)
            pool.wait_ge(rows_zeroed, 16)
            load_for_scatter(At(0, 0))
            straight(HG + 2, HG + 4, stage_a(True, True, 1))
            looped(pool, HG + 4, GROUPS - 2, stage_a(True, True, 1))
            straight(GROUPS - 2, GROUPS - 1, stage_a(True, True, 1))
            straight(GROUPS - 1, GROUPS, stage_a(False, True, 1))
            straight(GROUPS, GROUPS + 1, stage_a(False, True, 1))
            straight(GROUPS + 1, GROUPS + 2, stage_a(False, False, 2))
            pool.wait_ge(routed, 2)
            load_for_scatter(At(HG // 2, 0))

            def second(more):
                def body(h, par):
                    if more:
                        load_for_scatter(At(h, par, 1))
                    scatter(At(h, par), 0)
                    scatter(At(h, par), 1)
                return body

            looped(pool, HG, GROUPS - 2, second(True))
            straight(GROUPS - 2, GROUPS - 1, second(True))
            straight(GROUPS - 1, GROUPS, second(False))

            def gather_y(g, part):
                if part == 0:
                    wait(pool, x2_done, g.n - 1)
                    pool.wait_ge(slots_copied, GROUPS + g.n)
                    pool.sem_inc(pool_held, 1)
                    copy_slots(g)
                    pool.wait_ge(slots_copied, GROUPS + g.n + 1)
                    pool.sem_inc(pool_held, 1)
                for j in range(2 * part, 2 * part + 2):
                    for c in range(2):
                        at = slot_now[:, g.slot, 2 * j + c:2 * j + c + 1].bitcast(U32)
                        pool.indirect_dma_start(yg[:, g.slot, j, c], None, ys_dram,
                                                IndirectOffsetOnAxis(ap=at, axis=0)).then_inc(yg_in[g.slot], 16)

            def gather_be(g):
                pool.wait_ge(expert_ready, g.n + 1)
                wait(pool, out_done, g.n - 1)
                pool.sem_inc(pool_held, 1)
                for j in range(GT):
                    pool.indirect_dma_start(beg[:, g.slot, j], None, be,
                                            IndirectOffsetOnAxis(ap=expert[:, g.slot, j:j + 1].bitcast(U32),
                                                                 axis=0)).then_inc(beg_in[g.slot], 16)

            def norm2(g):
                rsqrt(g, mv1, mv3_done, ve1, ve3_done, rstd1, rstd3_done)

            def stage_c(nxt2, nxt, prev):
                def body(h, par):
                    if prev:
                        rsqrt(At(h, par, -1), mv2, mv4_done, ve2, ve4_done, rstd2, rstd4_done)
                    if nxt:
                        norm2(At(h, par, 1))
                    if nxt2:
                        gather_y(At(h, par, 2), 0)
                    if prev:
                        gather_be(At(h, par, -1))
                    if nxt2:
                        gather_y(At(h, par, 2), 1)
                return body

            for s in range(2):
                pool.wait_ge(ys_out[s], 16 * ITEMS // 2)
            for s in range(2):
                pool.wait_ge(scattered[s], 2 * GT * 16 * GROUPS // 2)
            for par in range(2):
                gather_y(At(0, par), 0)
                gather_y(At(0, par), 1)
            norm2(At(0, 0))
            straight(0, 1, stage_c(True, True, False))
            straight(1, 4, stage_c(True, True, True))
            looped(pool, 4, GROUPS - 2, stage_c(True, True, True))
            straight(GROUPS - 2, GROUPS - 1, stage_c(False, True, True))
            straight(GROUPS - 1, GROUPS + 1, stage_c(False, False, True))

        @blk.scalar
        def _(act):
            act.wait_ge(consts_in, 16 * CONSTS)
            for b in range(2):
                act.wait_ge(mp_mm, b + 1)
                act.activation(mp[:, b], bank[b][:, 0:D], ACT.Copy).then_inc(mp_ready, 1)

            def mask_adj(g):
                act.wait_ge(adj_in[g.slot], 32 * (g.used + 1))
                act.sem_inc(act_held, 1)
                for j in range(GT):
                    a = adj_sb[:, g.slot, j]
                    act.activation(a, a, ACT.Copy, scale=mask[:, ds(g.n * GT + j, 1)]).then_inc(adj_masked, 1)

            def copy_tt(g, j):
                t = g.n * GT + j
                act.wait_ge(tt_mm, t + 1)
                wait(act, uv_mm, t + 1 - GT)
                act.activation(tt[:, j].rearrange("p a k n -> p (a k n)"), bank[0][:, :], ACT.Copy
                               ).then_inc(tt_ready, 1)

            def copy_v(g, j):
                act.wait_ge(uv_mm, g.n * GT + j + 1)
                if j == 0:
                    wait(act, x1_done, g.n - 1)
                act.activation(v_sb[:, g.slot, j], bank[4 + j % 2][:, 0:D], ACT.Copy).then_inc(v_ready, 1)

            def exp_w(g):
                act.wait_ge(w_sub_done, g.n + 1)
                act.activation(w_exp[:, :, :], w_sub[:, :, :], ACT.Exp).then_inc(w_exp_done, 1)

            def copy_n1T(g, pair):
                act.wait_ge(n1T_mm, 2 * g.n + pair + 1)
                wait(act, logit_mm, g.n)
                act.activation(n1T[:, 2 * pair:2 * pair + 2].rearrange("p j k n -> p (j k n)"),
                               bank[1][:, :], ACT.Copy).then_inc(n1T_ready, 1)

            def copy_logit(g):
                act.wait_ge(logit_mm, g.n + 1)
                act.sem_inc(act_held, 1)
                act.activation(logit[:, ds(g.n * GT, GT), :].rearrange("p j e -> p (j e)"),
                               bank[7][:, 0:GT * E0], ACT.Copy).then_inc(logit_ready, 1)

            def stage_a(nxt, cur, prev, last):
                def body(h, par):
                    g1, g, gp, gl = (At(h, par, d) for d in (1, 0, -1, -2))
                    if cur:
                        copy_tt(g, 0)
                    if last:
                        copy_n1T(gl, 0)
                    for j in range(GT):
                        if cur:
                            if j + 1 < GT:
                                copy_tt(g, j + 1)
                            copy_v(g, j)
                        if last and j == 1:
                            copy_n1T(gl, 1)
                        if prev and j == 0:
                            exp_w(gp)
                    if nxt:
                        mask_adj(g1)
                    if last:
                        copy_logit(gl)
                return body

            mask_adj(At(0, 0))
            straight(0, 1, stage_a(True, True, False, False))
            straight(1, 2, stage_a(True, True, True, False))
            straight(2, 4, stage_a(True, True, True, True))
            looped(act, 4, HG + 2, stage_a(True, True, True, True))

            def route(half):
                for k in range(3):
                    act.wait_ge(route_exp, 6 * half + 2 * k + 1)
                    act.activation(r_b[:, :, :], r_a[:, :, :], ACT.Exp).then_inc(route_exp, 1)

            route(0)
            looped(act, HG + 2, GROUPS - 2, stage_a(True, True, True, True))
            straight(GROUPS - 2, GROUPS - 1, stage_a(True, True, True, True))
            straight(GROUPS - 1, GROUPS, stage_a(False, True, True, True))
            straight(GROUPS, GROUPS + 1, stage_a(False, False, True, True))
            straight(GROUPS + 1, GROUPS + 2, stage_a(False, False, False, True))
            route(1)

            for s in range(2):
                act.wait_ge(x1_out[s], 16 * GROUPS // 2)
                act.wait_ge(n1_out[s], 16 * GROUPS // 2)

            def gelu(i):
                act.wait_ge(w1_mm, i.n + 1)
                wait(act, h_done, i.n - 1)
                act.activation(g_sb[:, i.slot], bank[2 + i.slot][:, :], ACT.Gelu).then_inc(gelu_done, 1)

            def copy_hsT(i):
                act.wait_ge(hsT_mm, i.n + 1)
                wait(act, y_mm, i.n - 1)
                act.activation(hsT[:, i.slot].rearrange("p k n -> p (k n)"), bank[0][:, :], ACT.Copy
                               ).then_inc(hsT_ready, 1)

            def stage_f(h, par):
                copy_hsT(At(h, par, -2))
                gelu(At(h, par, -1))

            straight(1, 2, lambda h, par: gelu(At(h, par, -1)))
            straight(2, 6, stage_f)
            looped(act, 6, ITEMS, stage_f)
            straight(ITEMS, ITEMS + 1, stage_f)
            straight(ITEMS + 1, ITEMS + 2, lambda h, par: copy_hsT(At(h, par, -2)))

            def copy_a(g, layer, pair):
                act.wait_ge(a_mm[layer], 2 * g.n + pair + 1)
                act.activation(hT[:, 2 * pair:2 * pair + 2].rearrange("p j k n -> p (j k n)"),
                               bank[pair][:, :], ACT.Copy).then_inc(a_ready[layer], 1)

            def relu(g, layer, pair):
                act.wait_ge(b_added[layer], 2 * g.n + pair + 1)
                act.activation(hrelu[:, 2 * pair:2 * pair + 2], hsum[:, 2 * pair:2 * pair + 2],
                               ACT.Relu).then_inc(relu_done[layer], 1)

            def copy_n3T(g, pair):
                act.wait_ge(n3T_mm, 2 * g.n + pair + 1)
                wait(act, out_mm, 2 * (g.n - 1) + pair + 1)
                wait(act, m_done, g.n)
                for b in range(2):
                    ins = act.activation(
                        n3z[:, 2 * pair:2 * pair + 2, :, b, b * NODES:(b + 1) * NODES],
                        bank[4 + pair].rearrange("p (j k n) -> p j k n", j=2, k=KD)
                        [:, :, :, b * NODES:(b + 1) * NODES], ACT.Copy)
                ins.then_inc(n3z_ready, 1)

            def exp_lg(g):
                act.wait_ge(gate_step, GATE_STEPS * g.n + EXP_AFTER)
                act.activation(lg_e[:, :], lg_k[:, :], ACT.Exp, accum_out=lg_s[:, 2:3]).then_inc(lg_exp, 1)

            def stage_c(cur, prev):
                def body(h, par):
                    g, gp = At(h, par), At(h, par, -1)
                    if cur:
                        copy_a(g, 0, 0)
                        copy_a(g, 0, 1)
                        relu(g, 0, 0)
                        relu(g, 0, 1)
                    if prev:
                        copy_n3T(gp, 0)
                        copy_n3T(gp, 1)
                    if cur:
                        copy_a(g, 1, 0)
                        copy_a(g, 1, 1)
                    if prev:
                        exp_lg(gp)
                    if cur:
                        relu(g, 1, 0)
                        relu(g, 1, 1)
                        copy_a(g, 2, 0)
                        copy_a(g, 2, 1)
                return body

            straight(0, 1, stage_c(True, False))
            straight(1, 4, stage_c(True, True))
            looped(act, 4, GROUPS, stage_c(True, True))
            straight(GROUPS, GROUPS + 1, stage_c(False, True))

        @blk.tensor
        def _(pe):
            pe.wait_ge(wqk_in, 16)
            pe.wait_ge(consts_in, 16 * CONSTS)
            for b in range(KD):
                for k in range(KD):
                    mm = pe.matmul(bank[b][:, 0:D], wqk_stage[:, 1, k, b * P:(b + 1) * P],
                                   wqk_stage[:, 0, k, :], start=(k == 0), stop=(k == KD - 1))
                mm.then_inc(mp_mm, 1)
            pe.wait_ge(mp_ready, 2)

            def adj_and_transposes(g, j):
                t = g.n * GT + j
                pe.wait_ge(adj_masked, t + 1)
                pe.wait_ge(xn_done, t + 1)
                wait(pe, tt_ready, t)
                for k in range(KD):
                    pe.matmul(bank[0][:, k * P:(k + 1) * P], xn[:, g.slot, j, k * P:(k + 1) * P],
                              adj_sb[:, g.slot, j], start=True, stop=True)
                for k in range(KD):
                    mm = pe.transpose(bank[0][:, D + k * P:D + (k + 1) * P],
                                      xn[:, g.slot, j, k * P:(k + 1) * P], ident)
                mm.then_inc(tt_mm, 1)

            def u_and_v(g, j):
                t = g.n * GT + j
                pe.wait_ge(tt_ready, t + 1)
                wait(pe, w_dot, t - 1)
                wait(pe, v_ready, t - 1)
                for k in range(KD):
                    pe.matmul(bank[2 + j % 2][:, 0:D], tt[:, j, 0, k], mp[:, k], start=(k == 0), stop=(k == KD - 1))
                for k in range(KD):
                    mm = pe.matmul(bank[4 + j % 2][:, 0:D], tt[:, j, 1, k], wv_sb[:, k],
                                   start=(k == 0), stop=(k == KD - 1))
                mm.then_inc(uv_mm, 1)

            def w_to_rows(g):
                pe.wait_ge(w_masked_done, g.n + 1)
                wait(pe, p_col_done, g.n)
                pe.matmul(bank[6][0:GT, 0:P], w_masked[:, :], ident, start=True, stop=True).then_inc(w_row, 1)

            def p_to_columns(g):
                pe.wait_ge(w_prob_done, g.n + 1)
                pe.matmul(bank[6][:, P:P + GT], w_prob[:, :, :].rearrange("j g n -> j (g n)"),
                          ident[0:GT, 0:GT], start=True, stop=True).then_inc(p_mm, 1)

            def n1_transposes(g, pair):
                pe.wait_ge(n1_done, g.n + 1)
                wait(pe, n1T_ready, 2 * g.n + pair)
                for j in range(2):
                    for k in range(KD):
                        mm = pe.transpose(bank[1][:, (j * KD + k) * P:(j * KD + k + 1) * P],
                                          n1[:, g.slot, 2 * pair + j, k * P:(k + 1) * P], ident)
                mm.then_inc(n1T_mm, 1)

            def logits(g):
                pe.wait_ge(n1T_ready, 2 * g.n + 2)
                wait(pe, logit_ready, g.n)
                for j in range(GT):
                    for k in range(KD):
                        mm = pe.matmul(bank[7][:, j * E0:(j + 1) * E0], n1T[:, j, k], wg0_sb[:, k],
                                       start=(k == 0), stop=(k == KD - 1))
                mm.then_inc(logit_mm, 1)

            def stage_a(cur, prev, last):
                def body(h, par):
                    g, gp, gl = (At(h, par, d) for d in (0, -1, -2))
                    if cur:
                        adj_and_transposes(g, 0)
                    if last:
                        n1_transposes(gl, 0)
                    for j in range(GT):
                        if cur:
                            if j + 1 < GT:
                                adj_and_transposes(g, j + 1)
                            u_and_v(g, j)
                        if last and j == 1:
                            n1_transposes(gl, 1)
                        if prev and j == 0:
                            w_to_rows(gp)
                        if prev and j == 2:
                            p_to_columns(gp)
                    if last:
                        logits(gl)
                return body

            straight(0, 1, stage_a(True, False, False))
            straight(1, 2, stage_a(True, True, False))
            straight(2, 4, stage_a(True, True, True))
            looped(pe, 4, HG + 2, stage_a(True, True, True))

            def route(half):
                pe.wait_ge(counts_mm, 2 * half + 1)
                wait(pe, logit_ready, HG * (half + 1))
                a = both[:, :, :].rearrange("p t e -> p (t e)")
                pe.matmul(bank[7][:, 0:HT * E0], const_of("before"), a, start=True, stop=True)
                pe.matmul(bank[7][:, HT * E0:2 * HT * E0], const_of("ones"), a,
                          start=True, stop=True).then_inc(counts_mm, 1)

            route(0)
            pe.wait_ge(routed, 1)
            looped(pe, HG + 2, GROUPS, stage_a(True, True, True))
            straight(GROUPS, GROUPS + 1, stage_a(False, True, True))
            straight(GROUPS + 1, GROUPS + 2, stage_a(False, False, True))
            route(1)
            pe.wait_ge(routed, 2)
            pe.wait_ge(experts_in, 48)

            def rows_transposes(i):
                pe.wait_ge(xs_in[i.slot], 16 * (i.used + 1))
                wait(pe, xsT_ready, i.n)
                for k in range(KD):
                    mm = pe.transpose(bank[1][:, k * P:(k + 1) * P], xs[:, i.slot, k * P:(k + 1) * P], ident)
                mm.then_inc(xsT_mm, 1)

            def up(i):
                e = pe.value_load(expert_of[0:1, ds(i.n, 1)], min_val=0, max_val=E0 - 1)
                pe.wait_ge(xsT_ready, i.n + 1)
                wait(pe, h_done, i.n - 1)
                for w, done in ((0, w1_mm), (1, w3_mm)):
                    for k in range(KD):
                        mm = pe.matmul(bank[2 + 2 * w + i.slot][:, :], xsT[:, i.slot, k],
                                       w13_sb[w][:, ds(e * (KD * F0) + k * F0, F0)],
                                       start=(k == 0), stop=(k == KD - 1))
                    mm.then_inc(done, 1)
                return e

            def h_transposes(i):
                pe.wait_ge(h_done, i.n + 1)
                wait(pe, hsT_ready, i.n)
                for k in range(KF):
                    mm = pe.transpose(bank[0][:, k * P:(k + 1) * P], h_sb[:, i.slot, k * P:(k + 1) * P], ident)
                mm.then_inc(hsT_mm, 1)

            def down(i):
                e = pe.value_load(expert_of[0:1, ds(i.n, 1)], min_val=0, max_val=E0 - 1)
                pe.wait_ge(hsT_ready, i.n + 1)
                wait(pe, y_ready, i.n - 1)
                for k in range(KF):
                    mm = pe.matmul(bank[6 + i.slot][:, 0:D], hsT[:, i.slot, k],
                                   w2_sb[:, ds(e * (KF * D) + k * D, D)], start=(k == 0), stop=(k == KF - 1))
                mm.then_inc(y_mm, 1)

            def stage_f(first, second, third):
                def body(h, par):
                    if third:
                        h_transposes(At(h, par, -2))
                    if first:
                        rows_transposes(At(h, par))
                    if second:
                        up(At(h, par, -1))
                    if third:
                        down(At(h, par, -2))
                return body

            straight(0, 1, stage_f(True, False, False))
            straight(1, 2, stage_f(True, True, False))
            straight(2, 6, stage_f(True, True, True))
            looped(pe, 6, ITEMS, stage_f(True, True, True))
            straight(ITEMS, ITEMS + 1, stage_f(False, True, True))
            straight(ITEMS + 1, ITEMS + 2, stage_f(False, False, True))
            pe.wait_ge(y_ready, ITEMS)

            def times_adj(g, layer):
                for pair in range(2):
                    if layer == 0:
                        pe.wait_ge(n2_done, g.n + 1)
                        pe.wait_ge(adjc_in[g.slot], 32 * (g.used + 1))
                        src = n2[:, g.slot]
                        wait(pe, a_ready[2], 2 * (g.n - 1) + pair + 1)
                    else:
                        pe.wait_ge(relu_done[layer - 1], 2 * g.n + pair + 1)
                        src = hrelu
                        pe.wait_ge(a_ready[layer - 1], 2 * g.n + pair + 1)
                    for j in range(2):
                        for k in range(KD):
                            mm = pe.matmul(bank[pair][:, (j * KD + k) * P:(j * KD + k + 1) * P],
                                           src[:, 2 * pair + j, k * P:(k + 1) * P],
                                           adj_sb[:, g.slot, 2 * pair + j], start=True, stop=True)
                    mm.then_inc(a_mm[layer], 1)

            def times_w(g, layer):
                for pair in range(2):
                    pe.wait_ge(a_ready[layer], 2 * g.n + pair + 1)
                    if layer == 0:
                        wait(pe, b_added[2], 2 * (g.n - 1) + pair + 1)
                    else:
                        pe.wait_ge(b_added[layer - 1], 2 * g.n + pair + 1)
                    for j in range(2):
                        for k in range(KD):
                            mm = pe.matmul(bank[2 + pair][:, j * D:(j + 1) * D], hT[:, 2 * pair + j, k],
                                           gw_sb[:, layer, k], start=(k == 0), stop=(k == KD - 1))
                    mm.then_inc(b_mm[layer], 1)

            def n3_transposes(g):
                for pair in range(2):
                    pe.wait_ge(n3_done, g.n + 1)
                    wait(pe, n3z_ready, 2 * g.n - 2 + pair + 1)
                    for j in range(2):
                        for k in range(KD):
                            mm = pe.transpose(bank[4 + pair][:, (j * KD + k) * P:(j * KD + k + 1) * P],
                                              n3[:, 2 * pair + j, k * P:(k + 1) * P], ident)
                    mm.then_inc(n3T_mm, 1)

            def graph_logits(g):
                pe.wait_ge(m_done, g.n + 1)
                for k in range(KD):
                    mm = pe.matmul(bank[4][0:2 * GT, 0:E1], m_T[:, k].rearrange("p j g -> p (j g)"), wg1_sb[:, k],
                                   start=(k == 0), stop=(k == KD - 1))
                mm.then_inc(lg_mm, 1)

            def spread_gate(g):
                pe.wait_ge(spread_done, g.n + 1)
                pe.matmul(bank[4][:, E1:E1 + 2 * GT], const_of("half_of", 2 * GT),
                          spread[:, :, :].rearrange("g a j -> g (a j)"), start=True, stop=True
                          ).then_inc(spread_mm, 1)

            def graph_expert(g, pair):
                pe.wait_ge(expert_ready, g.n + 1)
                wait(pe, ysum_done, 2 * (g.n - 1) + pair + 1)
                pe.sem_inc(pe_held, 1)
                for j in range(2):
                    for b in range(2):
                        e = pe.value_load(expert[b * NODES:b * NODES + 1, g.slot, 2 * pair + j:2 * pair + j + 1],
                                          min_val=0, max_val=E1 - 1)
                        for k in range(KD):
                            mm = pe.matmul(bank[6 + pair][:, j * D:(j + 1) * D], n3z[:, 2 * pair + j, k, b],
                                           we_sb[:, ds(e * (KD * D) + k * D, D)],
                                           start=(b == 0 and k == 0), stop=(b == 1 and k == KD - 1))
                mm.then_inc(out_mm, 1)

            def stage_c(cur, prev):
                def body(h, par):
                    g, gp = At(h, par), At(h, par, -1)
                    if cur:
                        times_adj(g, 0)
                        times_w(g, 0)
                    if prev:
                        n3_transposes(gp)
                    if cur:
                        times_adj(g, 1)
                    if prev:
                        graph_logits(gp)
                    if cur:
                        times_w(g, 1)
                    if prev:
                        spread_gate(gp)
                    if cur:
                        times_adj(g, 2)
                    if prev:
                        graph_expert(gp, 0)
                    if cur:
                        times_w(g, 2)
                    if prev:
                        graph_expert(gp, 1)
                return body

            straight(0, 1, stage_c(True, False))
            pe.wait_ge(we_in, 16)
            straight(1, 4, stage_c(True, True))
            looped(pe, 4, GROUPS, stage_c(True, True))
            straight(GROUPS, GROUPS + 1, stage_c(False, True))

        @blk.vector
        def _(dve):
            dve.wait_ge(consts_in, 16 * CONSTS)

            def norm_stats(g, src, st, st_sem, mv, mv_sem, used_sem):
                wait(dve, mv_sem, g.n)
                for j in range(GT):
                    ins = dve.bn_stats(st[:, j], src[:, j])
                ins.then_inc(st_sem, 1)
                dve.wait_ge(st_sem, g.n + 1)
                wait(dve, used_sem, g.n)
                dve.sem_inc(dve_held, 1)
                for j in range(GT):
                    ins = dve.bn_aggr(mv[:, j], st[:, j])
                ins.then_inc(mv_sem, 1)

            def norm_rows(g, j, dst, src, mv, rstd):
                return dve.tensor_scalar(dst[:, j], src[:, j], mv[:, j, 0:1], rstd[:, j:j + 1],
                                         ALU.subtract, ALU.mult)

            def stats_x(g):
                dve.wait_ge(xin_in[g.slot], 16 * (g.used + 1))
                norm_stats(g, xin[:, g.slot], st1, st1_done, mv1, mv1_done, xn_group)

            xn_group = sem("xn_group")

            def norm_x(g):
                dve.wait_ge(rstd1_done, g.n + 1)
                wait(dve, tt_mm, GT * (g.n - 1))
                wait(dve, w_dot, GT * (g.n - 1))
                for j in range(GT):
                    norm_rows(g, j, xn[:, g.slot], xin[:, g.slot], mv1, rstd1).then_inc(xn_done, 1)
                dve.wait_ge(xn_done, GT * (g.n + 1))
                dve.sem_inc(xn_group, 1)

            def dot_w(g, j):
                dve.wait_ge(uv_mm, g.n * GT + j + 1)
                u = bank[2 + j % 2][:, 0:D]
                dve.tensor_tensor_reduce(u, u, xn[:, g.slot, j], ATT_SCALE, 0.0, ALU.mult, ALU.add,
                                         w_col[:, g.slot, j:j + 1]).then_inc(w_dot, 1)

            def mask_w(g):
                dve.wait_ge(w_dot, GT * (g.n + 1))
                dve.tensor_tensor(w_masked[:, :], w_col[:, g.slot], mask[:, ds(g.n * GT, GT)], ALU.mult
                                  ).then_inc(w_masked_done, 1)

            def sub_max(g):
                rows = bank[6][0:GT, 0:P].rearrange("j (g n) -> j g n", g=2)
                dve.wait_ge(w_row, g.n + 1)
                dve.tensor_reduce(w_max[:, :], rows, AX.X, ALU.max).then_inc(w_max_done, 1)
                dve.wait_ge(w_max_done, g.n + 1)
                dve.tensor_tensor(w_sub[:, :, :], rows, w_max[:, :].unsqueeze(2).to_broadcast([GT, 2, NODES]),
                                  ALU.subtract).then_inc(w_sub_done, 1)

            def prob(g):
                dve.wait_ge(w_exp_done, g.n + 1)
                dve.tensor_reduce(w_sum[:, :], w_exp[:, :, :], AX.X, ALU.add).then_inc(w_sum_done, 1)
                dve.wait_ge(w_sum_done, g.n + 1)
                dve.reciprocal(w_rcp[:, :], w_sum[:, :]).then_inc(w_rcp_done, 1)
                dve.wait_ge(w_rcp_done, g.n + 1)
                dve.tensor_tensor(w_prob[:, :, :], w_exp[:, :, :],
                                  w_rcp[:, :].unsqueeze(2).to_broadcast([GT, 2, NODES]), ALU.mult
                                  ).then_inc(w_prob_done, 1)

            def add_x1(g):
                dve.wait_ge(p_mm, g.n + 1)
                wait(dve, x1_done, g.n)
                dve.tensor_copy(p_col[:, :], bank[6][:, P:P + GT]).then_inc(p_col_done, 1)
                dve.wait_ge(p_col_done, g.n + 1)
                dve.wait_ge(v_ready, GT * (g.n + 1))
                wait(dve, x1_out[g.slot], 16 * g.used)
                for j in range(GT):
                    ins = dve.scalar_tensor_tensor(out=x1[:, g.slot, j], in0=v_sb[:, g.slot, j],
                                                   scalar=p_col[:, j:j + 1], in1=xin[:, g.slot, j],
                                                   op0=ALU.mult, op1=ALU.add)
                ins.then_inc(x1_done, 1)

            def stats_x1(g):
                dve.wait_ge(x1_done, g.n + 1)
                norm_stats(g, x1[:, g.slot], st2, st2_done, mv2, mv2_done, n1_done)

            def norm_x1(g):
                dve.wait_ge(rstd2_done, g.n + 1)
                wait(dve, n1_out[g.slot], 16 * g.used)
                wait(dve, n1T_mm, 2 * (g.n - 1))
                for j in range(GT):
                    ins = norm_rows(g, j, n1[:, g.slot], x1[:, g.slot], mv2, rstd2)
                ins.then_inc(n1_done, 1)

            def stage_a(nxt, cur, prev):
                def body(h, par):
                    g1, g, gp = (At(h, par, d) for d in (1, 0, -1))
                    if prev:
                        mask_w(gp)
                        sub_max(gp)
                    if cur:
                        dot_w(g, 0)
                    if prev:
                        prob(gp)
                    if cur:
                        dot_w(g, 1)
                    if prev:
                        add_x1(gp)
                    if cur:
                        dot_w(g, 2)
                    if prev:
                        stats_x1(gp)
                    if nxt:
                        stats_x(g1)
                    if cur:
                        dot_w(g, 3)
                    if prev:
                        norm_x1(gp)
                    if nxt:
                        norm_x(g1)
                return body

            stats_x(At(0, 0))
            norm_x(At(0, 0))
            straight(0, 1, stage_a(True, True, False))
            straight(1, 4, stage_a(True, True, True))
            looped(dve, 4, HG + 2, stage_a(True, True, True))

            steps = [0]

            def step(ins):
                steps[0] += 1
                ins.then_inc(route_step, 1)
                dve.wait_ge(route_step, steps[0])

            def over_e(v):
                return v.unsqueeze(2).to_broadcast([P, HT, E0])

            def over_t(v):
                return v.unsqueeze(1).to_broadcast([P, HT, E0])

            def exp_on_act(half, k):
                dve.sem_inc(route_exp, 1)
                dve.wait_ge(route_exp, 6 * half + 2 * k + 2)

            def route(half):
                t0 = half * HT
                base = half * ROUTED * P
                dve.wait_ge(logit_ready, HG * (half + 1))
                logits = logit[:, t0:t0 + HT, :]
                step(dve.tensor_tensor(r_c[:, :, :], logits, over_t(bg0_sb[:, :]), ALU.add))
                step(dve.tensor_reduce(r_k[:, :], r_c[:, :, :], AX.X, ALU.max))
                step(dve.tensor_tensor(r_a[:, :, :], r_c[:, :, :], over_e(r_k[:, :]), ALU.subtract))
                exp_on_act(half, 0)
                step(dve.tensor_reduce(r_k[:, :], r_b[:, :, :], AX.X, ALU.add))
                step(dve.reciprocal(r_k[:, :], r_k[:, :]))
                step(dve.tensor_tensor(r_p[:, :, :], r_b[:, :, :], over_e(r_k[:, :]), ALU.mult))
                for c in range(2):
                    if c == 0:
                        s = r_p
                    else:
                        step(dve.scalar_tensor_tensor(out=r_c[:, :, :], in0=pick[:, 0], scalar=-4.0,
                                                      in1=r_p[:, :, :], op0=ALU.mult, op1=ALU.add))
                        s = r_c
                    mx = top[:, c]
                    step(dve.tensor_reduce(mx, s[:, :, :], AX.X, ALU.max))
                    step(dve.tensor_tensor(r_a[:, :, :], s[:, :, :], over_e(mx), ALU.is_ge))
                    step(dve.tensor_tensor(r_a[:, :, :], r_a[:, :, :], over_t(const_of("rev0")), ALU.mult))
                    step(dve.tensor_reduce(r_k[:, :], r_a[:, :, :], AX.X, ALU.max))
                    step(dve.tensor_tensor(pick[:, c], r_a[:, :, :], over_e(r_k[:, :]), ALU.is_ge))
                    step(dve.tensor_tensor(r_a[:, :, :], r_p[:, :, :], over_e(mx), ALU.subtract))
                    exp_on_act(half, 1 + c)
                    step(dve.tensor_tensor(both[:, :, :], r_p[:, :, :], over_e(mx), ALU.max))
                    step(dve.scalar_tensor_tensor(out=r_c[:, :, :], in0=both[:, :, :], scalar=JITTER2,
                                                  in1=r_a[:, :, :], op0=ALU.mult, op1=ALU.add))
                    step(dve.scalar_tensor_tensor(out=r_b[:, :, :], in0=r_c[:, :, :], scalar=0.0,
                                                  in1=r_b[:, :, :], op0=ALU.is_ge, op1=ALU.mult))
                    if c == 1:
                        step(dve.tensor_scalar(r_c[:, :, :], pick[:, 0], -1.0, 1.0, ALU.mult, ALU.add))
                        step(dve.tensor_tensor(r_b[:, :, :], r_b[:, :, :], r_c[:, :, :], ALU.mult))
                    step(dve.tensor_reduce(r_k[:, :], r_b[:, :, :], AX.X, ALU.add))
                    step(dve.reciprocal(weight[:, t0:t0 + HT, c], r_k[:, :]))
                step(dve.tensor_tensor(both[:, :, :], pick[:, 0], pick[:, 1], ALU.add))
                dve.sem_inc(counts_mm, 1)
                dve.wait_ge(counts_mm, 2 * half + 2)
                by_e = [v[:, :, :].rearrange("p t e -> p (t e)").rearrange("p (e t) -> p e t", e=E0)
                        for v in (r_a, r_b)]
                counts = bank[7][:, HT * E0:2 * HT * E0].rearrange("p (t e) -> p e t", e=E0)
                rank = bank[7][:, 0:HT * E0].rearrange("p (t e) -> p e t", e=E0)
                flat = [v[:, :, :].rearrange("p t e -> p (t e)") for v in (r_a, r_b, r_c)]
                step(dve.tensor_copy(by_e[0], counts))
                step(dve.tensor_tensor_scan(flat[1], const_of("restart"), flat[0], 0.0, ALU.mult, ALU.add))
                step(dve.tensor_scalar(n_f[:, :], by_e[1][:, :, HT - 1], float(P - 1), None, ALU.add))
                step(dve.tensor_copy(n_i[:, :], n_f[:, :]))
                step(dve.tensor_scalar(n_i[:, :], n_i[:, :], 7, 7, ALU.logical_shift_right, ALU.logical_shift_left))
                step(dve.tensor_copy(n_f[:, :], n_i[:, :]))
                step(dve.tensor_tensor_scan(n_end[:, :], const_of("ones")[:, 0:E0], n_f[:, :], 0.0,
                                            ALU.mult, ALU.add))
                step(dve.tensor_tensor(n_base[:, :], n_end[:, :], n_f[:, :], ALU.subtract))
                step(dve.tensor_tensor(flat[1], flat[1], flat[0], ALU.subtract))
                step(dve.tensor_tensor(by_e[1], by_e[1], rank, ALU.add))
                step(dve.tensor_tensor(by_e[1], by_e[1],
                                       n_base[:, :].unsqueeze(2).to_broadcast([P, E0, HT]), ALU.add))
                for c in range(2):
                    step(dve.tensor_tensor(r_c[:, :, :], pick[:, c], by_e[1].rearrange("p e t -> p t e"), ALU.mult))
                    step(dve.tensor_reduce(slot_f[:, :], r_c[:, :, :], AX.X, ALU.add))
                    step(dve.tensor_scalar(slot_i[:, t0:t0 + HT, c], slot_f[:, :], float(base), None, ALU.add))
                step(dve.tensor_tensor(tile_e[:, :, :],
                                       const_of("tile_start", 1).unsqueeze(2).to_broadcast([1, ROUTED, E0]),
                                       n_end[0:1, :].unsqueeze(1).to_broadcast([1, ROUTED, E0]), ALU.is_ge))
                step(dve.tensor_reduce(tile_ef[:, :], tile_e[:, :, :], AX.X, ALU.add))
                dve.tensor_scalar(expert_of[:, half * ROUTED:(half + 1) * ROUTED], tile_ef[:, :],
                                  float(E0 - 1), None, ALU.min).then_inc(routed, 1)

            route(0)
            looped(dve, HG + 2, GROUPS - 2, stage_a(True, True, True))
            straight(GROUPS - 2, GROUPS - 1, stage_a(True, True, True))
            straight(GROUPS - 1, GROUPS, stage_a(False, True, True))
            straight(GROUPS, GROUPS + 1, stage_a(False, False, True))
            dve.wait_ge(routed, 1)
            route(1)

            for s in range(2):
                dve.wait_ge(x1_out[s], 16 * GROUPS // 2)
                dve.wait_ge(n1_out[s], 16 * GROUPS // 2)

            def copy_xsT(i):
                dve.wait_ge(xsT_mm, i.n + 1)
                wait(dve, w3_mm, i.n - 1)
                dve.tensor_copy(xsT[:, i.slot].rearrange("p k n -> p (k n)"), bank[1][:, 0:D]
                                ).then_inc(xsT_ready, 1)

            def mul_h(i):
                dve.wait_ge(gelu_done, i.n + 1)
                dve.wait_ge(w3_mm, i.n + 1)
                wait(dve, hsT_mm, i.n - 1)
                dve.tensor_tensor(h_sb[:, i.slot], bank[4 + i.slot][:, :], g_sb[:, i.slot], ALU.mult
                                  ).then_inc(h_done, 1)

            def copy_y(i):
                dve.wait_ge(y_mm, i.n + 1)
                wait(dve, ys_out[i.slot], 16 * i.used)
                dve.tensor_copy(y_sb[:, i.slot], bank[6 + i.slot][:, 0:D]).then_inc(y_ready, 1)

            def stage_f(first, second, third):
                def body(h, par):
                    if first:
                        copy_xsT(At(h, par))
                    if second:
                        mul_h(At(h, par, -1))
                    if third:
                        copy_y(At(h, par, -2))
                return body

            straight(0, 1, stage_f(True, False, False))
            straight(1, 2, stage_f(True, True, False))
            straight(2, 6, stage_f(True, True, True))
            looped(dve, 6, ITEMS, stage_f(True, True, True))
            straight(ITEMS, ITEMS + 1, stage_f(False, True, True))
            straight(ITEMS + 1, ITEMS + 2, stage_f(False, False, True))

            n2_prev = sem("n2_prev")
            dve.wait_ge(y_mm, ITEMS)
            for s in range(2):
                dve.wait_ge(ys_out[s], 16 * ITEMS // 2)
            dve.memset(n3z.rearrange("p j k g n -> p (j k g n)"), 0.0).then_inc(route_step, 1)
            steps[0] += 1
            dve.wait_ge(route_step, steps[0])

            def add_x2(g):
                dve.wait_ge(x1c_in[g.slot], 16 * (g.used + 1))
                dve.wait_ge(yg_in[g.slot], 2 * GT * 16 * (g.used + 1))
                wait(dve, x3_done, g.n - 1)
                for c in range(2):
                    for j in range(GT):
                        ins = dve.scalar_tensor_tensor(
                            out=x2[:, g.slot, j], in0=yg[:, g.slot, j, c],
                            scalar=weight[:, ds(g.n * GT + j, 1), c],
                            in1=(x1c if c == 0 else x2)[:, g.slot, j], op0=ALU.mult, op1=ALU.add)
                    if c == 0:
                        ins.then_inc(half_sum, 1)
                        dve.wait_ge(half_sum, g.n + 1)
                ins.then_inc(x2_done, 1)

            def stats_x2(g):
                dve.wait_ge(x2_done, g.n + 1)
                norm_stats(g, x2[:, g.slot], st1, st3_done, mv1, mv3_done, n2_done)

            def norm_x2(g):
                dve.wait_ge(rstd3_done, g.n + 1)
                wait(dve, a_mm[0], 2 * (g.n - 1))
                for j in range(GT):
                    ins = norm_rows(g, j, n2[:, g.slot], x2[:, g.slot], mv1, rstd1)
                ins.then_inc(n2_done, 1)

            def add_bias(g, layer):
                for pair in range(2):
                    part = hsum[:, 2 * pair:2 * pair + 2]
                    dve.wait_ge(b_mm[layer], 2 * g.n + pair + 1)
                    if layer:
                        dve.wait_ge(relu_done[layer - 1], 2 * g.n + pair + 1)
                    else:
                        wait(dve, x3_done, g.n)
                    dve.tensor_tensor(part, bank[2 + pair].rearrange("p (j n) -> p j n", j=2),
                                      gb_sb[:, layer].unsqueeze(1).to_broadcast([P, 2, D]), ALU.add
                                      ).then_inc(b_added[layer], 1)

            def add_x3(g):
                dve.wait_ge(b_added[2], 2 * g.n + 2)
                wait(dve, out_done, g.n - 1)
                dve.tensor_tensor(x3[:, g.slot].rearrange("p j n -> p (j n)"),
                                  hsum.rearrange("p j n -> p (j n)"),
                                  x2[:, g.slot].rearrange("p j n -> p (j n)"), ALU.add).then_inc(x3_done, 1)

            def norm_x3(g):
                dve.wait_ge(x3_done, g.n + 1)
                norm_stats(g, x3[:, g.slot], st2, st4_done, mv2, mv4_done, n3_done)

            def apply_x3(g):
                dve.wait_ge(rstd4_done, g.n + 1)
                wait(dve, n3T_mm, 2 * g.n)
                for j in range(GT):
                    ins = norm_rows(g, j, n3, x3[:, g.slot], mv2, rstd2)
                ins.then_inc(n3_done, 1)

            def graph_sum(g):
                dve.wait_ge(n3z_ready, 2 * g.n + 2)
                wait(dve, lg_mm, g.n)
                for b in range(2):
                    ins = dve.tensor_reduce(
                        m_T[:, :, :, b].rearrange("p k j -> p j k"),
                        n3z[:, :, :, b, b * NODES:(b + 1) * NODES], AX.X, ALU.add)
                ins.then_inc(m_done, 1)

            def graph_gate(g):
                at = [0]

                def link(ins):
                    at[0] += 1
                    ins.then_inc(gate_step, 1)
                    dve.wait_ge(gate_step, GATE_STEPS * g.n + at[0])

                dve.wait_ge(lg_mm, g.n + 1)
                link(dve.scalar_tensor_tensor(out=lg[:, :], in0=bank[4][0:2 * GT, 0:E1], scalar=1.0 / NODES,
                                              in1=bg1_sb[:, :], op0=ALU.mult, op1=ALU.add))
                link(dve.tensor_reduce(lg_s[:, 0:1], lg[:, :], AX.X, ALU.max))
                link(dve.tensor_scalar(lg_k[:, :], lg[:, :], lg_s[:, 0:1], None, ALU.subtract))
                link(dve.tensor_scalar(lg[:, :], lg[:, :], lg_s[:, 0:1], None, ALU.is_ge))
                link(dve.tensor_tensor(lg[:, :], lg[:, :], const_of("rev1", 2 * GT), ALU.mult))
                link(dve.tensor_reduce(lg_s[:, 1:2], lg[:, :], AX.X, ALU.max))
                link(dve.tensor_scalar(lg_s[:, 1:2], lg_s[:, 1:2], -1.0, float(E1), ALU.mult, ALU.add))
                dve.wait_ge(lg_exp, g.n + 1)
                link(dve.reciprocal(lg_s[:, 3:4], lg_s[:, 2:3]))
                link(dve.tensor_scalar(spread[:, 0], const_of("own_tile", 2 * GT), lg_s[:, 3:4], None, ALU.mult))
                link(dve.tensor_scalar(spread[:, 1], const_of("own_tile", 2 * GT), lg_s[:, 1:2], None, ALU.mult))
                assert at[0] == GATE_STEPS
                dve.sem_inc(spread_done, 1)

            def take_gate(g):
                dve.wait_ge(spread_mm, g.n + 1)
                wait(dve, out_done, g.n - 1)
                wait(dve, beg_in[g.slot], GT * 16 * g.used)
                dve.tensor_copy(gate[:, g.slot], bank[4][:, E1:E1 + GT])
                dve.tensor_copy(expert[:, g.slot], bank[4][:, E1 + GT:E1 + 2 * GT]).then_inc(expert_ready, 1)

            def finish(g):
                dve.wait_ge(beg_in[g.slot], GT * 16 * (g.used + 1))
                wait(dve, ygate_done, g.n)
                for pair in range(2):
                    dve.wait_ge(out_mm, 2 * g.n + pair + 1)
                    dve.tensor_tensor(ysum[:, 2 * pair:2 * pair + 2].rearrange("p j n -> p (j n)"),
                                      bank[6 + pair][:, :],
                                      beg[:, g.slot, 2 * pair:2 * pair + 2].rearrange("p j n -> p (j n)"),
                                      ALU.add).then_inc(ysum_done, 1)
                dve.wait_ge(ysum_done, 2 * g.n + 2)
                wait(dve, out_out[g.slot], 16 * g.used)
                for j in range(GT):
                    ins = dve.scalar_tensor_tensor(out=outc[:, g.slot, j], in0=ysum[:, j],
                                                   scalar=gate[:, g.slot, j:j + 1], in1=x3[:, g.slot, j],
                                                   op0=ALU.mult, op1=ALU.add)
                ins.then_inc(out_done, 1)
                dve.wait_ge(out_done, g.n + 1)
                dve.sem_inc(ygate_done, 1)

            def stage_c(nxt, cur, prev):
                def body(h, par):
                    g1, g, gp = (At(h, par, d) for d in (1, 0, -1))
                    if prev:
                        norm_x3(gp)
                        apply_x3(gp)
                    if cur:
                        add_bias(g, 0)
                    if prev:
                        graph_sum(gp)
                        graph_gate(gp)
                    if nxt:
                        add_x2(g1)
                    if cur:
                        add_bias(g, 1)
                    if prev:
                        take_gate(gp)
                    if nxt:
                        stats_x2(g1)
                        norm_x2(g1)
                    if cur:
                        add_bias(g, 2)
                        add_x3(g)
                    if prev:
                        finish(gp)
                return body

            add_x2(At(0, 0))
            stats_x2(At(0, 0))
            norm_x2(At(0, 0))
            straight(0, 1, stage_c(True, True, False))
            straight(1, 4, stage_c(True, True, True))
            looped(dve, 4, GROUPS - 2, stage_c(True, True, True))
            straight(GROUPS - 2, GROUPS - 1, stage_c(True, True, True))
            straight(GROUPS - 1, GROUPS, stage_c(False, True, True))
            straight(GROUPS, GROUPS + 1, stage_c(False, False, True))


def shape_constants():
    import numpy as np

    c = np.zeros((P, CONST_COLS), np.float32)
    i = np.arange(P)

    def put(name, value):
        n, at = CONST[name]
        c[:, at:at + n] = value

    put("ident", i[:, None] == i[None, :])
    put("before", i[:, None] < i[None, :])
    put("ones", 1.0)
    put("half_of", (i[:, None] % 2) == (i[None, :] // NODES))
    put("own_tile", (i[:, None] // 2) == np.arange(GT)[None, :])
    put("rev0", E0 - np.arange(E0))
    put("rev1", E1 - np.arange(E1))
    put("restart", np.arange(E0 * HT) % HT != 0)
    put("tile_start", P * np.arange(ROUTED))
    put("eps", EPS)
    put("minus_half", -0.5)
    return c


def kernel(x, adj, nodemask, L0_gnn_Wqk, L0_gnn_Wv, L0_ffn_wg, L0_ffn_bg, L0_ffn_w1, L0_ffn_w3, L0_ffn_w2,
           L1_gnn_W1, L1_gnn_b1, L1_gnn_W2, L1_gnn_b2, L1_gnn_W3, L1_gnn_b3, L1_ffn_Wg, L1_ffn_bg, L1_ffn_We,
           L1_ffn_be):
    import numpy as np
    import concourse.bacc as bacc
    from concourse.bass_utils import run_bass_kernel_spmd

    nc = bacc.Bacc("TRN2", target_bir_lowering=False, num_devices=1)
    arrays = {}

    def give(name, a):
        a = np.ascontiguousarray(a)
        arrays[name] = a
        return nc.dram_tensor(name, a.shape, mybir.dt.from_np(a.dtype), kind="ExternalInput").ap()

    def row(a):
        return np.asarray(a)

    args = dict(
        x=give("in_x", np.asarray(x).reshape(TOKENS, D)),
        adjT=give("in_adjT", np.asarray(adj).transpose(0, 2, 1)),
        maskT=give("in_maskT", np.asarray(nodemask).reshape(TILES, P).T),
        wqkT=give("in_wqkT", np.asarray(L0_gnn_Wqk).T),
        wv=give("in_wv", L0_gnn_Wv),
        wg0=give("in_wg0", L0_ffn_wg), bg0=give("in_bg0", row(L0_ffn_bg)),
        w1=give("in_w1", L0_ffn_w1), w3=give("in_w3", L0_ffn_w3), w2=give("in_w2", L0_ffn_w2),
        gw=[give(f"in_gw{i}", w) for i, w in enumerate((L1_gnn_W1, L1_gnn_W2, L1_gnn_W3))],
        gb=[give(f"in_gb{i}", row(b)) for i, b in enumerate((L1_gnn_b1, L1_gnn_b2, L1_gnn_b3))],
        wg1=give("in_wg1", L1_ffn_Wg), bg1=give("in_bg1", row(L1_ffn_bg)),
        we=give("in_we", L1_ffn_We), be=give("in_be", L1_ffn_be),
        const=give("in_const", shape_constants()),
    )
    out = nc.dram_tensor("out", (TOKENS, D), F32, kind="ExternalOutput").ap()
    program(nc, out=out, **args)
    r = run_bass_kernel_spmd(nc, [arrays], core_ids=[0])
    return r.results[0]["out"].reshape(GRAPHS, NODES, D)
```

```python
from contextlib import ExitStack

import concourse.bass as bass
from concourse import mybir
from concourse.bass import IndirectOffsetOnAxis, ds

F32 = mybir.dt.float32
I32 = mybir.dt.int32
U32 = mybir.dt.uint32
ALU = mybir.AluOpType
ACT = mybir.ActivationFunctionType
AX = mybir.AxisListType

P = 128
GRAPHS, NODES, D = 128, 64, 256
TOKENS = GRAPHS * NODES
TILES = TOKENS // P
GT = 4
GROUPS = TILES // GT
KD = D // P
E0, F0 = 8, 512
KF = F0 // P
E1 = 16
FG = 6
PART_T0 = (0, FG * GT)
PART_T = (FG * GT, TILES - FG * GT)
HT = max(PART_T)
MOST_PAD = E0 * (P - 1) // P
PART_ITEMS = tuple(2 * t + MOST_PAD for t in PART_T)
FI = PART_ITEMS[0]
ITEMS = sum(PART_ITEMS)
SPARE = E0
EPS = 1e-5
JITTER2 = 2.0 * 0.01
ATT_SCALE = 1.0 / float(D) ** 0.5

CONST = {}
_at = 0
for _name, _n in (("ident", P), ("before", P), ("ones", P), ("half_of", P), ("own_tile", GT),
                  ("rev0", E0), ("rev1", E1), ("restart0", E0 * PART_T[0]),
                  ("restart1", E0 * PART_T[1]), ("tile_start", max(PART_ITEMS)), ("row", 1),
                  ("spare0", SPARE), ("spare1", SPARE), ("eps", GT), ("minus_half", GT)):
    CONST[_name] = (_n, _at)
    _at += _n
CONST_COLS = _at


def wait(eng, sem, value):
    if isinstance(value, int) and value <= 0:
        return
    eng.wait_ge(sem, value)


class At:

    def __init__(self, h, parity, shift=0):
        self.n = 2 * h + parity + shift
        self.slot = (parity + shift) % 2
        self.used = h + (parity + shift) // 2


def straight(first, last, body):
    for k in range(first, last):
        body(k // 2, k % 2)


def looped(eng, first, last, body):
    with eng.Fori(first // 2, last // 2, 1) as h:
        body(h, 0)
        body(h, 1)


def program(nc, x, adjT, maskT, wqkT, wv, wg0, bg0, w1, w3, w2, gw, gb, wg1, bg1, we, be, const, out):
    ctx = ExitStack()
    with ctx:
        def sb(name, shape, dt=F32):
            return ctx.enter_context(nc.sbuf_tensor(name, shape, dt))

        def sem(name):
            return ctx.enter_context(nc.semaphore(name))

        def dram(name, rows):
            return nc.dram_tensor(name, [rows, D], F32, kind="Internal").ap()

        x1_dram = dram("x1_dram", TOKENS)
        n1_dram = dram("n1_dram", TOKENS)
        xs_dram = [dram(f"xs_dram{part}", (PART_ITEMS[part] + SPARE) * P) for part in range(2)]
        ys_dram = [dram(f"ys_dram{part}", PART_ITEMS[part] * P) for part in range(2)]

        big = sb("big", [P, E0 * (2 * KD * F0 + KF * D)])
        mid = sb("mid", [P, 14336])
        cst = sb("cst", [P, CONST_COLS])
        mask = sb("mask", [P, TILES])
        mp = sb("mp", [P, KD, D])
        wv_sb = sb("wv_sb", [P, KD, D])
        wg0_sb = sb("wg0_sb", [P, KD, E0])
        bg0_sb = sb("bg0_sb", [P, E0])
        gw_sb = sb("gw_sb", [P, 3, KD, D])
        gb_sb = sb("gb_sb", [P, 3, D])
        wg1_sb = sb("wg1_sb", [P, KD, E1])
        bg1_sb = sb("bg1_sb", [2 * GT, E1])
        zero = sb("zero", [P, D])
        n2 = sb("n2", [P, 2, GT, D])

        def const_of(name, rows=P):
            n, at = CONST[name]
            return cst[0:rows, at:at + n]

        ident = const_of("ident")

        class Carve:

            def __init__(self, buf):
                self.buf, self.at = buf, 0

            def __call__(self, n, pattern=None, **sizes):
                part = self.buf[:, self.at:self.at + n]
                self.at += n
                return part.rearrange(pattern, **sizes) if pattern else part

        c = Carve(mid)
        adj_sb = c(2 * GT * P, "p (s j n) -> p s j n", s=2, j=GT)
        xin = c(2 * GT * D, "p (s j n) -> p s j n", s=2, j=GT)
        xn = c(2 * GT * D, "p (s j n) -> p s j n", s=2, j=GT)
        tt = c(GT * 2 * D, "p (j a k n) -> p j a k n", j=GT, a=2, k=KD)
        v_sb = c(2 * GT * D, "p (s j n) -> p s j n", s=2, j=GT)
        x1 = c(2 * GT * D, "p (s j n) -> p s j n", s=2, j=GT)
        n1 = c(2 * GT * D, "p (s j n) -> p s j n", s=2, j=GT)
        n1T = c(GT * D, "p (j k n) -> p j k n", j=GT, k=KD)
        assert c.at <= 14336, c.at
        wqk_stage = tt.rearrange("p j a k n -> p (j a k n)")[:, 0:4 * D]\
            .rearrange("p (h k n) -> p h k n", h=2, k=KD)
        c = Carve(big)
        w13_sb = [c(E0 * KD * F0) for _ in range(2)]
        w2_sb = c(E0 * KF * D)
        c = Carve(mid)
        c(2 * GT * P)
        x1c = c(2 * GT * D, "p (s j n) -> p s j n", s=2, j=GT)
        yg = c(2 * GT * 2 * D, "p (s j c n) -> p s j c n", s=2, j=GT, c=2)
        x2 = c(2 * GT * D, "p (s j n) -> p s j n", s=2, j=GT)
        c(2 * F0)
        assert c.at == 9216 + 2 * F0
        c(2 * F0)
        hT = c(GT * D, "p (j k n) -> p j k n", j=GT, k=KD)
        hsum = c(GT * D, "p (j n) -> p j n", j=GT)
        assert c.at <= 14336, c.at
        c = Carve(mid)
        c(9216)
        g_sb = c(2 * F0, "p (s n) -> p s n", s=2)
        h_sb = c(2 * F0, "p (s n) -> p s n", s=2)
        hsT = c(2 * F0, "p (s k n) -> p s k n", s=2, k=KF)
        y_sb = c(2 * D, "p (s n) -> p s n", s=2)
        xs = c(2 * D, "p (s n) -> p s n", s=2)
        xsT = c(2 * D, "p (s k n) -> p s k n", s=2, k=KD)
        assert c.at <= 14336, c.at
        c = Carve(big)
        we_sb = c(E1 * KD * D)
        hrelu = c(GT * D, "p (j n) -> p j n", j=GT)
        x3 = c(2 * GT * D, "p (s j n) -> p s j n", s=2, j=GT)
        n3 = c(GT * D, "p (j n) -> p j n", j=GT)
        n3z = c(GT * KD * 2 * P, "p (j k g n) -> p j k g n", j=GT, k=KD, g=2)
        beg = c(2 * GT * D, "p (s j n) -> p s j n", s=2, j=GT)
        ysum = c(GT * D, "p (j n) -> p j n", j=GT)
        outc = c(2 * GT * D, "p (s j n) -> p s j n", s=2, j=GT)
        assert c.at <= 24576, c.at

        st1 = sb("st1", [P, GT, 6])
        mv1 = sb("mv1", [P, GT, 2])
        ve1 = sb("ve1", [P, GT])
        rstd1 = sb("rstd1", [P, GT])
        st2 = sb("st2", [P, GT, 6])
        mv2 = sb("mv2", [P, GT, 2])
        ve2 = sb("ve2", [P, GT])
        rstd2 = sb("rstd2", [P, GT])
        w_col = sb("w_col", [P, 2, GT])
        w_masked = sb("w_masked", [P, GT])
        w_max = sb("w_max", [GT, 2])
        w_sub = sb("w_sub", [GT, 2, NODES])
        w_exp = sb("w_exp", [GT, 2, NODES])
        w_sum = sb("w_sum", [GT, 2])
        w_rcp = sb("w_rcp", [GT, 2])
        w_prob = sb("w_prob", [GT, 2, NODES])
        p_col = sb("p_col", [P, GT])
        logit = sb("logit", [P, TILES, E0])
        r_a = sb("r_a", [P, HT, E0])
        r_b = sb("r_b", [P, HT, E0])
        r_c = sb("r_c", [P, HT, E0])
        r_p = sb("r_p", [P, HT, E0])
        pick = sb("pick", [P, 2, HT, E0])
        both = sb("both", [P, HT, E0])
        top = sb("top", [P, 2, HT])
        r_k = sb("r_k", [P, HT])
        weight = sb("weight", [P, TILES, 2])
        slot_f = sb("slot_f", [P, HT])
        slot_i = sb("slot_i", [P, TILES, 2], I32)
        n_f = sb("n_f", [P, E0])
        n_i = sb("n_i", [P, E0], I32)
        n_end = sb("n_end", [P, E0])
        n_base = sb("n_base", [P, E0])
        tile_e = sb("tile_e", [1, max(PART_ITEMS), E0])
        tile_ef = sb("tile_ef", [1, max(PART_ITEMS)])
        pad_f = sb("pad_f", [P, E0])
        pad_ok = sb("pad_ok", [P, E0])
        pad_i = sb("pad_i", [P, 2, E0], I32)
        expert_of = sb("expert_of", [1, ITEMS], I32)
        xg = sb("xg", [P, 2, GT, D])
        slot_now = sb("slot_now", [P, 2, GT * 2], I32)
        m_T = sb("m_T", [P, KD, GT, 2])
        lg = sb("lg", [2 * GT, E1])
        lg_e = sb("lg_e", [2 * GT, E1])
        lg_k = sb("lg_k", [2 * GT, E1])
        lg_s = sb("lg_s", [2 * GT, 4])
        spread = sb("spread", [2 * GT, 2, GT])
        gate = sb("gate", [P, 2, GT])
        expert = sb("expert", [P, 2, GT], I32)

        bank = [ctx.enter_context(nc.psum_tensor(f"bank{i}", [P, 512], F32)) for i in range(8)]

        consts_in = sem("consts_in")
        early_in = sem("early_in")
        padded = sem("padded")
        x_copied = sem("x_copied")
        rank_read = sem("rank_read")
        wqk_in = sem("wqk_in")
        zeroed = sem("zeroed")
        mp_mm = sem("mp_mm")
        mp_ready = sem("mp_ready")
        experts_in = sem("experts_in")
        rows_zeroed = sem("rows_zeroed")
        xin_in = [sem(f"xin_in{s}") for s in range(2)]
        adj_in = [sem(f"adj_in{s}") for s in range(2)]
        x1_out = [sem(f"x1_out{s}") for s in range(2)]
        n1_out = [sem(f"n1_out{s}") for s in range(2)]
        st1_done = sem("st1_done")
        mv1_done = sem("mv1_done")
        ve1_done = sem("ve1_done")
        rstd1_done = sem("rstd1_done")
        xn_done = sem("xn_done")
        st2_done = sem("st2_done")
        mv2_done = sem("mv2_done")
        ve2_done = sem("ve2_done")
        rstd2_done = sem("rstd2_done")
        n1_done = sem("n1_done")
        adj_masked = sem("adj_masked")
        tt_mm = sem("tt_mm")
        tt_ready = sem("tt_ready")
        uv_mm = sem("uv_mm")
        v_ready = sem("v_ready")
        w_dot = sem("w_dot")
        w_masked_done = sem("w_masked_done")
        w_row = sem("w_row")
        w_max_done = sem("w_max_done")
        w_sub_done = sem("w_sub_done")
        w_exp_done = sem("w_exp_done")
        w_sum_done = sem("w_sum_done")
        w_rcp_done = sem("w_rcp_done")
        w_prob_done = sem("w_prob_done")
        p_mm = sem("p_mm")
        p_col_done = sem("p_col_done")
        x1_done = sem("x1_done")
        n1T_mm = sem("n1T_mm")
        n1T_ready = sem("n1T_ready")
        logit_mm = sem("logit_mm")
        logit_ready = sem("logit_ready")
        route_step = sem("route_step")
        route_exp = sem("route_exp")
        both_ready = sem("both_ready")
        counts_mm = sem("counts_mm")
        counts_read = sem("counts_read")
        ranks_mm = sem("ranks_mm")
        routed = sem("routed")
        xg_in = [sem(f"xg_in{s}") for s in range(2)]
        slots_copied = sem("slots_copied")
        scattered = [sem(f"scattered{s}") for s in range(2)]
        xs_in = [sem(f"xs_in{s}") for s in range(2)]
        xsT_mm = sem("xsT_mm")
        xsT_ready = sem("xsT_ready")
        w1_mm = sem("w1_mm")
        w3_mm = sem("w3_mm")
        gelu_done = sem("gelu_done")
        h_done = sem("h_done")
        hsT_mm = sem("hsT_mm")
        hsT_ready = sem("hsT_ready")
        y_mm = sem("y_mm")
        y_ready = sem("y_ready")
        ys_out = [sem(f"ys_out{s}") for s in range(2)]
        we_in = sem("we_in")
        n3z_zeroed = sem("n3z_zeroed")
        x1c_in = [sem(f"x1c_in{s}") for s in range(2)]
        adjc_in = [sem(f"adjc_in{s}") for s in range(2)]
        yg_in = [sem(f"yg_in{s}") for s in range(2)]
        beg_in = [sem(f"beg_in{s}") for s in range(2)]
        out_out = [sem(f"out_out{s}") for s in range(2)]
        half_sum = sem("half_sum")
        x2_done = sem("x2_done")
        st3_done = sem("st3_done")
        mv3_done = sem("mv3_done")
        ve3_done = sem("ve3_done")
        rstd3_done = sem("rstd3_done")
        n2_done = sem("n2_done")
        a_mm = [sem(f"a_mm{i}") for i in range(3)]
        a_ready = [sem(f"a_ready{i}") for i in range(3)]
        b_mm = [sem(f"b_mm{i}") for i in range(3)]
        b_added = [sem(f"b_added{i}") for i in range(3)]
        relu_done = [sem(f"relu_done{i}") for i in range(2)]
        x3_done = sem("x3_done")
        st4_done = sem("st4_done")
        mv4_done = sem("mv4_done")
        ve4_done = sem("ve4_done")
        rstd4_done = sem("rstd4_done")
        n3_done = sem("n3_done")
        n3T_mm = sem("n3T_mm")
        n3z_ready = sem("n3z_ready")
        m_done = sem("m_done")
        lg_mm = sem("lg_mm")
        gate_step = sem("gate_step")
        lg_exp = sem("lg_exp")
        spread_done = sem("spread_done")
        spread_mm = sem("spread_mm")
        expert_ready = sem("expert_ready")
        out_mm = sem("out_mm")
        ysum_done = sem("ysum_done")
        ygate_done = sem("ygate_done")
        out_done = sem("out_done")
        sp_held = sem("sp_held")
        pe_held = sem("pe_held")
        act_held = sem("act_held")
        dve_held = sem("dve_held")
        pool_held = sem("pool_held")

        EARLY, CONSTS = 3, 10
        SCATTER_FROM = 12
        SCATTER_TILES = ((0,), (1, 2), (3,))
        ROUTE_STEPS = (8, 9, 10, 11)
        X2_AT = FI + 41
        ROUTE_F_STEPS = (2, 3, 4, 5)
        GATE_STEPS, EXP_AFTER = 10, 3
        blk = ctx.enter_context(nc.Block())

        def tokens4(t, g):
            return t[ds(g * (GT * P), GT * P), :].rearrange("(j p) n -> p j n", p=P)

        @blk.sync
        def _(sp):
            def load(dst, src, done):
                sp.dma_start(dst, src).then_inc(done, 16)

            def by_k(w):
                return w.rearrange("(k p) n -> p k n", p=P)

            load(wqk_stage, wqkT.rearrange("(h k p) n -> p h k n", h=2, p=P), wqk_in)
            load(xin[:, 0], tokens4(x, 0), xin_in[0])
            load(cst[:, :], const, early_in)
            load(mask[:, :], maskT, early_in)
            load(wv_sb[:, :, :], by_k(wv), early_in)
            sp.wait_ge(zeroed, 2)

            def load_adj(g, sems, free_sem, free_at):
                wait(sp, free_sem, free_at)
                for b in range(2):
                    rows = slice(b * NODES, (b + 1) * NODES)
                    sp.dma_start(adj_sb[rows, g.slot, :, rows],
                                 adjT[ds(g.n * (GT * 2), GT * 2), :, :]
                                 .rearrange("(j b) p n -> b p j n", b=2)[b]).then_inc(sems[g.slot], 16)

            def load_x(g):
                wait(sp, x_copied, g.n - 1)
                sp.sem_inc(sp_held, 1)
                wait(sp, xn_done, GT * (g.n - 1))
                sp.dma_start(xin[:, g.slot], tokens4(x, g.n)).then_inc(xin_in[g.slot], 16)

            def store_x1(g):
                sp.wait_ge(x1_done, g.n + 1)
                sp.dma_start(tokens4(x1_dram, g.n), x1[:, g.slot]).then_inc(x1_out[g.slot], 16)

            def store_n1(g):
                sp.wait_ge(n1_done, g.n + 1)
                sp.dma_start(tokens4(n1_dram, g.n), n1[:, g.slot]).then_inc(n1_out[g.slot], 16)

            def load_expert(e):
                for w_sb, w in ((w13_sb[0], w1), (w13_sb[1], w3), (w2_sb, w2)):
                    n = KD * F0
                    sp.dma_start(w_sb[:, ds(e * n, n)].rearrange("p (k n) -> p k n", n=w.shape[2]),
                                 w[ds(e, 1), :, :].rearrange("e (k p) n -> p (e k) n", p=P)
                                 ).then_inc(experts_in, 16)

            def stage_a(nxt2, nxt, prev, expert=False):
                def body(h, par):
                    g1, g0 = At(h, par, 1), At(h, par, -1)
                    if expert:
                        load_expert(2 * h + par - 2)
                    if nxt:
                        load_adj(g1, adj_in, tt_mm, GT * (g1.n - 1))
                    if nxt2:
                        load_x(At(h, par, 2))
                    if prev:
                        store_x1(g0)
                        store_n1(g0)
                return body

            load_adj(At(0, 0), adj_in, tt_mm, 0)
            load_x(At(0, 1))
            for dst, src in (
                (wg0_sb[:, :, :], by_k(wg0)), (bg0_sb[:, :], bg0.partition_broadcast(P)),
                (gw_sb[:, 0], by_k(gw[0])), (gw_sb[:, 1], by_k(gw[1])), (gw_sb[:, 2], by_k(gw[2])),
                (gb_sb[:, 0], gb[0].partition_broadcast(P)), (gb_sb[:, 1], gb[1].partition_broadcast(P)),
                (gb_sb[:, 2], gb[2].partition_broadcast(P)),
                (wg1_sb[:, :, :], by_k(wg1)), (bg1_sb[:, :], bg1.partition_broadcast(2 * GT)),
            ):
                load(dst, src, consts_in)
            for part, end in enumerate(PART_ITEMS):
                sp.dma_start(xs_dram[part][(end - MOST_PAD) * P:end * P, :].rearrange("(i p) n -> p i n", p=P),
                             zero[:, :].unsqueeze(1).to_broadcast([P, MOST_PAD, D])).then_inc(rows_zeroed, 16)
            straight(0, 1, stage_a(True, True, False))
            straight(1, 2, stage_a(True, True, True))
            looped(sp, 2, 2 + E0, stage_a(True, True, True, True))
            looped(sp, 2 + E0, GROUPS - 2, stage_a(True, True, True))
            straight(GROUPS - 2, GROUPS - 1, stage_a(False, True, True))
            straight(GROUPS - 1, GROUPS + 1, stage_a(False, False, True))

            def load_rows(i, part):
                wait(sp, xsT_mm, i.n - 1)
                sp.dma_start(xs[:, i.slot], xs_dram[part][ds((i.n - part * FI) * P, P), :]
                             ).then_inc(xs_in[i.slot], 16)

            def store_rows(i, part):
                sp.wait_ge(y_ready, i.n + 1)
                sp.dma_start(ys_dram[part][ds((i.n - part * FI) * P, P), :], y_sb[:, i.slot]
                             ).then_inc(ys_out[i.slot], 16)

            def stage_f(load_part, store_part):
                def body(h, par):
                    load_rows(At(h, par), load_part)
                    store_rows(At(h, par, -4), store_part)
                return body

            def part_scattered(groups, part):
                for s in range(2):
                    sp.wait_ge(scattered[s], (groups // 2) * GT * 2 * 16)
                sp.wait_ge(padded, (part + 1) * E0 * 16)

            for s in range(2):
                sp.wait_ge(x1_out[s], 16 * GROUPS // 2)
                sp.wait_ge(n1_out[s], 16 * GROUPS // 2)
            sp.wait_ge(n1T_mm, 2 * GROUPS)

            def load_c(g):
                wait(sp, x2_done, g.n - 1)
                sp.dma_start(x1c[:, g.slot], tokens4(x1_dram, g.n)).then_inc(x1c_in[g.slot], 16)

            def load_adj_c(g):
                load_adj(g, adjc_in, a_mm[2], 2 * (g.n - 1))

            part_scattered(FG, 0)
            straight(0, 4, lambda h, par: load_rows(At(h, par), 0))
            straight(4, 6, stage_f(0, 0))
            looped(sp, 6, FI - 1, stage_f(0, 0))
            straight(FI - 1, FI, stage_f(0, 0))
            part_scattered(GROUPS, 1)
            straight(FI, FI + 4, stage_f(1, 0))
            straight(FI + 4, FI + 5, stage_f(1, 1))
            for par in range(2):
                load_c(At(0, par))
                load_adj_c(At(0, par))
            looped(sp, FI + 5, ITEMS, stage_f(1, 1))

            straight(ITEMS, ITEMS + 4, lambda h, par: store_rows(At(h, par, -4), 1))
            sp.wait_ge(y_mm, ITEMS)
            sp.dma_start(we_sb.rearrange("p (e k n) -> p e k n", e=E1, k=KD),
                         we.rearrange("e (k p) n -> p e k n", p=P)).then_inc(we_in, 16)

            def store_out(g):
                sp.wait_ge(out_done, g.n + 1)
                sp.dma_start(tokens4(out, g.n), outc[:, g.slot]).then_inc(out_out[g.slot], 16)

            def stage_c(nxt, prev):
                def body(h, par):
                    if nxt:
                        load_c(At(h, par, 1))
                        load_adj_c(At(h, par, 1))
                    if prev:
                        store_out(At(h, par, -1))
                return body

            straight(1, 4, stage_c(True, True))
            looped(sp, 4, GROUPS - 2, stage_c(True, True))
            straight(GROUPS - 2, GROUPS - 1, stage_c(True, True))
            straight(GROUPS - 1, GROUPS + 1, stage_c(False, True))
            for s in range(2):
                sp.wait_ge(out_out[s], 16 * GROUPS // 2)
                sp.wait_ge(n1_out[s], 16 * GROUPS // 2)
                sp.wait_ge(ys_out[s], 16 * ITEMS // 2)

        @blk.gpsimd
        def _(pool):
            pool.memset(adj_sb, 0.0).then_inc(zeroed, 1)
            pool.memset(zero[:, :], 0.0).then_inc(zeroed, 1)
            pool.wait_ge(early_in, 16 * EARLY)

            def rsqrt(g, mv, mv_sem, ve, ve_sem, rstd, rstd_sem):
                pool.wait_ge(mv_sem, g.n + 1)
                pool.tensor_tensor(ve[:, :], mv[:, :, 1], const_of("eps"), ALU.add).then_inc(ve_sem, 1)
                pool.wait_ge(ve_sem, g.n + 1)
                pool.tensor_tensor(rstd[:, :], ve[:, :], const_of("minus_half"), ALU.pow).then_inc(rstd_sem, 1)

            def load_for_scatter(q):
                wait(pool, scattered[q.slot], 2 * GT * 16 * q.used)
                pool.wait_ge(n1_out[q.slot], 16 * (q.used + 1))
                pool.sem_inc(pool_held, 1)
                pool.dma_start(xg[:, q.slot], tokens4(n1_dram, q.n)).then_inc(xg_in[q.slot], 16)

            def copy_slots(q):
                pool.tensor_copy(slot_now[:, q.slot],
                                 slot_i[:, ds(q.n * GT, GT), :].rearrange("p j c -> p (j c)")
                                 ).then_inc(slots_copied, 1)

            def scatter(q, turn, part):
                if turn == 0:
                    copy_slots(q)
                    pool.wait_ge(slots_copied, q.n + 1)
                    pool.wait_ge(xg_in[q.slot], 16 * (q.used + 1))
                    pool.sem_inc(pool_held, 1)
                for j in SCATTER_TILES[turn]:
                    for c in range(2):
                        at = slot_now[:, q.slot, 2 * j + c:2 * j + c + 1].bitcast(U32)
                        pool.indirect_dma_start(xs_dram[part], IndirectOffsetOnAxis(ap=at, axis=0),
                                                xg[:, q.slot, j], None).then_inc(scattered[q.slot], 16)

            def pad(part):
                for e in range(E0):
                    at = pad_i[:, part, e:e + 1].bitcast(U32)
                    pool.indirect_dma_start(xs_dram[part], IndirectOffsetOnAxis(ap=at, axis=0),
                                            zero[:, :], None).then_inc(padded, 16)

            def stage_a(nxt, prev, scat):
                def body(h, par):
                    if scat:
                        q = At(h - SCATTER_FROM // 2, par)
                        load_for_scatter(At(h - SCATTER_FROM // 2, par, 1)) if scat == 1 else None
                        scatter(q, 0, 0)
                    if nxt:
                        rsqrt(At(h, par, 1), mv1, mv1_done, ve1, ve1_done, rstd1, rstd1_done)
                    if scat:
                        scatter(q, 1, 0)
                    if prev:
                        rsqrt(At(h, par, -1), mv2, mv2_done, ve2, ve2_done, rstd2, rstd2_done)
                    if scat:
                        scatter(q, 2, 0)
                return body

            straight(-1, 0, stage_a(True, False, 0))
            straight(0, 1, stage_a(True, False, 0))
            straight(1, 4, stage_a(True, True, 0))
            looped(pool, 4, SCATTER_FROM, stage_a(True, True, 0))
            pool.wait_ge(routed, 1)
            pool.wait_ge(rows_zeroed, 2 * 16)
            load_for_scatter(At(0, 0))
            pad(0)
            straight(SCATTER_FROM, GROUPS - 1, stage_a(True, True, 1))
            straight(GROUPS - 1, GROUPS + 1, stage_a(False, True, 1))
            straight(GROUPS + 1, GROUPS + 2, stage_a(False, False, 2))
            assert SCATTER_FROM + FG == GROUPS + 2
            pool.wait_ge(routed, 2)
            load_for_scatter(At(FG // 2, 0))
            pad(1)

            def second(more):
                def body(h, par):
                    if more:
                        load_for_scatter(At(h, par, 1))
                    for third in range(3):
                        scatter(At(h, par), third, 1)
                return body

            looped(pool, FG, GROUPS - 2, second(True))
            straight(GROUPS - 2, GROUPS - 1, second(True))
            straight(GROUPS - 1, GROUPS, second(False))

            def gather_y(g, part):
                wait(pool, x2_done, g.n - 1)
                pool.wait_ge(slots_copied, GROUPS + g.n)
                pool.sem_inc(pool_held, 1)
                copy_slots(g)
                pool.wait_ge(slots_copied, GROUPS + g.n + 1)
                pool.sem_inc(pool_held, 1)
                for j in range(GT):
                    for c in range(2):
                        at = slot_now[:, g.slot, 2 * j + c:2 * j + c + 1].bitcast(U32)
                        pool.indirect_dma_start(yg[:, g.slot, j, c], None, ys_dram[part],
                                                IndirectOffsetOnAxis(ap=at, axis=0)).then_inc(yg_in[g.slot], 16)

            def gather_be(g):
                pool.wait_ge(expert_ready, g.n + 1)
                wait(pool, out_done, g.n - 1)
                pool.sem_inc(pool_held, 1)
                for j in range(GT):
                    pool.indirect_dma_start(beg[:, g.slot, j], None, be,
                                            IndirectOffsetOnAxis(ap=expert[:, g.slot, j:j + 1].bitcast(U32),
                                                                 axis=0)).then_inc(beg_in[g.slot], 16)

            def norm2(g):
                rsqrt(g, mv1, mv3_done, ve1, ve3_done, rstd1, rstd3_done)

            def stage_c(nxt2, nxt, cur, prev, part=0):
                def body(h, par):
                    if nxt2:
                        gather_y(At(h, par, 2), part)
                    if nxt:
                        norm2(At(h, par, 1))
                    if prev:
                        gather_be(At(h, par, -1))
                    if cur:
                        rsqrt(At(h, par), mv2, mv4_done, ve2, ve4_done, rstd2, rstd4_done)
                return body

            for s in range(2):
                pool.wait_ge(ys_out[s], 16 * ((FI + 1 - s) // 2))
            for s in range(2):
                pool.wait_ge(scattered[s], 2 * GT * 16 * GROUPS // 2)
            for par in range(2):
                gather_y(At(0, par), 0)
            norm2(At(0, 0))
            pool.wait_ge(y_mm, ITEMS)
            pool.memset(n3z.rearrange("p j k g n -> p (j k g n)"), 0.0).then_inc(n3z_zeroed, 1)
            straight(0, 1, stage_c(True, True, True, False))
            straight(1, 4, stage_c(True, True, True, True))
            assert FG == 4 + 2
            for s in range(2):
                pool.wait_ge(ys_out[s], 16 * ITEMS // 2)
            looped(pool, 4, GROUPS - 2, stage_c(True, True, True, True, 1))
            straight(GROUPS - 2, GROUPS - 1, stage_c(False, True, True, True))
            straight(GROUPS - 1, GROUPS, stage_c(False, False, True, True))
            straight(GROUPS, GROUPS + 1, stage_c(False, False, False, True))

        @blk.scalar
        def _(act):
            act.wait_ge(early_in, 16 * EARLY)
            for b in range(2):
                act.wait_ge(mp_mm, b + 1)
                act.activation(mp[:, b], bank[b][:, 0:D], ACT.Copy).then_inc(mp_ready, 1)

            def mask_adj(g):
                act.wait_ge(adj_in[g.slot], 32 * (g.used + 1))
                act.sem_inc(act_held, 1)
                for j in range(GT):
                    a = adj_sb[:, g.slot, j]
                    act.activation(a, a, ACT.Copy, scale=mask[:, ds(g.n * GT + j, 1)]).then_inc(adj_masked, 1)

            def copy_tt(g, j):
                t = g.n * GT + j
                act.wait_ge(tt_mm, t + 1)
                wait(act, uv_mm, t + 1 - GT)
                act.activation(tt[:, j].rearrange("p a k n -> p (a k n)"), bank[0][:, :], ACT.Copy
                               ).then_inc(tt_ready, 1)

            def copy_v(g, j):
                act.wait_ge(uv_mm, g.n * GT + j + 1)
                if j == 0:
                    wait(act, x1_done, g.n - 1)
                act.activation(v_sb[:, g.slot, j], bank[4 + j % 2][:, 0:D], ACT.Copy).then_inc(v_ready, 1)

            def copy_x(g):
                act.wait_ge(xin_in[g.slot], 16 * (g.used + 1))
                wait(act, n1_done, g.n - 1)
                wait(act, x1_out[g.slot], 16 * g.used)
                act.sem_inc(act_held, 1)
                act.activation(x1[:, g.slot].rearrange("p j n -> p (j n)"),
                               xin[:, g.slot].rearrange("p j n -> p (j n)"), ACT.Copy).then_inc(x_copied, 1)

            def exp_w(g):
                act.wait_ge(w_sub_done, g.n + 1)
                act.activation(w_exp[:, :, :], w_sub[:, :, :], ACT.Exp).then_inc(w_exp_done, 1)

            def copy_n1T(g, pair):
                act.wait_ge(n1T_mm, 2 * g.n + pair + 1)
                wait(act, logit_mm, g.n)
                act.activation(n1T[:, 2 * pair:2 * pair + 2].rearrange("p j k n -> p (j k n)"),
                               bank[1][:, :], ACT.Copy).then_inc(n1T_ready, 1)

            def copy_logit(g):
                act.wait_ge(logit_mm, g.n + 1)
                act.sem_inc(act_held, 1)
                act.activation(logit[:, ds(g.n * GT, GT), :].rearrange("p j e -> p (j e)"),
                               bank[7][:, 0:GT * E0], ACT.Copy).then_inc(logit_ready, 1)

            def route_exps(part, k):
                act.wait_ge(route_exp, 6 * part + 2 * k + 1)
                act.activation(r_b[:, 0:PART_T[part], :], r_a[:, 0:PART_T[part], :], ACT.Exp
                               ).then_inc(route_exp, 1)

            def stage_a(nxt, cur, prev, last, route=None):
                def body(h, par):
                    g1, g, gp, gl = (At(h, par, d) for d in (1, 0, -1, -2))
                    if cur:
                        copy_tt(g, 1)
                        copy_v(g, 0)
                    if last:
                        copy_n1T(gl, 0)
                    if prev:
                        exp_w(gp)
                    if cur:
                        copy_tt(g, 2)
                        copy_v(g, 1)
                    if last:
                        copy_n1T(gl, 1)
                    if cur:
                        copy_tt(g, 3)
                        copy_x(g)
                    if nxt:
                        mask_adj(g1)
                    if cur:
                        copy_v(g, 2)
                    if route is not None:
                        route_exps(0, route)
                    if cur:
                        copy_v(g, 3)
                    if nxt:
                        copy_tt(g1, 0)
                    if last:
                        copy_logit(gl)
                return body

            mask_adj(At(0, 0))
            copy_tt(At(0, 0), 0)
            straight(0, 1, stage_a(True, True, False, False))
            straight(1, 2, stage_a(True, True, True, False))
            straight(2, 4, stage_a(True, True, True, True))
            looped(act, 4, ROUTE_STEPS[0], stage_a(True, True, True, True))
            for k in range(3):
                straight(ROUTE_STEPS[k], ROUTE_STEPS[k] + 1, stage_a(True, True, True, True, k))
            straight(ROUTE_STEPS[3], ROUTE_STEPS[3] + 1, stage_a(True, True, True, True))
            straight(ROUTE_STEPS[3] + 1, GROUPS - 1, stage_a(True, True, True, True))
            straight(GROUPS - 1, GROUPS, stage_a(False, True, True, True))
            straight(GROUPS, GROUPS + 1, stage_a(False, False, True, True))
            straight(GROUPS + 1, GROUPS + 2, stage_a(False, False, False, True))

            for s in range(2):
                act.wait_ge(x1_out[s], 16 * GROUPS // 2)
                act.wait_ge(n1_out[s], 16 * GROUPS // 2)

            def gelu(i):
                act.wait_ge(w1_mm, i.n + 1)
                wait(act, h_done, i.n - 1)
                act.activation(g_sb[:, i.slot], bank[2 + i.slot][:, :], ACT.Gelu).then_inc(gelu_done, 1)

            def copy_hsT(i):
                act.wait_ge(hsT_mm, i.n + 1)
                wait(act, y_mm, i.n - 1)
                act.activation(hsT[:, i.slot].rearrange("p k n -> p (k n)"), bank[0][:, :], ACT.Copy
                               ).then_inc(hsT_ready, 1)

            def stage_f(h, par):
                copy_hsT(At(h, par, -2))
                gelu(At(h, par, -1))

            straight(1, 2, lambda h, par: gelu(At(h, par, -1)))
            for k in range(2, 6):
                straight(k, k + 1, stage_f)
                if k in ROUTE_F_STEPS[0:3]:
                    route_exps(1, ROUTE_F_STEPS.index(k))
            looped(act, 6, ITEMS, stage_f)
            straight(ITEMS, ITEMS + 1, stage_f)
            straight(ITEMS + 1, ITEMS + 2, lambda h, par: copy_hsT(At(h, par, -2)))

            def copy_a(g, layer, pair):
                act.wait_ge(a_mm[layer], 2 * g.n + pair + 1)
                act.activation(hT[:, 2 * pair:2 * pair + 2].rearrange("p j k n -> p (j k n)"),
                               bank[pair][:, :], ACT.Copy).then_inc(a_ready[layer], 1)

            def relu(g, layer, pair):
                act.wait_ge(b_added[layer], 2 * g.n + pair + 1)
                act.activation(hrelu[:, 2 * pair:2 * pair + 2], hsum[:, 2 * pair:2 * pair + 2],
                               ACT.Relu).then_inc(relu_done[layer], 1)

            def copy_n3T(g, pair):
                act.wait_ge(n3T_mm, 2 * g.n + pair + 1)
                wait(act, out_mm, 2 * (g.n - 1) + pair + 1)
                wait(act, m_done, g.n)
                for b in range(2):
                    ins = act.activation(
                        n3z[:, 2 * pair:2 * pair + 2, :, b, b * NODES:(b + 1) * NODES],
                        bank[4 + pair].rearrange("p (j k n) -> p j k n", j=2, k=KD)
                        [:, :, :, b * NODES:(b + 1) * NODES], ACT.Copy)
                ins.then_inc(n3z_ready, 1)

            def exp_lg(g):
                act.wait_ge(gate_step, GATE_STEPS * g.n + EXP_AFTER)
                act.activation(lg_e[:, :], lg_k[:, :], ACT.Exp, accum_out=lg_s[:, 2:3]).then_inc(lg_exp, 1)

            def stage_c(cur, prev):
                def body(h, par):
                    g, gp = At(h, par), At(h, par, -1)
                    if cur:
                        copy_a(g, 0, 0)
                        copy_a(g, 0, 1)
                    if prev:
                        copy_n3T(gp, 0)
                        copy_n3T(gp, 1)
                    if cur:
                        relu(g, 0, 0)
                        relu(g, 0, 1)
                        copy_a(g, 1, 0)
                        copy_a(g, 1, 1)
                        relu(g, 1, 0)
                        relu(g, 1, 1)
                    if prev:
                        exp_lg(gp)
                    if cur:
                        copy_a(g, 2, 0)
                        copy_a(g, 2, 1)
                return body

            act.wait_ge(n3z_zeroed, 1)
            straight(0, 1, stage_c(True, False))
            straight(1, 4, stage_c(True, True))
            looped(act, 4, GROUPS, stage_c(True, True))
            straight(GROUPS, GROUPS + 1, stage_c(False, True))

        @blk.tensor
        def _(pe):
            pe.wait_ge(wqk_in, 16)
            pe.wait_ge(early_in, 16 * EARLY)
            for b in range(KD):
                for k in range(KD):
                    mm = pe.matmul(bank[b][:, 0:D], wqk_stage[:, 1, k, b * P:(b + 1) * P],
                                   wqk_stage[:, 0, k, :], start=(k == 0), stop=(k == KD - 1))
                mm.then_inc(mp_mm, 1)
            pe.wait_ge(mp_ready, 2)

            def adj_and_transposes(g, j):
                t = g.n * GT + j
                pe.wait_ge(adj_masked, t + 1)
                pe.wait_ge(xn_done, t + 1)
                wait(pe, tt_ready, t)
                for k in range(KD):
                    pe.matmul(bank[0][:, k * P:(k + 1) * P], xn[:, g.slot, j, k * P:(k + 1) * P],
                              adj_sb[:, g.slot, j], start=True, stop=True)
                for k in range(KD):
                    mm = pe.transpose(bank[0][:, D + k * P:D + (k + 1) * P],
                                      xn[:, g.slot, j, k * P:(k + 1) * P], ident)
                mm.then_inc(tt_mm, 1)

            def u_and_v(g, j):
                t = g.n * GT + j
                pe.wait_ge(tt_ready, t + 1)
                wait(pe, w_dot, t - 1)
                wait(pe, v_ready, t - 1)
                for k in range(KD):
                    pe.matmul(bank[2 + j % 2][:, 0:D], tt[:, j, 0, k], mp[:, k], start=(k == 0), stop=(k == KD - 1))
                for k in range(KD):
                    mm = pe.matmul(bank[4 + j % 2][:, 0:D], tt[:, j, 1, k], wv_sb[:, k],
                                   start=(k == 0), stop=(k == KD - 1))
                mm.then_inc(uv_mm, 1)

            def w_to_rows(g):
                pe.wait_ge(w_masked_done, g.n + 1)
                wait(pe, p_col_done, g.n)
                pe.matmul(bank[6][0:GT, 0:P], w_masked[:, :], ident, start=True, stop=True).then_inc(w_row, 1)

            def p_to_columns(g):
                pe.wait_ge(w_prob_done, g.n + 1)
                pe.matmul(bank[6][:, P:P + GT], w_prob[:, :, :].rearrange("j g n -> j (g n)"),
                          ident[0:GT, 0:GT], start=True, stop=True).then_inc(p_mm, 1)

            def n1_transposes(g, pair):
                pe.wait_ge(n1_done, g.n + 1)
                wait(pe, n1T_ready, 2 * g.n + pair)
                for j in range(2):
                    for k in range(KD):
                        mm = pe.transpose(bank[1][:, (j * KD + k) * P:(j * KD + k + 1) * P],
                                          n1[:, g.slot, 2 * pair + j, k * P:(k + 1) * P], ident)
                mm.then_inc(n1T_mm, 1)

            def logits(g):
                pe.wait_ge(n1T_ready, 2 * g.n + 2)
                wait(pe, logit_ready, g.n)
                for j in range(GT):
                    for k in range(KD):
                        mm = pe.matmul(bank[7][:, j * E0:(j + 1) * E0], n1T[:, j, k], wg0_sb[:, k],
                                       start=(k == 0), stop=(k == KD - 1))
                mm.then_inc(logit_mm, 1)

            def route_counts(part):
                pe.wait_ge(both_ready, part + 1)
                wait(pe, logit_ready, (ROUTE_STEPS[3] - 2, GROUPS)[part])
                n = PART_T[part] * E0
                a = both[:, 0:PART_T[part], :].rearrange("p t e -> p (t e)")
                pe.matmul(bank[7][:, 0:n], const_of("ones"), a, start=True, stop=True).then_inc(counts_mm, 1)

            def route_ranks(part):
                pe.wait_ge(counts_read, part + 1)
                n = PART_T[part] * E0
                a = both[:, 0:PART_T[part], :].rearrange("p t e -> p (t e)")
                pe.matmul(bank[7][:, 0:n], const_of("before"), a, start=True, stop=True).then_inc(ranks_mm, 1)

            def stage_a(nxt, cur, prev, last, route=False):
                def body(h, par):
                    g1, g, gp, gl = (At(h, par, d) for d in (1, 0, -1, -2))
                    if cur:
                        adj_and_transposes(g, 1)
                        u_and_v(g, 0)
                    if prev:
                        w_to_rows(gp)
                    if last:
                        n1_transposes(gl, 0)
                    if cur:
                        adj_and_transposes(g, 2)
                        u_and_v(g, 1)
                    if route:
                        route_counts(0)
                    if prev:
                        p_to_columns(gp)
                    if last:
                        n1_transposes(gl, 1)
                    if cur:
                        adj_and_transposes(g, 3)
                        u_and_v(g, 2)
                        u_and_v(g, 3)
                    if route:
                        route_ranks(0)
                    if nxt:
                        adj_and_transposes(g1, 0)
                    if route:
                        pe.wait_ge(rank_read, 1)
                    if last:
                        logits(gl)
                return body

            adj_and_transposes(At(0, 0), 0)
            straight(0, 1, stage_a(True, True, False, False))
            straight(1, 2, stage_a(True, True, True, False))
            pe.wait_ge(consts_in, 16 * CONSTS)
            straight(2, 4, stage_a(True, True, True, True))
            looped(pe, 4, ROUTE_STEPS[3] - 1, stage_a(True, True, True, True))
            straight(ROUTE_STEPS[3] - 1, ROUTE_STEPS[3], stage_a(True, True, True, True))
            straight(ROUTE_STEPS[3], ROUTE_STEPS[3] + 1, stage_a(True, True, True, True, True))
            straight(ROUTE_STEPS[3] + 1, GROUPS - 1, stage_a(True, True, True, True))
            straight(GROUPS - 1, GROUPS, stage_a(False, True, True, True))
            straight(GROUPS, GROUPS + 1, stage_a(False, False, True, True))
            straight(GROUPS + 1, GROUPS + 2, stage_a(False, False, False, True))
            pe.wait_ge(experts_in, 3 * E0 * 16)
            pe.wait_ge(routed, 1)

            def rows_transposes(i):
                pe.wait_ge(xs_in[i.slot], 16 * (i.used + 1))
                wait(pe, xsT_ready, i.n)
                for k in range(KD):
                    mm = pe.transpose(bank[1][:, k * P:(k + 1) * P], xs[:, i.slot, k * P:(k + 1) * P], ident)
                mm.then_inc(xsT_mm, 1)

            def up(i):
                e = pe.value_load(expert_of[0:1, ds(i.n, 1)], min_val=0, max_val=E0 - 1)
                pe.wait_ge(xsT_ready, i.n + 1)
                wait(pe, h_done, i.n - 1)
                for w, done in ((0, w1_mm), (1, w3_mm)):
                    for k in range(KD):
                        mm = pe.matmul(bank[2 + 2 * w + i.slot][:, :], xsT[:, i.slot, k],
                                       w13_sb[w][:, ds(e * (KD * F0) + k * F0, F0)],
                                       start=(k == 0), stop=(k == KD - 1))
                    mm.then_inc(done, 1)
                return e

            def h_transposes(i):
                pe.wait_ge(h_done, i.n + 1)
                wait(pe, hsT_ready, i.n)
                for k in range(KF):
                    mm = pe.transpose(bank[0][:, k * P:(k + 1) * P], h_sb[:, i.slot, k * P:(k + 1) * P], ident)
                mm.then_inc(hsT_mm, 1)

            def down(i):
                e = pe.value_load(expert_of[0:1, ds(i.n, 1)], min_val=0, max_val=E0 - 1)
                pe.wait_ge(hsT_ready, i.n + 1)
                wait(pe, y_ready, i.n)
                for k in range(KF):
                    mm = pe.matmul(bank[6][:, 0:D], hsT[:, i.slot, k],
                                   w2_sb[:, ds(e * (KF * D) + k * D, D)], start=(k == 0), stop=(k == KF - 1))
                mm.then_inc(y_mm, 1)

            def stage_f(first, second, third):
                def body(h, par):
                    if third:
                        h_transposes(At(h, par, -2))
                    if first:
                        rows_transposes(At(h, par))
                    if second:
                        up(At(h, par, -1))
                    if third:
                        down(At(h, par, -2))
                return body

            straight(0, 1, stage_f(True, False, False))
            straight(1, 2, stage_f(True, True, False))
            straight(2, 5, stage_f(True, True, True))
            straight(5, 6, stage_f(True, True, True))
            route_counts(1)
            straight(6, 7, stage_f(True, True, True))
            route_ranks(1)
            straight(7, 8, stage_f(True, True, True))
            looped(pe, 8, FI - 1 - 20, stage_f(True, True, True))
            pe.wait_ge(routed, 2)
            looped(pe, FI - 1 - 20, ITEMS, stage_f(True, True, True))
            straight(ITEMS, ITEMS + 1, stage_f(False, True, True))
            straight(ITEMS + 1, ITEMS + 2, stage_f(False, False, True))

            def times_adj(g, layer):
                for pair in range(2):
                    if layer == 0:
                        pe.wait_ge(n2_done, g.n + 1)
                        pe.wait_ge(adjc_in[g.slot], 32 * (g.used + 1))
                        src = n2[:, g.slot]
                        wait(pe, a_ready[2], 2 * (g.n - 1) + pair + 1)
                    else:
                        pe.wait_ge(relu_done[layer - 1], 2 * g.n + pair + 1)
                        src = hrelu
                        pe.wait_ge(a_ready[layer - 1], 2 * g.n + pair + 1)
                    for j in range(2):
                        for k in range(KD):
                            mm = pe.matmul(bank[pair][:, (j * KD + k) * P:(j * KD + k + 1) * P],
                                           src[:, 2 * pair + j, k * P:(k + 1) * P],
                                           adj_sb[:, g.slot, 2 * pair + j], start=True, stop=True)
                    mm.then_inc(a_mm[layer], 1)

            def times_w(g, layer):
                for pair in range(2):
                    pe.wait_ge(a_ready[layer], 2 * g.n + pair + 1)
                    if layer == 0:
                        wait(pe, b_added[2], 2 * (g.n - 1) + pair + 1)
                    else:
                        pe.wait_ge(b_added[layer - 1], 2 * g.n + pair + 1)
                    for j in range(2):
                        for k in range(KD):
                            mm = pe.matmul(bank[2 + pair][:, j * D:(j + 1) * D], hT[:, 2 * pair + j, k],
                                           gw_sb[:, layer, k], start=(k == 0), stop=(k == KD - 1))
                    mm.then_inc(b_mm[layer], 1)

            def n3_transposes(g):
                for pair in range(2):
                    pe.wait_ge(n3_done, g.n + 1)
                    wait(pe, n3z_ready, 2 * g.n - 2 + pair + 1)
                    for j in range(2):
                        for k in range(KD):
                            mm = pe.transpose(bank[4 + pair][:, (j * KD + k) * P:(j * KD + k + 1) * P],
                                              n3[:, 2 * pair + j, k * P:(k + 1) * P], ident)
                    mm.then_inc(n3T_mm, 1)

            def graph_logits(g):
                pe.wait_ge(m_done, g.n + 1)
                for k in range(KD):
                    mm = pe.matmul(bank[4][0:2 * GT, 0:E1], m_T[:, k].rearrange("p j g -> p (j g)"), wg1_sb[:, k],
                                   start=(k == 0), stop=(k == KD - 1))
                mm.then_inc(lg_mm, 1)

            def spread_gate(g):
                pe.wait_ge(spread_done, g.n + 1)
                pe.matmul(bank[4][:, E1:E1 + 2 * GT], const_of("half_of", 2 * GT),
                          spread[:, :, :].rearrange("g a j -> g (a j)"), start=True, stop=True
                          ).then_inc(spread_mm, 1)

            def graph_expert(g, pair):
                pe.wait_ge(expert_ready, g.n + 1)
                wait(pe, ysum_done, 2 * (g.n - 1) + pair + 1)
                pe.sem_inc(pe_held, 1)
                for j in range(2):
                    for b in range(2):
                        e = pe.value_load(expert[b * NODES:b * NODES + 1, g.slot, 2 * pair + j:2 * pair + j + 1],
                                          min_val=0, max_val=E1 - 1)
                        for k in range(KD):
                            mm = pe.matmul(bank[6 + pair][:, j * D:(j + 1) * D], n3z[:, 2 * pair + j, k, b],
                                           we_sb[:, ds(e * (KD * D) + k * D, D)],
                                           start=(b == 0 and k == 0), stop=(b == 1 and k == KD - 1))
                mm.then_inc(out_mm, 1)

            def stage_c(cur, prev):
                def body(h, par):
                    g, gp = At(h, par), At(h, par, -1)
                    if cur:
                        times_adj(g, 0)
                    if prev:
                        n3_transposes(gp)
                    if cur:
                        times_w(g, 0)
                        times_adj(g, 1)
                    if prev:
                        graph_logits(gp)
                    if cur:
                        times_w(g, 1)
                        times_adj(g, 2)
                    if prev:
                        spread_gate(gp)
                    if cur:
                        times_w(g, 2)
                    if prev:
                        graph_expert(gp, 0)
                        graph_expert(gp, 1)
                return body

            straight(0, 1, stage_c(True, False))
            pe.wait_ge(we_in, 16)
            pe.wait_ge(y_ready, ITEMS)
            straight(1, 4, stage_c(True, True))
            looped(pe, 4, GROUPS, stage_c(True, True))
            straight(GROUPS, GROUPS + 1, stage_c(False, True))

        @blk.vector
        def _(dve):
            dve.wait_ge(early_in, 16 * EARLY)

            def norm_stats(g, src, st, st_sem, mv, mv_sem, used_sem):
                wait(dve, mv_sem, g.n)
                for j in range(GT):
                    ins = dve.bn_stats(st[:, j], src[:, j])
                ins.then_inc(st_sem, 1)
                dve.wait_ge(st_sem, g.n + 1)
                wait(dve, used_sem, g.n)
                dve.sem_inc(dve_held, 1)
                for j in range(GT):
                    ins = dve.bn_aggr(mv[:, j], st[:, j])
                ins.then_inc(mv_sem, 1)

            def norm_rows(g, j, dst, src, mv, rstd):
                return dve.tensor_scalar(dst[:, j], src[:, j], mv[:, j, 0:1], rstd[:, j:j + 1],
                                         ALU.subtract, ALU.mult)

            def stats_x(g):
                dve.wait_ge(xin_in[g.slot], 16 * (g.used + 1))
                norm_stats(g, xin[:, g.slot], st1, st1_done, mv1, mv1_done, xn_group)

            xn_group = sem("xn_group")

            def norm_x(g):
                dve.wait_ge(rstd1_done, g.n + 1)
                wait(dve, tt_mm, GT * (g.n - 1))
                wait(dve, w_dot, GT * (g.n - 1))
                for j in range(GT):
                    norm_rows(g, j, xn[:, g.slot], xin[:, g.slot], mv1, rstd1).then_inc(xn_done, 1)
                dve.wait_ge(xn_done, GT * (g.n + 1))
                dve.sem_inc(xn_group, 1)

            def dot_w(g, j):
                dve.wait_ge(uv_mm, g.n * GT + j + 1)
                u = bank[2 + j % 2][:, 0:D]
                dve.tensor_tensor_reduce(u, u, xn[:, g.slot, j], ATT_SCALE, 0.0, ALU.mult, ALU.add,
                                         w_col[:, g.slot, j:j + 1]).then_inc(w_dot, 1)

            def mask_w(g):
                dve.wait_ge(w_dot, GT * (g.n + 1))
                dve.tensor_tensor(w_masked[:, :], w_col[:, g.slot], mask[:, ds(g.n * GT, GT)], ALU.mult
                                  ).then_inc(w_masked_done, 1)

            def sub_max(g):
                rows = bank[6][0:GT, 0:P].rearrange("j (g n) -> j g n", g=2)
                dve.wait_ge(w_row, g.n + 1)
                dve.tensor_reduce(w_max[:, :], rows, AX.X, ALU.max).then_inc(w_max_done, 1)
                dve.wait_ge(w_max_done, g.n + 1)
                dve.tensor_tensor(w_sub[:, :, :], rows, w_max[:, :].unsqueeze(2).to_broadcast([GT, 2, NODES]),
                                  ALU.subtract).then_inc(w_sub_done, 1)

            def prob(g):
                dve.wait_ge(w_exp_done, g.n + 1)
                dve.tensor_reduce(w_sum[:, :], w_exp[:, :, :], AX.X, ALU.add).then_inc(w_sum_done, 1)
                dve.wait_ge(w_sum_done, g.n + 1)
                dve.reciprocal(w_rcp[:, :], w_sum[:, :]).then_inc(w_rcp_done, 1)
                dve.wait_ge(w_rcp_done, g.n + 1)
                dve.tensor_tensor(w_prob[:, :, :], w_exp[:, :, :],
                                  w_rcp[:, :].unsqueeze(2).to_broadcast([GT, 2, NODES]), ALU.mult
                                  ).then_inc(w_prob_done, 1)

            def add_x1(g):
                dve.wait_ge(p_mm, g.n + 1)
                wait(dve, x1_done, g.n)
                dve.tensor_copy(p_col[:, :], bank[6][:, P:P + GT]).then_inc(p_col_done, 1)
                dve.wait_ge(p_col_done, g.n + 1)
                dve.wait_ge(v_ready, GT * (g.n + 1))
                dve.wait_ge(x_copied, g.n + 1)
                for j in range(GT):
                    ins = dve.scalar_tensor_tensor(out=x1[:, g.slot, j], in0=v_sb[:, g.slot, j],
                                                   scalar=p_col[:, j:j + 1], in1=x1[:, g.slot, j],
                                                   op0=ALU.mult, op1=ALU.add)
                ins.then_inc(x1_done, 1)

            def stats_x1(g):
                dve.wait_ge(x1_done, g.n + 1)
                norm_stats(g, x1[:, g.slot], st2, st2_done, mv2, mv2_done, n1_done)

            def norm_x1(g):
                dve.wait_ge(rstd2_done, g.n + 1)
                wait(dve, n1_out[g.slot], 16 * g.used)
                wait(dve, n1T_mm, 2 * (g.n - 1))
                for j in range(GT):
                    ins = norm_rows(g, j, n1[:, g.slot], x1[:, g.slot], mv2, rstd2)
                ins.then_inc(n1_done, 1)

            steps = [0]

            def step(ins):
                steps[0] += 1
                ins.then_inc(route_step, 1)
                dve.wait_ge(route_step, steps[0])

            def exp_on_act(part, k):
                dve.sem_inc(route_exp, 1)
                dve.wait_ge(route_exp, 6 * part + 2 * k + 2)

            class Route:

                def __init__(self, part):
                    self.part, self.T, self.t0 = part, PART_T[part], PART_T0[part]
                    self.a, self.b, self.c, self.p, self.both = (
                        v[:, 0:self.T, :] for v in (r_a, r_b, r_c, r_p, both))
                    self.pick = [pick[:, c, 0:self.T, :] for c in range(2)]
                    self.k = r_k[:, 0:self.T]

                def over_e(self, v):
                    return v.unsqueeze(2).to_broadcast([P, self.T, E0])

                def over_t(self, v):
                    return v.unsqueeze(1).to_broadcast([P, self.T, E0])

                def scores(self):
                    dve.wait_ge(logit_ready, (self.t0 + self.T) // GT)
                    dve.wait_ge(consts_in, 16 * CONSTS)
                    step(dve.tensor_tensor(self.c, logit[:, self.t0:self.t0 + self.T, :],
                                           self.over_t(bg0_sb[:, :]), ALU.add))
                    step(dve.tensor_reduce(self.k, self.c, AX.X, ALU.max))
                    step(dve.tensor_tensor(self.a, self.c, self.over_e(self.k), ALU.subtract))
                    exp_on_act(self.part, 0)
                    step(dve.tensor_reduce(self.k, self.b, AX.X, ALU.add))
                    step(dve.reciprocal(self.k, self.k))
                    step(dve.tensor_tensor(self.p, self.b, self.over_e(self.k), ALU.mult))

                def choice(self, c):
                    if c == 0:
                        s = self.p
                    else:
                        step(dve.scalar_tensor_tensor(out=self.c, in0=self.pick[0], scalar=-4.0,
                                                      in1=self.p, op0=ALU.mult, op1=ALU.add))
                        s = self.c
                    mx = top[:, c, 0:self.T]
                    step(dve.tensor_reduce(mx, s, AX.X, ALU.max))
                    step(dve.tensor_tensor(self.a, s, self.over_e(mx), ALU.is_ge))
                    step(dve.tensor_tensor(self.a, self.a, self.over_t(const_of("rev0")), ALU.mult))
                    step(dve.tensor_reduce(self.k, self.a, AX.X, ALU.max))
                    step(dve.tensor_tensor(self.pick[c], self.a, self.over_e(self.k), ALU.is_ge))
                    step(dve.tensor_tensor(self.a, self.p, self.over_e(mx), ALU.subtract))
                    exp_on_act(self.part, 1 + c)
                    step(dve.tensor_tensor(self.both, self.p, self.over_e(mx), ALU.max))
                    step(dve.scalar_tensor_tensor(out=self.c, in0=self.both, scalar=JITTER2,
                                                  in1=self.a, op0=ALU.mult, op1=ALU.add))
                    step(dve.scalar_tensor_tensor(out=self.b, in0=self.c, scalar=0.0,
                                                  in1=self.b, op0=ALU.is_ge, op1=ALU.mult))
                    if c == 1:
                        step(dve.tensor_scalar(self.c, self.pick[0], -1.0, 1.0, ALU.mult, ALU.add))
                        step(dve.tensor_tensor(self.b, self.b, self.c, ALU.mult))
                    step(dve.tensor_reduce(self.k, self.b, AX.X, ALU.add))
                    step(dve.reciprocal(weight[:, self.t0:self.t0 + self.T, c], self.k))
                    if c == 1:
                        dve.tensor_tensor(self.both, self.pick[0], self.pick[1], ALU.add).then_inc(both_ready, 1)

                def by_e(self, v):
                    return self.flat(v).rearrange("p (e t) -> p e t", e=E0)

                def flat(self, v):
                    return v.rearrange("p t e -> p (t e)")

                def counts(self):
                    n = self.T * E0
                    dve.wait_ge(counts_mm, self.part + 1)
                    step(dve.tensor_copy(self.by_e(self.a), bank[7][:, 0:n].rearrange("p (t e) -> p e t", e=E0)))
                    dve.sem_inc(counts_read, 1)
                    step(dve.tensor_tensor_scan(self.flat(self.b), const_of(f"restart{self.part}"),
                                                self.flat(self.a), 0.0, ALU.mult, ALU.add))
                    count = self.by_e(self.b)[:, :, self.T - 1]
                    step(dve.tensor_scalar(n_f[:, :], count, float(P - 1), None, ALU.add))
                    step(dve.tensor_copy(n_i[:, :], n_f[:, :]))
                    step(dve.tensor_scalar(n_i[:, :], n_i[:, :], 7, 7, ALU.logical_shift_right,
                                           ALU.logical_shift_left))
                    step(dve.tensor_copy(n_f[:, :], n_i[:, :]))
                    step(dve.tensor_tensor_scan(n_end[:, :], const_of("ones")[:, 0:E0], n_f[:, :], 0.0,
                                                ALU.mult, ALU.add))
                    step(dve.tensor_tensor(n_base[:, :], n_end[:, :], n_f[:, :], ALU.subtract))
                    spare = const_of(f"spare{self.part}")
                    step(dve.scalar_tensor_tensor(out=pad_f[:, :], in0=count, scalar=const_of("row"),
                                                  in1=n_base[:, :], op0=ALU.add, op1=ALU.add))
                    step(dve.tensor_tensor(pad_ok[:, :], n_end[:, :], pad_f[:, :], ALU.is_gt))
                    step(dve.tensor_tensor(pad_f[:, :], pad_f[:, :], spare, ALU.subtract))
                    step(dve.tensor_tensor(pad_f[:, :], pad_f[:, :], pad_ok[:, :], ALU.mult))
                    step(dve.tensor_tensor(pad_i[:, self.part], pad_f[:, :], spare, ALU.add))
                    step(dve.tensor_tensor(self.flat(self.b), self.flat(self.b), self.flat(self.a), ALU.subtract))

                def places(self):
                    n, items = self.T * E0, PART_ITEMS[self.part]
                    row = self.by_e(self.b)
                    dve.wait_ge(ranks_mm, self.part + 1)
                    step(dve.tensor_tensor(row, row, bank[7][:, 0:n].rearrange("p (t e) -> p e t", e=E0), ALU.add))
                    dve.sem_inc(rank_read, 1)
                    step(dve.tensor_tensor(row, row, n_base[:, :].unsqueeze(2).to_broadcast([P, E0, self.T]),
                                           ALU.add))
                    for c in range(2):
                        step(dve.tensor_tensor(self.c, self.pick[c], row.rearrange("p e t -> p t e"), ALU.mult))
                        step(dve.tensor_reduce(slot_f[:, 0:self.T], self.c, AX.X, ALU.add))
                        step(dve.tensor_copy(slot_i[:, self.t0:self.t0 + self.T, c], slot_f[:, 0:self.T]))
                    step(dve.tensor_tensor(tile_e[:, 0:items, :],
                                           const_of("tile_start", 1)[:, 0:items].unsqueeze(2)
                                           .to_broadcast([1, items, E0]),
                                           n_end[0:1, :].unsqueeze(1).to_broadcast([1, items, E0]), ALU.is_ge))
                    step(dve.tensor_reduce(tile_ef[:, 0:items], tile_e[:, 0:items, :], AX.X, ALU.add))
                    dve.tensor_scalar(expert_of[:, self.part * FI:self.part * FI + items], tile_ef[:, 0:items],
                                      float(E0 - 1), None, ALU.min).then_inc(routed, 1)

                def piece(self, k):
                    (self.scores, lambda: self.choice(0), lambda: self.choice(1), self.counts, self.places)[k]()

            route0, route1 = Route(0), Route(1)

            def stage_a(nxt, cur, prev, route=None):
                def body(h, par):
                    g1, g, gp = (At(h, par, d) for d in (1, 0, -1))
                    if prev:
                        mask_w(gp)
                    if nxt:
                        stats_x(g1)
                    if prev:
                        sub_max(gp)
                    if cur:
                        dot_w(g, 0)
                    if prev:
                        prob(gp)
                    if cur:
                        dot_w(g, 1)
                    if nxt:
                        norm_x(g1)
                    if prev:
                        add_x1(gp)
                    if cur:
                        dot_w(g, 2)
                    if route is not None:
                        route0.piece(route)
                    if prev:
                        stats_x1(gp)
                    if cur:
                        dot_w(g, 3)
                    if route == 3:
                        route0.piece(4)
                    if prev:
                        norm_x1(gp)
                return body

            stats_x(At(0, 0))
            norm_x(At(0, 0))
            straight(0, 1, stage_a(True, True, False))
            straight(1, 4, stage_a(True, True, True))
            looped(dve, 4, ROUTE_STEPS[0], stage_a(True, True, True))
            for k in range(4):
                straight(ROUTE_STEPS[k], ROUTE_STEPS[k] + 1, stage_a(True, True, True, k))
            straight(ROUTE_STEPS[3] + 1, GROUPS - 1, stage_a(True, True, True))
            straight(GROUPS - 1, GROUPS, stage_a(False, True, True))
            straight(GROUPS, GROUPS + 1, stage_a(False, False, True))

            for s in range(2):
                dve.wait_ge(x1_out[s], 16 * GROUPS // 2)
                dve.wait_ge(n1_out[s], 16 * GROUPS // 2)
            dve.wait_ge(routed, 1)

            def add_x2(g):
                dve.wait_ge(x1c_in[g.slot], 16 * (g.used + 1))
                dve.wait_ge(yg_in[g.slot], 2 * GT * 16 * (g.used + 1))
                wait(dve, x3_done, g.n - 1)
                for c in range(2):
                    for j in range(GT):
                        ins = dve.scalar_tensor_tensor(
                            out=x2[:, g.slot, j], in0=yg[:, g.slot, j, c],
                            scalar=weight[:, ds(g.n * GT + j, 1), c],
                            in1=(x1c if c == 0 else x2)[:, g.slot, j], op0=ALU.mult, op1=ALU.add)
                    if c == 0:
                        ins.then_inc(half_sum, 1)
                        dve.wait_ge(half_sum, g.n + 1)
                ins.then_inc(x2_done, 1)

            def stats_x2(g):
                dve.wait_ge(x2_done, g.n + 1)
                norm_stats(g, x2[:, g.slot], st1, st3_done, mv1, mv3_done, n2_done)

            def norm_x2(g):
                dve.wait_ge(rstd3_done, g.n + 1)
                wait(dve, a_mm[0], 2 * (g.n - 1))
                for j in range(GT):
                    ins = norm_rows(g, j, n2[:, g.slot], x2[:, g.slot], mv1, rstd1)
                ins.then_inc(n2_done, 1)

            def copy_xsT(i):
                dve.wait_ge(xsT_mm, i.n + 1)
                wait(dve, w3_mm, i.n - 1)
                dve.tensor_copy(xsT[:, i.slot].rearrange("p k n -> p (k n)"), bank[1][:, 0:D]
                                ).then_inc(xsT_ready, 1)

            def mul_h(i):
                dve.wait_ge(gelu_done, i.n + 1)
                dve.wait_ge(w3_mm, i.n + 1)
                wait(dve, hsT_mm, i.n - 1)
                dve.tensor_tensor(h_sb[:, i.slot], bank[4 + i.slot][:, :], g_sb[:, i.slot], ALU.mult
                                  ).then_inc(h_done, 1)

            def copy_y(i):
                dve.wait_ge(y_mm, i.n + 1)
                wait(dve, ys_out[i.slot], 16 * i.used)
                dve.tensor_copy(y_sb[:, i.slot], bank[6][:, 0:D]).then_inc(y_ready, 1)

            def stage_f(first, second, third):
                def body(h, par):
                    if first:
                        copy_xsT(At(h, par))
                    if second:
                        mul_h(At(h, par, -1))
                    if third:
                        copy_y(At(h, par, -2))
                return body

            straight(0, 1, stage_f(True, False, False))
            straight(1, 2, stage_f(True, True, False))
            for k in range(2, 8):
                straight(k, k + 1, stage_f(True, True, True))
                if k in ROUTE_F_STEPS:
                    route1.piece(ROUTE_F_STEPS.index(k))
                elif k == ROUTE_F_STEPS[-1] + 1:
                    route1.piece(4)
            looped(dve, 8, X2_AT, stage_f(True, True, True))
            add_x2(At(0, 0))
            stats_x2(At(0, 0))
            norm_x2(At(0, 0))
            looped(dve, X2_AT, ITEMS, stage_f(True, True, True))
            straight(ITEMS, ITEMS + 1, stage_f(False, True, True))
            straight(ITEMS + 1, ITEMS + 2, stage_f(False, False, True))

            def add_bias(g, layer):
                for pair in range(2):
                    part = hsum[:, 2 * pair:2 * pair + 2]
                    dve.wait_ge(b_mm[layer], 2 * g.n + pair + 1)
                    if layer:
                        dve.wait_ge(relu_done[layer - 1], 2 * g.n + pair + 1)
                    else:
                        wait(dve, x3_done, g.n)
                    dve.tensor_tensor(part, bank[2 + pair].rearrange("p (j n) -> p j n", j=2),
                                      gb_sb[:, layer].unsqueeze(1).to_broadcast([P, 2, D]), ALU.add
                                      ).then_inc(b_added[layer], 1)

            def add_x3(g):
                dve.wait_ge(b_added[2], 2 * g.n + 2)
                wait(dve, out_done, g.n - 1)
                dve.tensor_tensor(x3[:, g.slot].rearrange("p j n -> p (j n)"),
                                  hsum.rearrange("p j n -> p (j n)"),
                                  x2[:, g.slot].rearrange("p j n -> p (j n)"), ALU.add).then_inc(x3_done, 1)

            def norm_x3(g):
                dve.wait_ge(x3_done, g.n + 1)
                norm_stats(g, x3[:, g.slot], st2, st4_done, mv2, mv4_done, n3_done)

            def apply_x3(g):
                dve.wait_ge(rstd4_done, g.n + 1)
                wait(dve, n3T_mm, 2 * g.n)
                for j in range(GT):
                    ins = norm_rows(g, j, n3, x3[:, g.slot], mv2, rstd2)
                ins.then_inc(n3_done, 1)

            def graph_sum(g):
                dve.wait_ge(n3z_ready, 2 * g.n + 2)
                wait(dve, lg_mm, g.n)
                for b in range(2):
                    ins = dve.tensor_reduce(
                        m_T[:, :, :, b].rearrange("p k j -> p j k"),
                        n3z[:, :, :, b, b * NODES:(b + 1) * NODES], AX.X, ALU.add)
                ins.then_inc(m_done, 1)

            def graph_gate(g):
                at = [0]

                def link(ins):
                    at[0] += 1
                    ins.then_inc(gate_step, 1)
                    dve.wait_ge(gate_step, GATE_STEPS * g.n + at[0])

                dve.wait_ge(lg_mm, g.n + 1)
                link(dve.scalar_tensor_tensor(out=lg[:, :], in0=bank[4][0:2 * GT, 0:E1], scalar=1.0 / NODES,
                                              in1=bg1_sb[:, :], op0=ALU.mult, op1=ALU.add))
                link(dve.tensor_reduce(lg_s[:, 0:1], lg[:, :], AX.X, ALU.max))
                link(dve.tensor_scalar(lg_k[:, :], lg[:, :], lg_s[:, 0:1], None, ALU.subtract))
                link(dve.tensor_scalar(lg[:, :], lg[:, :], lg_s[:, 0:1], None, ALU.is_ge))
                link(dve.tensor_tensor(lg[:, :], lg[:, :], const_of("rev1", 2 * GT), ALU.mult))
                link(dve.tensor_reduce(lg_s[:, 1:2], lg[:, :], AX.X, ALU.max))
                link(dve.tensor_scalar(lg_s[:, 1:2], lg_s[:, 1:2], -1.0, float(E1), ALU.mult, ALU.add))
                dve.wait_ge(lg_exp, g.n + 1)
                link(dve.reciprocal(lg_s[:, 3:4], lg_s[:, 2:3]))
                link(dve.tensor_scalar(spread[:, 0], const_of("own_tile", 2 * GT), lg_s[:, 3:4], None, ALU.mult))
                link(dve.tensor_scalar(spread[:, 1], const_of("own_tile", 2 * GT), lg_s[:, 1:2], None, ALU.mult))
                assert at[0] == GATE_STEPS
                dve.sem_inc(spread_done, 1)

            def take_gate(g):
                dve.wait_ge(spread_mm, g.n + 1)
                wait(dve, out_done, g.n - 1)
                wait(dve, beg_in[g.slot], GT * 16 * g.used)
                dve.tensor_copy(gate[:, g.slot], bank[4][:, E1:E1 + GT])
                dve.tensor_copy(expert[:, g.slot], bank[4][:, E1 + GT:E1 + 2 * GT]).then_inc(expert_ready, 1)

            def finish(g):
                dve.wait_ge(beg_in[g.slot], GT * 16 * (g.used + 1))
                wait(dve, ygate_done, g.n)
                for pair in range(2):
                    dve.wait_ge(out_mm, 2 * g.n + pair + 1)
                    dve.tensor_tensor(ysum[:, 2 * pair:2 * pair + 2].rearrange("p j n -> p (j n)"),
                                      bank[6 + pair][:, :],
                                      beg[:, g.slot, 2 * pair:2 * pair + 2].rearrange("p j n -> p (j n)"),
                                      ALU.add).then_inc(ysum_done, 1)
                dve.wait_ge(ysum_done, 2 * g.n + 2)
                wait(dve, out_out[g.slot], 16 * g.used)
                for j in range(GT):
                    ins = dve.scalar_tensor_tensor(out=outc[:, g.slot, j], in0=ysum[:, j],
                                                   scalar=gate[:, g.slot, j:j + 1], in1=x3[:, g.slot, j],
                                                   op0=ALU.mult, op1=ALU.add)
                ins.then_inc(out_done, 1)
                dve.wait_ge(out_done, g.n + 1)
                dve.sem_inc(ygate_done, 1)

            def stage_c(nxt, cur, prev):
                def body(h, par):
                    g1, g, gp = (At(h, par, d) for d in (1, 0, -1))
                    if cur:
                        add_bias(g, 0)
                    if prev:
                        graph_sum(gp)
                    if nxt:
                        add_x2(g1)
                    if cur:
                        add_bias(g, 1)
                    if prev:
                        graph_gate(gp)
                    if nxt:
                        stats_x2(g1)
                    if prev:
                        take_gate(gp)
                    if cur:
                        add_bias(g, 2)
                        add_x3(g)
                        norm_x3(g)
                    if nxt:
                        norm_x2(g1)
                    if cur:
                        apply_x3(g)
                    if prev:
                        finish(gp)
                return body

            dve.wait_ge(y_mm, ITEMS)
            for s in range(2):
                dve.wait_ge(ys_out[s], 16 * ITEMS // 2)
            straight(0, 1, stage_c(True, True, False))
            straight(1, 4, stage_c(True, True, True))
            looped(dve, 4, GROUPS - 2, stage_c(True, True, True))
            straight(GROUPS - 2, GROUPS - 1, stage_c(True, True, True))
            straight(GROUPS - 1, GROUPS, stage_c(False, True, True))
            straight(GROUPS, GROUPS + 1, stage_c(False, False, True))


def shape_constants():
    import numpy as np

    c = np.zeros((P, CONST_COLS), np.float32)
    i = np.arange(P)

    def put(name, value):
        n, at = CONST[name]
        c[:, at:at + n] = value

    put("ident", i[:, None] == i[None, :])
    put("before", i[:, None] < i[None, :])
    put("ones", 1.0)
    put("half_of", (i[:, None] % 2) == (i[None, :] // NODES))
    put("own_tile", (i[:, None] // 2) == np.arange(GT)[None, :])
    put("rev0", E0 - np.arange(E0))
    put("rev1", E1 - np.arange(E1))
    for part in range(2):
        put(f"restart{part}", np.arange(E0 * PART_T[part]) % PART_T[part] != 0)
        put(f"spare{part}", P * (PART_ITEMS[part] + np.arange(SPARE))[None, :] + i[:, None])
    put("tile_start", P * np.arange(max(PART_ITEMS)))
    put("row", i[:, None])
    put("eps", EPS)
    put("minus_half", -0.5)
    return c


def kernel(x, adj, nodemask, L0_gnn_Wqk, L0_gnn_Wv, L0_ffn_wg, L0_ffn_bg, L0_ffn_w1, L0_ffn_w3, L0_ffn_w2,
           L1_gnn_W1, L1_gnn_b1, L1_gnn_W2, L1_gnn_b2, L1_gnn_W3, L1_gnn_b3, L1_ffn_Wg, L1_ffn_bg, L1_ffn_We,
           L1_ffn_be):
    import numpy as np
    import concourse.bacc as bacc
    from concourse.bass_utils import run_bass_kernel_spmd

    nc = bacc.Bacc("TRN2", target_bir_lowering=False, num_devices=1)
    arrays = {}

    def give(name, a):
        a = np.ascontiguousarray(a)
        arrays[name] = a
        return nc.dram_tensor(name, a.shape, mybir.dt.from_np(a.dtype), kind="ExternalInput").ap()

    def row(a):
        return np.asarray(a)

    args = dict(
        x=give("in_x", np.asarray(x).reshape(TOKENS, D)),
        adjT=give("in_adjT", np.asarray(adj).transpose(0, 2, 1)),
        maskT=give("in_maskT", np.asarray(nodemask).reshape(TILES, P).T),
        wqkT=give("in_wqkT", np.asarray(L0_gnn_Wqk).T),
        wv=give("in_wv", L0_gnn_Wv),
        wg0=give("in_wg0", L0_ffn_wg), bg0=give("in_bg0", row(L0_ffn_bg)),
        w1=give("in_w1", L0_ffn_w1), w3=give("in_w3", L0_ffn_w3), w2=give("in_w2", L0_ffn_w2),
        gw=[give(f"in_gw{i}", w) for i, w in enumerate((L1_gnn_W1, L1_gnn_W2, L1_gnn_W3))],
        gb=[give(f"in_gb{i}", row(b)) for i, b in enumerate((L1_gnn_b1, L1_gnn_b2, L1_gnn_b3))],
        wg1=give("in_wg1", L1_ffn_Wg), bg1=give("in_bg1", row(L1_ffn_bg)),
        we=give("in_we", L1_ffn_We), be=give("in_be", L1_ffn_be),
        const=give("in_const", shape_constants()),
    )
    out = nc.dram_tensor("out", (TOKENS, D), F32, kind="ExternalOutput").ap()
    program(nc, out=out, **args)
    r = run_bass_kernel_spmd(nc, [arrays], core_ids=[0])
    return r.results[0]["out"].reshape(GRAPHS, NODES, D)
```

```python
from contextlib import ExitStack

import concourse.bass as bass
from concourse import mybir
from concourse.bass import IndirectOffsetOnAxis, ds

F32 = mybir.dt.float32
F32R = mybir.dt.float32r
I32 = mybir.dt.int32
U32 = mybir.dt.uint32
ALU = mybir.AluOpType
ACT = mybir.ActivationFunctionType
AX = mybir.AxisListType

P = 128
GRAPHS, NODES, D = 128, 64, 256
TOKENS = GRAPHS * NODES
TILES = TOKENS // P
GT = 4
GROUPS = TILES // GT
KD = D // P
E0, F0 = 8, 512
KF = F0 // P
E1 = 16
FG = 6
PART_T0 = (0, FG * GT)
PART_T = (FG * GT, TILES - FG * GT)
HT = max(PART_T)
MOST_PAD = E0 * (P - 1) // P
PART_ITEMS = tuple(2 * t + MOST_PAD for t in PART_T)
FI = PART_ITEMS[0]
ITEMS = sum(PART_ITEMS)
WEIGHTS = 2 * KD * F0 + KF * D
LOADS = 2 * E0
SPARE = E0
EPS = 1e-5
JITTER2 = 2.0 * 0.01
ATT_SCALE = 1.0 / float(D) ** 0.5

CONST = {}
_at = 0
for _name, _n in (("ident", P), ("before", P), ("ones", P), ("half_of", P), ("own_tile", GT),
                  ("rev0", E0), ("rev1", E1), ("restart0", E0 * PART_T[0]),
                  ("restart1", E0 * PART_T[1]), ("tile_start", max(PART_ITEMS)), ("row", 1),
                  ("spare0", SPARE), ("spare1", SPARE), ("last0", E0), ("last1", E0), ("eps", GT), ("minus_half", GT),
                  ("minus_one", GT)):
    CONST[_name] = (_n, _at)
    _at += _n
CONST_COLS = _at


def wait(eng, sem, value):
    if isinstance(value, int) and value <= 0:
        return
    eng.wait_ge(sem, value)


class At:

    def __init__(self, h, parity, shift=0):
        self.n = 2 * h + parity + shift
        self.slot = (parity + shift) % 2
        self.used = h + (parity + shift) // 2


def straight(first, last, body):
    for k in range(first, last):
        body(k // 2, k % 2)


def looped(eng, first, last, body):
    with eng.Fori(first // 2, last // 2, 1) as h:
        body(h, 0)
        body(h, 1)


def program(nc, x, adjT, maskT, wqkT, wv, wg0, bg0, w1, w3, w2, gw, gb, wg1, bg1, we, be, const, out):
    ctx = ExitStack()
    with ctx:
        def sb(name, shape, dt=F32):
            return ctx.enter_context(nc.sbuf_tensor(name, shape, dt))

        def sem(name):
            return ctx.enter_context(nc.semaphore(name))

        def dram(name, rows):
            return nc.dram_tensor(name, [rows, D], F32, kind="Internal").ap()

        x1_dram = dram("x1_dram", TOKENS)
        n1_dram = dram("n1_dram", TOKENS)
        xs_dram = [dram(f"xs_dram{part}", (PART_ITEMS[part] + SPARE) * P) for part in range(2)]
        ys_dram = [dram(f"ys_dram{part}", PART_ITEMS[part] * P) for part in range(2)]

        work = sb("work", [P, 25600])
        w_hi = sb("w_hi", [P, 2 * WEIGHTS], F32R)
        w_lo = sb("w_lo", [P, 2 * WEIGHTS], F32R)
        xsT_hi = sb("xsT_hi", [P, 2, KD * P], F32R)
        xsT_lo = sb("xsT_lo", [P, 2, KD * P], F32R)
        hsT_hi = sb("hsT_hi", [P, 2, F0], F32R)
        hsT_lo = sb("hsT_lo", [P, 2, F0], F32R)
        cst = sb("cst", [P, CONST_COLS])
        mask = sb("mask", [P, TILES])
        mp = sb("mp", [P, KD, D])
        wv_sb = sb("wv_sb", [P, KD, D])
        wg0_sb = sb("wg0_sb", [P, KD, E0])
        bg0_sb = sb("bg0_sb", [P, E0])
        gw_sb = sb("gw_sb", [P, 3, KD, D])
        gb_sb = sb("gb_sb", [P, 3, D])
        wg1_sb = sb("wg1_sb", [P, KD, E1])
        bg1_sb = sb("bg1_sb", [2 * GT, E1])
        zero = sb("zero", [P, D])

        def const_of(name, rows=P):
            n, at = CONST[name]
            return cst[0:rows, at:at + n]

        ident = const_of("ident")

        class Carve:

            def __init__(self, at):
                self.at = at

            def __call__(self, n, pattern=None, **sizes):
                part = work[:, self.at:self.at + n]
                self.at += n
                return part.rearrange(pattern, **sizes) if pattern else part

        c = Carve(0)
        adj_sb = c(2 * GT * P, "p (s j n) -> p s j n", s=2, j=GT)
        xin = c(2 * GT * D, "p (s j n) -> p s j n", s=2, j=GT)
        xn = c(2 * GT * D, "p (s j n) -> p s j n", s=2, j=GT)
        tt = c(GT * 2 * D, "p (j a k n) -> p j a k n", j=GT, a=2, k=KD)
        v_sb = c(2 * GT * D, "p (s j n) -> p s j n", s=2, j=GT)
        x1 = c(2 * GT * D, "p (s j n) -> p s j n", s=2, j=GT)
        n1 = c(2 * GT * D, "p (s j n) -> p s j n", s=2, j=GT)
        n1T = c(GT * D, "p (j k n) -> p j k n", j=GT, k=KD)
        stage_a_end = c.at
        wqk_stage = tt.rearrange("p j a k n -> p (j a k n)")[:, 0:4 * D]\
            .rearrange("p (h k n) -> p h k n", h=2, k=KD)
        c = Carve(2 * GT * P)
        yg = c(2 * GT * 2 * D, "p (s j c n) -> p s j c n", s=2, j=GT, c=2)
        x2 = c(2 * GT * D, "p (s j n) -> p s j n", s=2, j=GT)
        n2 = c(2 * GT * D, "p (s j n) -> p s j n", s=2, j=GT)
        under_f_end = c.at
        hT = c(GT * D, "p (j k n) -> p j k n", j=GT, k=KD)
        hsum = c(GT * D, "p (j n) -> p j n", j=GT)
        x3 = c(2 * GT * D, "p (s j n) -> p s j n", s=2, j=GT)
        n3z = c(GT * KD * 2 * P, "p (j k g n) -> p j k g n", j=GT, k=KD, g=2)
        we_at = c.at
        we_sb = c(E1 * KD * D)
        we_end = c.at
        beg = c(GT * D, "p (j n) -> p j n", j=GT)
        outc = c(GT * D, "p (j n) -> p j n", j=GT)
        assert c.at <= 25600 and stage_a_end <= we_at - KD * F0
        c = Carve(under_f_end)
        g_sb = c(2 * F0, "p (s n) -> p s n", s=2)
        h_sb = c(2 * F0, "p (s n) -> p s n", s=2)
        xs = c(2 * D, "p (s n) -> p s n", s=2)
        y_sb = c(2 * D, "p (s n) -> p s n", s=2)
        w_raw = [Carve(at)(KD * F0) for at in (we_at - KD * F0, we_end, we_end + KD * F0)]

        shift1 = sb("shift1", [P, GT])
        shift2 = sb("shift2", [P, GT])
        st1 = sb("st1", [P, GT, 6])
        mv1 = sb("mv1", [P, GT, 2])
        ve1 = sb("ve1", [P, GT])
        rstd1 = sb("rstd1", [P, GT])
        st2 = sb("st2", [P, GT, 6])
        mv2 = sb("mv2", [P, GT, 2])
        ve2 = sb("ve2", [P, GT])
        rstd2 = sb("rstd2", [P, GT])
        w_col = sb("w_col", [P, 2, GT])
        w_masked = sb("w_masked", [P, GT])
        w_max = sb("w_max", [GT, 2])
        w_sub = sb("w_sub", [GT, 2, NODES])
        w_exp = sb("w_exp", [GT, 2, NODES])
        w_sum = sb("w_sum", [GT, 2])
        w_rcp = sb("w_rcp", [GT, 2])
        w_prob = sb("w_prob", [GT, 2, NODES])
        p_col = sb("p_col", [P, GT])
        logit = sb("logit", [P, TILES, E0])
        r_a = sb("r_a", [P, HT, E0])
        r_b = sb("r_b", [P, HT, E0])
        r_c = sb("r_c", [P, HT, E0])
        r_p = sb("r_p", [P, HT, E0])
        pick = sb("pick", [P, 2, HT, E0])
        both = sb("both", [P, HT, E0])
        top = sb("top", [P, 2, HT])
        r_k = sb("r_k", [P, HT])
        weight = sb("weight", [P, TILES, 2])
        slot_f = sb("slot_f", [P, HT])
        slot_i = sb("slot_i", [P, TILES, 2], I32)
        n_f = sb("n_f", [P, E0])
        n_i = sb("n_i", [P, E0], I32)
        n_end = sb("n_end", [P, E0])
        n_base = sb("n_base", [P, E0])
        tile_e = sb("tile_e", [1, max(PART_ITEMS), E0])
        tile_ef = sb("tile_ef", [1, max(PART_ITEMS)])
        pad_f = sb("pad_f", [P, E0])
        pad_ok = sb("pad_ok", [P, E0])
        pad_i = sb("pad_i", [P, 2, E0], I32)
        load_of = sb("load_of", [1, ITEMS], I32)
        used_at = sb("used_at", [1, LOADS], I32)
        n_used = sb("n_used", [1, E0])
        xg = sb("xg", [P, 2, GT, D])
        hrelu, n3 = xg[:, 0], xg[:, 1]
        slot_now = sb("slot_now", [P, 2, GT * 2], I32)
        m_T = sb("m_T", [P, KD, GT, 2])
        lg = sb("lg", [2 * GT, E1])
        lg_e = sb("lg_e", [2 * GT, E1])
        lg_k = sb("lg_k", [2 * GT, E1])
        lg_s = sb("lg_s", [2 * GT, 4])
        spread = sb("spread", [2 * GT, 2, GT])
        gate = sb("gate", [P, 2, GT])
        expert = sb("expert", [P, 2, GT], I32)

        bank = [ctx.enter_context(nc.psum_tensor(f"bank{i}", [P, 512], F32)) for i in range(8)]

        consts_in = sem("consts_in")
        early_in = sem("early_in")
        padded = [sem(f"padded{part}") for part in range(2)]
        x_copied = sem("x_copied")
        rank_read = sem("rank_read")
        wqk_in = sem("wqk_in")
        zeroed = sem("zeroed")
        mp_mm = sem("mp_mm")
        mp_ready = sem("mp_ready")
        raw_in = [sem(f"raw_in{w}") for w in range(3)]
        hi_in = [sem(f"hi_in{w}") for w in range(3)]
        lo_done = sem("lo_done")
        w_ready = sem("w_ready")
        rows_zeroed = sem("rows_zeroed")
        xin_in = [sem(f"xin_in{s}") for s in range(2)]
        adj_in = [sem(f"adj_in{s}") for s in range(2)]
        x1_out = [sem(f"x1_out{s}") for s in range(2)]
        n1_out = [sem(f"n1_out{s}") for s in range(2)]
        st1_done = sem("st1_done")
        pow1_done, pow2_done, pow3_done, pow4_done = (sem(f"pow{i}_done") for i in range(1, 5))
        mv1_done = sem("mv1_done")
        ve1_done = sem("ve1_done")
        rstd1_done = sem("rstd1_done")
        xn_done = sem("xn_done")
        st2_done = sem("st2_done")
        mv2_done = sem("mv2_done")
        ve2_done = sem("ve2_done")
        rstd2_done = sem("rstd2_done")
        n1_done = sem("n1_done")
        adj_masked = sem("adj_masked")
        tt_mm = sem("tt_mm")
        tt_ready = sem("tt_ready")
        uv_mm = sem("uv_mm")
        v_ready = sem("v_ready")
        w_dot = sem("w_dot")
        w_masked_done = sem("w_masked_done")
        w_row = sem("w_row")
        w_max_done = sem("w_max_done")
        w_sub_done = sem("w_sub_done")
        w_exp_done = sem("w_exp_done")
        w_sum_done = sem("w_sum_done")
        w_rcp_done = sem("w_rcp_done")
        w_prob_done = sem("w_prob_done")
        p_mm = sem("p_mm")
        p_col_done = sem("p_col_done")
        x1_done = sem("x1_done")
        n1T_mm = sem("n1T_mm")
        n1T_ready = sem("n1T_ready")
        logit_mm = sem("logit_mm")
        logit_ready = sem("logit_ready")
        route_step = sem("route_step")
        route_exp = sem("route_exp")
        both_ready = sem("both_ready")
        counts_mm = sem("counts_mm")
        counts_read = sem("counts_read")
        ranks_mm = sem("ranks_mm")
        routed = sem("routed")
        xg_in = [sem(f"xg_in{s}") for s in range(2)]
        slots_copied = sem("slots_copied")
        scattered = [sem(f"scattered{s}") for s in range(2)]
        xs_in = [sem(f"xs_in{s}") for s in range(2)]
        xsT_mm = sem("xsT_mm")
        xsT_hi_ready = sem("xsT_hi_ready")
        xsT_ready = sem("xsT_ready")
        w1_mm = sem("w1_mm")
        w3_mm = sem("w3_mm")
        gelu_done = sem("gelu_done")
        h_done = sem("h_done")
        hsT_mm = sem("hsT_mm")
        hsT_hi_ready = sem("hsT_hi_ready")
        hsT_ready = sem("hsT_ready")
        y_mm = sem("y_mm")
        y_ready = sem("y_ready")
        ys_out = [sem(f"ys_out{s}") for s in range(2)]
        we_in = sem("we_in")
        n3z_zeroed = sem("n3z_zeroed")
        x2_in = [sem(f"x2_in{s}") for s in range(2)]
        adjc_in = [sem(f"adjc_in{s}") for s in range(2)]
        yg_in = [sem(f"yg_in{s}") for s in range(2)]
        beg_in = [sem(f"beg_in{s}") for s in range(2)]
        out_out = sem("out_out")
        half_sum = sem("half_sum")
        x2_done = sem("x2_done")
        st3_done = sem("st3_done")
        mv3_done = sem("mv3_done")
        ve3_done = sem("ve3_done")
        rstd3_done = sem("rstd3_done")
        n2_done = sem("n2_done")
        a_mm = [sem(f"a_mm{i}") for i in range(3)]
        a_ready = [sem(f"a_ready{i}") for i in range(3)]
        b_mm = [sem(f"b_mm{i}") for i in range(3)]
        b_added = [sem(f"b_added{i}") for i in range(3)]
        relu_done = [sem(f"relu_done{i}") for i in range(2)]
        x3_done = sem("x3_done")
        st4_done = sem("st4_done")
        mv4_done = sem("mv4_done")
        ve4_done = sem("ve4_done")
        rstd4_done = sem("rstd4_done")
        n3_done = sem("n3_done")
        n3T_mm = sem("n3T_mm")
        n3z_ready = sem("n3z_ready")
        m_done = sem("m_done")
        lg_mm = sem("lg_mm")
        gate_step = sem("gate_step")
        lg_exp = sem("lg_exp")
        spread_done = sem("spread_done")
        spread_mm = sem("spread_mm")
        expert_ready = sem("expert_ready")
        out_mm = sem("out_mm")
        ysum_done = sem("ysum_done")
        out_done = sem("out_done")
        sp_held = sem("sp_held")
        pe_held = sem("pe_held")
        act_held = sem("act_held")
        dve_held = sem("dve_held")
        pool_held = sem("pool_held")

        EARLY, CONSTS = 3, 10
        SCATTER_FROM = 12
        SCATTER_TILES = ((0,), (1, 2), (3,))
        ROWS_BEFORE_LOAD = (3, 2, 1, 2, 1)
        EARLY_T = PART_T[1] - 2 * GT
        ROUTE_TURNS = ((0, 0, PART_T[0]), (PART_T0[1], 0, EARLY_T), (PART_T0[1] + EARLY_T, EARLY_T, 2 * GT))
        ROUTE_STEPS = (8, 9, 10, 11)
        X2_AT = FI + 41
        GATE_STEPS, EXP_AFTER = 10, 3
        blk = ctx.enter_context(nc.Block())

        def tokens4(t, g):
            return t[ds(g * (GT * P), GT * P), :].rearrange("(j p) n -> p j n", p=P)

        @blk.sync
        def _(sp):
            def load(dst, src, done):
                sp.dma_start(dst, src).then_inc(done, 16)

            def by_k(w):
                return w.rearrange("(k p) n -> p k n", p=P)

            load(wqk_stage, wqkT.rearrange("(h k p) n -> p h k n", h=2, p=P), wqk_in)
            load(xin[:, 0], tokens4(x, 0), xin_in[0])
            load(cst[:, :], const, early_in)
            load(mask[:, :], maskT, early_in)
            load(wv_sb[:, :, :], by_k(wv), early_in)
            sp.wait_ge(zeroed, 2)

            def load_adj(g, sems, free_sem, free_at):
                wait(sp, free_sem, free_at)
                for b in range(2):
                    rows = slice(b * NODES, (b + 1) * NODES)
                    sp.dma_start(adj_sb[rows, g.slot, :, rows],
                                 adjT[ds(g.n * (GT * 2), GT * 2), :, :]
                                 .rearrange("(j b) p n -> b p j n", b=2)[b]).then_inc(sems[g.slot], 16)

            def load_x(g):
                wait(sp, x_copied, g.n - 1)
                sp.sem_inc(sp_held, 1)
                wait(sp, xn_done, GT * (g.n - 1))
                sp.dma_start(xin[:, g.slot], tokens4(x, g.n)).then_inc(xin_in[g.slot], 16)

            def store_x1(g):
                sp.wait_ge(x1_done, g.n + 1)
                sp.dma_start(tokens4(x1_dram, g.n), x1[:, g.slot]).then_inc(x1_out[g.slot], 16)

            def store_n1(g):
                sp.wait_ge(n1_done, g.n + 1)
                sp.dma_start(tokens4(n1_dram, g.n), n1[:, g.slot]).then_inc(n1_out[g.slot], 16)

            def stage_a(nxt2, nxt, prev, last):
                def body(h, par):
                    if nxt:
                        g1 = At(h, par, 1)
                        load_adj(g1, adj_in, tt_mm, GT * (g1.n - 1))
                    if last:
                        store_n1(At(h, par, -2))
                    if nxt2:
                        load_x(At(h, par, 2))
                    if prev:
                        store_x1(At(h, par, -1))
                return body

            load_adj(At(0, 0), adj_in, tt_mm, 0)
            load_x(At(0, 1))
            for dst, src in (
                (wg0_sb[:, :, :], by_k(wg0)), (bg0_sb[:, :], bg0.partition_broadcast(P)),
                (gw_sb[:, 0], by_k(gw[0])), (gw_sb[:, 1], by_k(gw[1])), (gw_sb[:, 2], by_k(gw[2])),
                (gb_sb[:, 0], gb[0].partition_broadcast(P)), (gb_sb[:, 1], gb[1].partition_broadcast(P)),
                (gb_sb[:, 2], gb[2].partition_broadcast(P)),
                (wg1_sb[:, :, :], by_k(wg1)), (bg1_sb[:, :], bg1.partition_broadcast(2 * GT)),
            ):
                load(dst, src, consts_in)
            for part, end in enumerate(PART_ITEMS):
                sp.dma_start(xs_dram[part][(end - MOST_PAD) * P:end * P, :].rearrange("(i p) n -> p i n", p=P),
                             zero[:, :].unsqueeze(1).to_broadcast([P, MOST_PAD, D])).then_inc(rows_zeroed, 16)
            straight(0, 1, stage_a(True, True, False, False))
            straight(1, 2, stage_a(True, True, True, False))
            looped(sp, 2, GROUPS - 2, stage_a(True, True, True, True))
            straight(GROUPS - 2, GROUPS - 1, stage_a(False, True, True, True))
            straight(GROUPS - 1, GROUPS + 1, stage_a(False, False, True, True))
            straight(GROUPS + 1, GROUPS + 2, stage_a(False, False, False, True))

            def load_rows(i, part):
                wait(sp, xsT_mm, i.n - 1)
                sp.dma_start(xs[:, i.slot], xs_dram[part][ds((i.n - part * FI) * P, P), :]
                             ).then_inc(xs_in[i.slot], 16)

            def store_rows(i, part):
                sp.wait_ge(y_ready, i.n + 1)
                sp.dma_start(ys_dram[part][ds((i.n - part * FI) * P, P), :], y_sb[:, i.slot]
                             ).then_inc(ys_out[i.slot], 16)

            def stage_f(load_part, store_part):
                def body(h, par):
                    load_rows(At(h, par), load_part)
                    store_rows(At(h, par, -4), store_part)
                return body

            def part_scattered(groups, part):
                for s in range(2):
                    sp.wait_ge(scattered[s], (groups // 2) * GT * 2 * 16)
                sp.wait_ge(padded[part], E0 * 16)

            for s in range(2):
                sp.wait_ge(x1_out[s], 16 * GROUPS // 2)
                sp.wait_ge(n1_out[s], 16 * GROUPS // 2)
            sp.wait_ge(n1T_mm, 2 * GROUPS)

            def load_c(g):
                wait(sp, x3_done, g.n - 1)
                sp.dma_start(x2[:, g.slot], tokens4(x1_dram, g.n)).then_inc(x2_in[g.slot], 16)

            def load_adj_c(g):
                load_adj(g, adjc_in, a_mm[2], 2 * (g.n - 1))

            part_scattered(FG, 0)
            straight(0, 4, lambda h, par: load_rows(At(h, par), 0))
            straight(4, 6, stage_f(0, 0))
            looped(sp, 6, FI - 1, stage_f(0, 0))
            straight(FI - 1, FI, stage_f(0, 0))
            part_scattered(GROUPS, 1)
            straight(FI, FI + 4, stage_f(1, 0))
            straight(FI + 4, FI + 5, stage_f(1, 1))
            for par in range(2):
                load_c(At(0, par))
                load_adj_c(At(0, par))

            def load_we(h, par):
                e = 2 * h + par - (FI + 5)
                sp.dma_start(we_sb[:, ds(e * (KD * D), KD * D)].rearrange("p (k n) -> p k n", k=KD),
                             we[ds(e, 1), :, :].rearrange("e (k p) n -> p (e k) n", p=P)).then_inc(we_in, 16)

            def stage_f_we(h, par):
                stage_f(1, 1)(h, par)
                load_we(h, par)

            looped(sp, FI + 5, FI + 5 + E1, stage_f_we)
            looped(sp, FI + 5 + E1, ITEMS, stage_f(1, 1))

            straight(ITEMS, ITEMS + 4, lambda h, par: store_rows(At(h, par, -4), 1))
            def store_out(g):
                sp.wait_ge(out_done, g.n + 1)
                sp.dma_start(tokens4(out, g.n), outc).then_inc(out_out, 16)

            def stage_c(nxt2, nxt, prev):
                def body(h, par):
                    if nxt:
                        load_adj_c(At(h, par, 1))
                    if nxt2:
                        load_c(At(h, par, 2))
                    if prev:
                        store_out(At(h, par, -1))
                return body

            straight(0, 1, stage_c(True, False, False))
            straight(1, 4, stage_c(True, True, True))
            looped(sp, 4, GROUPS - 2, stage_c(True, True, True))
            straight(GROUPS - 2, GROUPS - 1, stage_c(False, True, True))
            straight(GROUPS - 1, GROUPS + 1, stage_c(False, False, True))
            sp.wait_ge(out_out, 16 * GROUPS)
            for s in range(2):
                sp.wait_ge(n1_out[s], 16 * GROUPS // 2)
                sp.wait_ge(ys_out[s], 16 * ITEMS // 2)

        @blk.gpsimd
        def _(pool):
            pool.memset(adj_sb, 0.0).then_inc(zeroed, 1)
            pool.memset(zero[:, :], 0.0).then_inc(zeroed, 1)
            pool.wait_ge(early_in, 16 * EARLY)

            def rsqrt(g, mv, mv_sem, ve, ve_sem, rstd, pow_sem, shift, rstd_sem):
                pool.wait_ge(mv_sem, g.n + 1)
                pool.tensor_tensor(ve[:, :], mv[:, :, 1], const_of("eps"), ALU.add).then_inc(ve_sem, 1)
                pool.wait_ge(ve_sem, 2 * g.n + 1)
                pool.tensor_tensor(rstd[:, :], ve[:, :], const_of("minus_half"), ALU.pow).then_inc(pow_sem, 1)
                pool.wait_ge(pow_sem, g.n + 1)
                pool.tensor_tensor(shift[:, :], mv[:, :, 0], rstd[:, :], ALU.mult).then_inc(ve_sem, 1)
                pool.wait_ge(ve_sem, 2 * (g.n + 1))
                pool.tensor_tensor(shift[:, :], shift[:, :], const_of("minus_one"), ALU.mult
                                   ).then_inc(rstd_sem, 1)

            def load_for_scatter(q):
                wait(pool, scattered[q.slot], 2 * GT * 16 * q.used)
                pool.wait_ge(n1_out[q.slot], 16 * (q.used + 1))
                pool.sem_inc(pool_held, 1)
                pool.dma_start(xg[:, q.slot], tokens4(n1_dram, q.n)).then_inc(xg_in[q.slot], 16)

            def copy_slots(q):
                pool.tensor_copy(slot_now[:, q.slot],
                                 slot_i[:, ds(q.n * GT, GT), :].rearrange("p j c -> p (j c)")
                                 ).then_inc(slots_copied, 1)

            def scatter(q, turn, part):
                if turn == 0:
                    copy_slots(q)
                    pool.wait_ge(slots_copied, q.n + 1)
                    pool.wait_ge(xg_in[q.slot], 16 * (q.used + 1))
                    pool.sem_inc(pool_held, 1)
                for j in SCATTER_TILES[turn]:
                    for c in range(2):
                        at = slot_now[:, q.slot, 2 * j + c:2 * j + c + 1].bitcast(U32)
                        pool.indirect_dma_start(xs_dram[part], IndirectOffsetOnAxis(ap=at, axis=0),
                                                xg[:, q.slot, j], None).then_inc(scattered[q.slot], 16)

            def matrix(w, e):
                src = (w1, w3, w2)[w]
                return src[ds(e, 1), :, :].rearrange("e (k p) n -> p (e k) n", p=P)

            def as_rows(part, w):
                return part.rearrange("p (k n) -> p k n", n=(F0, F0, D)[w])

            def load_raw(e):
                for w in range(3):
                    pool.dma_start(as_rows(w_raw[w], w), matrix(w, e)).then_inc(raw_in[w], 16)

            def in_ring(t, w, slot):
                at = slot * WEIGHTS + w * KD * F0
                return t[:, at:at + KD * F0]

            def load_hi(e, slot):
                for w in range(3):
                    pool.dma_start(as_rows(in_ring(w_hi, w, slot), w), matrix(w, e)).then_inc(hi_in[w], 16)

            def split(q, slot, w):
                pool.wait_ge(raw_in[w], 16 * (q + 1))
                pool.wait_ge(hi_in[w], 16 * (q + 1))
                pool.sem_inc(pool_held, 1)
                pool.tensor_tensor(in_ring(w_lo, w, slot), w_raw[w], in_ring(w_hi, w, slot).bitcast(F32),
                                   ALU.subtract).then_inc(lo_done, 1)
                if w == 2:
                    pool.wait_ge(lo_done, 3 * (q + 1))
                    pool.sem_inc(w_ready, 1)

            def prepare(q, e, slot, more=True):
                used = pool.value_load(used_at[0:1, ds(q - 2, 1)], min_val=1, max_val=ITEMS + 1)
                pool.wait_ge(y_mm, used)
                pool.sem_inc(pool_held, 1)
                load_hi(e, slot)
                for w in range(3):
                    split(q, slot, w)
                if more:
                    load_raw(e + 1 if isinstance(e, int) and e < E0 - 1 else 0 if isinstance(e, int) else e + 1)

            def pad(part):
                for e in range(E0):
                    at = pad_i[:, part, e:e + 1].bitcast(U32)
                    pool.indirect_dma_start(xs_dram[part], IndirectOffsetOnAxis(ap=at, axis=0),
                                            zero[:, :], None).then_inc(padded[part], 16)

            def stage_a(nxt, prev, scat):
                def body(h, par):
                    if scat:
                        q = At(h - SCATTER_FROM // 2, par)
                        load_for_scatter(At(h - SCATTER_FROM // 2, par, 1)) if scat == 1 else None
                        scatter(q, 0, 0)
                    if nxt:
                        rsqrt(At(h, par, 1), mv1, mv1_done, ve1, ve1_done, rstd1, pow1_done, shift1, rstd1_done)
                    if scat:
                        scatter(q, 1, 0)
                    if prev:
                        rsqrt(At(h, par, -1), mv2, mv2_done, ve2, ve2_done, rstd2, pow2_done, shift2, rstd2_done)
                    if scat:
                        scatter(q, 2, 0)
                return body

            straight(-1, 0, stage_a(True, False, 0))
            straight(0, 1, stage_a(True, False, 0))
            for e in range(2):
                load_raw(e)
                load_hi(e, e)
                for w in range(3):
                    straight(1 + 3 * e + w, 2 + 3 * e + w, stage_a(True, True, 0))
                    split(e, e, w)
            load_raw(2)
            straight(7, 8, stage_a(True, True, 0))
            looped(pool, 8, SCATTER_FROM, stage_a(True, True, 0))
            pool.wait_ge(routed, 1)
            pool.wait_ge(rows_zeroed, 2 * 16)
            load_for_scatter(At(0, 0))
            straight(SCATTER_FROM, GROUPS - 1, stage_a(True, True, 1))
            straight(GROUPS - 1, GROUPS + 1, stage_a(False, True, 1))
            straight(GROUPS + 1, SCATTER_FROM + FG - 1, stage_a(False, False, 1))
            straight(SCATTER_FROM + FG - 1, SCATTER_FROM + FG, stage_a(False, False, 2))
            pad(0)
            pool.wait_ge(routed, 2)
            load_for_scatter(At(FG // 2, 0))

            def second(more):
                def body(h, par):
                    if more:
                        load_for_scatter(At(h, par, 1))
                    for turn in range(3):
                        scatter(At(h, par), turn, 1)
                return body

            g = FG
            for q, groups in zip(range(2, E0), ROWS_BEFORE_LOAD):
                straight(g, g + groups, second(True))
                g += groups
                prepare(q, q, q % 2)
            straight(g, GROUPS - 1, second(True))
            straight(GROUPS - 1, GROUPS, second(False))
            pad(1)
            prepare(E0 - 1, E0 - 1, 1)
            for q in (E0, E0 + 1):
                prepare(q, q - E0, q % 2)

            def gather_y(g, part):
                wait(pool, x2_done, g.n - 1)
                pool.wait_ge(slots_copied, GROUPS + g.n)
                pool.sem_inc(pool_held, 1)
                copy_slots(g)
                pool.wait_ge(slots_copied, GROUPS + g.n + 1)
                pool.sem_inc(pool_held, 1)
                for j in range(GT):
                    for c in range(2):
                        at = slot_now[:, g.slot, 2 * j + c:2 * j + c + 1].bitcast(U32)
                        pool.indirect_dma_start(yg[:, g.slot, j, c], None, ys_dram[part],
                                                IndirectOffsetOnAxis(ap=at, axis=0)).then_inc(yg_in[g.slot], 16)

            def gather_be(g):
                pool.wait_ge(expert_ready, g.n + 1)
                wait(pool, out_done, g.n)
                pool.sem_inc(pool_held, 1)
                for j in range(GT):
                    pool.indirect_dma_start(beg[:, j], None, be,
                                            IndirectOffsetOnAxis(ap=expert[:, g.slot, j:j + 1].bitcast(U32),
                                                                 axis=0)).then_inc(beg_in[g.slot], 16)

            def norm2(g):
                rsqrt(g, mv1, mv3_done, ve1, ve3_done, rstd1, pow3_done, shift1, rstd3_done)

            def stage_c(nxt2, nxt, cur, prev, part=0):
                def body(h, par):
                    if nxt2:
                        gather_y(At(h, par, 2), part)
                    if prev:
                        gather_be(At(h, par, -1))
                    if nxt:
                        norm2(At(h, par, 1))
                    if cur:
                        rsqrt(At(h, par), mv2, mv4_done, ve2, ve4_done, rstd2, pow4_done, shift2, rstd4_done)
                return body

            for s in range(2):
                pool.wait_ge(ys_out[s], 16 * ((FI + 1 - s) // 2))
            for s in range(2):
                pool.wait_ge(scattered[s], 2 * GT * 16 * GROUPS // 2)
            for par in range(2):
                gather_y(At(0, par), 0)
            with pool.Fori(E0 // 2 + 1, E0 - 1, 1) as h:
                prepare(2 * h, 2 * h - E0, 0)
                prepare(2 * h + 1, 2 * h + 1 - E0, 1)
            prepare(LOADS - 2, E0 - 2, 0)
            prepare(LOADS - 1, E0 - 1, 1, more=False)
            pool.wait_ge(w_ready, LOADS)
            pool.memset(n3z.rearrange("p j k g n -> p (j k g n)"), 0.0).then_inc(n3z_zeroed, 1)

            norm2(At(0, 0))
            straight(0, 1, stage_c(True, True, True, False))
            straight(1, 4, stage_c(True, True, True, True))
            straight(4, FG - 2, stage_c(True, True, True, True))
            for s in range(2):
                pool.wait_ge(ys_out[s], 16 * ITEMS // 2)
            looped(pool, FG - 2, GROUPS - 2, stage_c(True, True, True, True, 1))
            straight(GROUPS - 2, GROUPS - 1, stage_c(False, True, True, True))
            straight(GROUPS - 1, GROUPS, stage_c(False, False, True, True))
            straight(GROUPS, GROUPS + 1, stage_c(False, False, False, True))

        @blk.scalar
        def _(act):
            act.wait_ge(early_in, 16 * EARLY)
            for b in range(2):
                act.wait_ge(mp_mm, b + 1)
                act.activation(mp[:, b], bank[b][:, 0:D], ACT.Copy).then_inc(mp_ready, 1)

            def mask_adj(g):
                act.wait_ge(adj_in[g.slot], 32 * (g.used + 1))
                act.sem_inc(act_held, 1)
                for j in range(GT):
                    a = adj_sb[:, g.slot, j]
                    act.activation(a, a, ACT.Copy, scale=mask[:, ds(g.n * GT + j, 1)]).then_inc(adj_masked, 1)

            def copy_tt(g, j):
                t = g.n * GT + j
                act.wait_ge(tt_mm, t + 1)
                wait(act, uv_mm, t + 1 - GT)
                act.activation(tt[:, j].rearrange("p a k n -> p (a k n)"), bank[0][:, :], ACT.Copy
                               ).then_inc(tt_ready, 1)

            def copy_v(g, j):
                act.wait_ge(uv_mm, g.n * GT + j + 1)
                if j == 0:
                    wait(act, x1_done, g.n - 1)
                act.activation(v_sb[:, g.slot, j], bank[4 + j % 2][:, 0:D], ACT.Copy).then_inc(v_ready, 1)

            def copy_x(g):
                act.wait_ge(xin_in[g.slot], 16 * (g.used + 1))
                wait(act, n1_done, g.n - 1)
                wait(act, x1_out[g.slot], 16 * g.used)
                act.sem_inc(act_held, 1)
                act.activation(x1[:, g.slot].rearrange("p j n -> p (j n)"),
                               xin[:, g.slot].rearrange("p j n -> p (j n)"), ACT.Copy).then_inc(x_copied, 1)

            def norm_rows(dst, src, rstd, shift):
                return [act.activation(dst[:, j], src[:, j], ACT.Identity, scale=rstd[:, j:j + 1],
                                       bias=shift[:, j:j + 1]) for j in range(GT)]

            def norm_x(g):
                act.wait_ge(rstd1_done, g.n + 1)
                wait(act, tt_mm, GT * (g.n - 1))
                wait(act, w_dot, GT * (g.n - 1))
                for ins in norm_rows(xn[:, g.slot], xin[:, g.slot], rstd1, shift1):
                    ins.then_inc(xn_done, 1)

            def norm_x1(g):
                act.wait_ge(rstd2_done, g.n + 1)
                wait(act, n1_out[g.slot], 16 * g.used)
                wait(act, n1T_mm, 2 * (g.n - 1))
                norm_rows(n1[:, g.slot], x1[:, g.slot], rstd2, shift2)[-1].then_inc(n1_done, 1)

            def exp_w(g):
                act.wait_ge(w_sub_done, g.n + 1)
                act.activation(w_exp[:, :, :], w_sub[:, :, :], ACT.Exp).then_inc(w_exp_done, 1)

            def copy_n1T(g, pair):
                act.wait_ge(n1T_mm, 2 * g.n + pair + 1)
                wait(act, logit_mm, g.n)
                act.activation(n1T[:, 2 * pair:2 * pair + 2].rearrange("p j k n -> p (j k n)"),
                               bank[1][:, :], ACT.Copy).then_inc(n1T_ready, 1)

            def copy_logit(g):
                act.wait_ge(logit_mm, g.n + 1)
                act.sem_inc(act_held, 1)
                act.activation(logit[:, ds(g.n * GT, GT), :].rearrange("p j e -> p (j e)"),
                               bank[7][:, 0:GT * E0], ACT.Copy).then_inc(logit_ready, 1)

            def route_exps(turn, k):
                act.wait_ge(route_exp, 6 * turn + 2 * k + 1)
                at, tiles = ROUTE_TURNS[turn][1:]
                act.activation(r_b[:, at:at + tiles, :], r_a[:, at:at + tiles, :], ACT.Exp
                               ).then_inc(route_exp, 1)

            def stage_a(nxt, cur, prev, last, route=None, early=None):
                def body(h, par):
                    g1, g, gp, gl = (At(h, par, d) for d in (1, 0, -1, -2))
                    if cur:
                        copy_tt(g, 1)
                    if last:
                        norm_x1(gl)
                    if early is not None:
                        route_exps(1, early)
                    if cur:
                        copy_v(g, 0)
                        copy_x(g)
                    if prev:
                        exp_w(gp)
                    if cur:
                        copy_tt(g, 2)
                        copy_v(g, 1)
                    if last:
                        copy_n1T(gl, 0)
                    if cur:
                        copy_tt(g, 3)
                    if last:
                        copy_n1T(gl, 1)
                    if nxt:
                        norm_x(g1)
                        mask_adj(g1)
                    if cur:
                        copy_v(g, 2)
                    if route is not None:
                        route_exps(0, route)
                    if cur:
                        copy_v(g, 3)
                    if nxt:
                        copy_tt(g1, 0)
                    if last:
                        copy_logit(gl)
                return body

            mask_adj(At(0, 0))
            norm_x(At(0, 0))
            copy_tt(At(0, 0), 0)
            straight(0, 1, stage_a(True, True, False, False))
            straight(1, 2, stage_a(True, True, True, False))
            straight(2, 4, stage_a(True, True, True, True))
            looped(act, 4, ROUTE_STEPS[0], stage_a(True, True, True, True))
            for k in range(3):
                straight(ROUTE_STEPS[k], ROUTE_STEPS[k] + 1, stage_a(True, True, True, True, k))
            straight(ROUTE_STEPS[3], ROUTE_STEPS[3] + 1, stage_a(True, True, True, True))
            straight(ROUTE_STEPS[3] + 1, GROUPS - 1, stage_a(True, True, True, True))
            straight(GROUPS - 1, GROUPS, stage_a(False, True, True, True))
            straight(GROUPS, GROUPS + 1, stage_a(False, False, True, True, early=0))
            straight(GROUPS + 1, GROUPS + 2, stage_a(False, False, False, True, early=1))
            route_exps(1, 2)
            for k in range(3):
                route_exps(2, k)

            for s in range(2):
                act.wait_ge(x1_out[s], 16 * GROUPS // 2)
                act.wait_ge(n1_out[s], 16 * GROUPS // 2)

            def gelu(i):
                act.wait_ge(w1_mm, i.n + 1)
                wait(act, h_done, i.n - 1)
                act.activation(g_sb[:, i.slot], bank[2 + i.slot][:, :], ACT.Gelu).then_inc(gelu_done, 1)

            def hi_h(i):
                act.wait_ge(hsT_mm, i.n + 1)
                wait(act, y_mm, i.n)
                act.activation(hsT_hi[:, i.slot], bank[0][:, :], ACT.Copy).then_inc(hsT_hi_ready, 1)

            def hi_x(i):
                act.wait_ge(xsT_mm, i.n + 1)
                wait(act, w3_mm, i.n - 1)
                act.activation(xsT_hi[:, i.slot], bank[1][:, 0:D], ACT.Copy).then_inc(xsT_hi_ready, 1)

            def stage_f(first, second, third):
                def body(h, par):
                    if third:
                        hi_h(At(h, par, -2))
                    if first:
                        hi_x(At(h, par))
                    if second:
                        gelu(At(h, par, -1))
                return body

            straight(0, 1, stage_f(True, False, False))
            straight(1, 2, stage_f(True, True, False))
            straight(2, 4, stage_f(True, True, True))
            looped(act, 4, ITEMS, stage_f(True, True, True))
            straight(ITEMS, ITEMS + 1, stage_f(False, True, True))
            straight(ITEMS + 1, ITEMS + 2, stage_f(False, False, True))
            def norm_x2(g):
                act.wait_ge(rstd3_done, g.n + 1)
                wait(act, a_mm[0], 2 * (g.n - 1))
                norm_rows(n2[:, g.slot], x2[:, g.slot], rstd1, shift1)[-1].then_inc(n2_done, 1)

            def norm_x3(g):
                act.wait_ge(rstd4_done, g.n + 1)
                wait(act, n3T_mm, 2 * g.n)
                norm_rows(n3, x3[:, g.slot], rstd2, shift2)[-1].then_inc(n3_done, 1)

            norm_x2(At(0, 0))
            for s in range(2):
                act.wait_ge(scattered[s], 2 * GT * 16 * GROUPS // 2)

            def copy_a(g, layer, pair):
                act.wait_ge(a_mm[layer], 2 * g.n + pair + 1)
                act.activation(hT[:, 2 * pair:2 * pair + 2].rearrange("p j k n -> p (j k n)"),
                               bank[pair][:, :], ACT.Copy).then_inc(a_ready[layer], 1)

            def relu(g, layer, pair):
                act.wait_ge(b_added[layer], 2 * g.n + pair + 1)
                act.activation(hrelu[:, 2 * pair:2 * pair + 2], hsum[:, 2 * pair:2 * pair + 2],
                               ACT.Relu).then_inc(relu_done[layer], 1)

            def copy_n3T(g, pair):
                act.wait_ge(n3T_mm, 2 * g.n + pair + 1)
                wait(act, out_mm, 2 * (g.n - 1) + pair + 1)
                wait(act, m_done, g.n)
                for b in range(2):
                    ins = act.activation(
                        n3z[:, 2 * pair:2 * pair + 2, :, b, b * NODES:(b + 1) * NODES],
                        bank[4 + pair].rearrange("p (j k n) -> p j k n", j=2, k=KD)
                        [:, :, :, b * NODES:(b + 1) * NODES], ACT.Copy)
                ins.then_inc(n3z_ready, 1)

            def exp_lg(g):
                act.wait_ge(gate_step, GATE_STEPS * g.n + EXP_AFTER)
                act.activation(lg_e[:, :], lg_k[:, :], ACT.Exp, accum_out=lg_s[:, 2:3]).then_inc(lg_exp, 1)

            def stage_c(nxt, cur, prev):
                def body(h, par):
                    g, gp = At(h, par), At(h, par, -1)
                    if cur:
                        copy_a(g, 0, 0)
                        copy_a(g, 0, 1)
                    if prev:
                        norm_x3(gp)
                    if cur:
                        relu(g, 0, 0)
                    if prev:
                        copy_n3T(gp, 0)
                    if cur:
                        relu(g, 0, 1)
                    if prev:
                        copy_n3T(gp, 1)
                    if cur:
                        copy_a(g, 1, 0)
                        copy_a(g, 1, 1)
                        relu(g, 1, 0)
                        relu(g, 1, 1)
                    if prev:
                        exp_lg(gp)
                    if cur:
                        copy_a(g, 2, 0)
                        copy_a(g, 2, 1)
                    if nxt:
                        norm_x2(At(h, par, 1))
                return body

            act.wait_ge(n3z_zeroed, 1)
            straight(0, 1, stage_c(True, True, False))
            straight(1, 4, stage_c(True, True, True))
            looped(act, 4, GROUPS - 2, stage_c(True, True, True))
            straight(GROUPS - 2, GROUPS - 1, stage_c(True, True, True))
            straight(GROUPS - 1, GROUPS, stage_c(False, True, True))
            straight(GROUPS, GROUPS + 1, stage_c(False, False, True))

        @blk.tensor
        def _(pe):
            pe.wait_ge(wqk_in, 16)
            pe.wait_ge(early_in, 16 * EARLY)
            for b in range(KD):
                for k in range(KD):
                    mm = pe.matmul(bank[b][:, 0:D], wqk_stage[:, 1, k, b * P:(b + 1) * P],
                                   wqk_stage[:, 0, k, :], start=(k == 0), stop=(k == KD - 1))
                mm.then_inc(mp_mm, 1)
            pe.wait_ge(mp_ready, 2)

            def adj_and_transposes(g, j):
                t = g.n * GT + j
                pe.wait_ge(adj_masked, t + 1)
                pe.wait_ge(xn_done, t + 1)
                wait(pe, tt_ready, t)
                for k in range(KD):
                    pe.matmul(bank[0][:, k * P:(k + 1) * P], xn[:, g.slot, j, k * P:(k + 1) * P],
                              adj_sb[:, g.slot, j], start=True, stop=True)
                for k in range(KD):
                    mm = pe.transpose(bank[0][:, D + k * P:D + (k + 1) * P],
                                      xn[:, g.slot, j, k * P:(k + 1) * P], ident)
                mm.then_inc(tt_mm, 1)

            def u_and_v(g, j):
                t = g.n * GT + j
                pe.wait_ge(tt_ready, t + 1)
                wait(pe, w_dot, t - 1)
                wait(pe, v_ready, t - 1)
                for k in range(KD):
                    pe.matmul(bank[2 + j % 2][:, 0:D], tt[:, j, 0, k], mp[:, k], start=(k == 0), stop=(k == KD - 1))
                for k in range(KD):
                    mm = pe.matmul(bank[4 + j % 2][:, 0:D], tt[:, j, 1, k], wv_sb[:, k],
                                   start=(k == 0), stop=(k == KD - 1))
                mm.then_inc(uv_mm, 1)

            def w_to_rows(g):
                pe.wait_ge(w_masked_done, g.n + 1)
                wait(pe, p_col_done, g.n)
                pe.matmul(bank[6][0:GT, 0:P], w_masked[:, :], ident, start=True, stop=True).then_inc(w_row, 1)

            def p_to_columns(g):
                pe.wait_ge(w_prob_done, g.n + 1)
                pe.matmul(bank[6][:, P:P + GT], w_prob[:, :, :].rearrange("j g n -> j (g n)"),
                          ident[0:GT, 0:GT], start=True, stop=True).then_inc(p_mm, 1)

            def n1_transposes(g, pair):
                pe.wait_ge(n1_done, g.n + 1)
                wait(pe, n1T_ready, 2 * g.n + pair)
                for j in range(2):
                    for k in range(KD):
                        mm = pe.transpose(bank[1][:, (j * KD + k) * P:(j * KD + k + 1) * P],
                                          n1[:, g.slot, 2 * pair + j, k * P:(k + 1) * P], ident)
                mm.then_inc(n1T_mm, 1)

            def logits(g):
                pe.wait_ge(n1T_ready, 2 * g.n + 2)
                wait(pe, logit_ready, g.n)
                for j in range(GT):
                    for k in range(KD):
                        mm = pe.matmul(bank[7][:, j * E0:(j + 1) * E0], n1T[:, j, k], wg0_sb[:, k],
                                       start=(k == 0), stop=(k == KD - 1))
                mm.then_inc(logit_mm, 1)

            def route_counts(part):
                pe.wait_ge(both_ready, part + 1)
                wait(pe, logit_ready, (ROUTE_STEPS[3] - 2, GROUPS)[part])
                n = PART_T[part] * E0
                a = both[:, 0:PART_T[part], :].rearrange("p t e -> p (t e)")
                pe.matmul(bank[7][:, 0:n], const_of("ones"), a, start=True, stop=True).then_inc(counts_mm, 1)

            def route_ranks(part):
                pe.wait_ge(counts_read, part + 1)
                n = PART_T[part] * E0
                a = both[:, 0:PART_T[part], :].rearrange("p t e -> p (t e)")
                pe.matmul(bank[7][:, 0:n], const_of("before"), a, start=True, stop=True).then_inc(ranks_mm, 1)

            def stage_a(nxt, cur, prev, last, route=False):
                def body(h, par):
                    g1, g, gp, gl = (At(h, par, d) for d in (1, 0, -1, -2))
                    if cur:
                        adj_and_transposes(g, 1)
                        u_and_v(g, 0)
                    if prev:
                        w_to_rows(gp)
                    if cur:
                        adj_and_transposes(g, 2)
                        u_and_v(g, 1)
                    if route:
                        route_counts(0)
                    if last:
                        n1_transposes(gl, 0)
                    if cur:
                        adj_and_transposes(g, 3)
                    if prev:
                        p_to_columns(gp)
                    if last:
                        n1_transposes(gl, 1)
                    if cur:
                        u_and_v(g, 2)
                        u_and_v(g, 3)
                    if route:
                        route_ranks(0)
                    if nxt:
                        adj_and_transposes(g1, 0)
                    if route:
                        pe.wait_ge(rank_read, 1)
                    if last:
                        logits(gl)
                return body

            adj_and_transposes(At(0, 0), 0)
            straight(0, 1, stage_a(True, True, False, False))
            straight(1, 2, stage_a(True, True, True, False))
            pe.wait_ge(consts_in, 16 * CONSTS)
            straight(2, 4, stage_a(True, True, True, True))
            looped(pe, 4, ROUTE_STEPS[3] - 1, stage_a(True, True, True, True))
            straight(ROUTE_STEPS[3] - 1, ROUTE_STEPS[3], stage_a(True, True, True, True))
            straight(ROUTE_STEPS[3], ROUTE_STEPS[3] + 1, stage_a(True, True, True, True, True))
            straight(ROUTE_STEPS[3] + 1, GROUPS - 1, stage_a(True, True, True, True))
            straight(GROUPS - 1, GROUPS, stage_a(False, True, True, True))
            straight(GROUPS, GROUPS + 1, stage_a(False, False, True, True))
            straight(GROUPS + 1, GROUPS + 2, stage_a(False, False, False, True))
            route_counts(1)
            route_ranks(1)
            pe.wait_ge(routed, 1)
            pe.sem_inc(y_mm, 1)

            def rows_transposes(i):
                pe.wait_ge(xs_in[i.slot], 16 * (i.used + 1))
                wait(pe, xsT_ready, i.n)
                for k in range(KD):
                    mm = pe.transpose(bank[1][:, k * P:(k + 1) * P], xs[:, i.slot, k * P:(k + 1) * P], ident)
                mm.then_inc(xsT_mm, 1)

            def three_passes(to, hi, lo, w_columns, depth):
                n = to.shape[1]
                for a, w in ((hi, w_hi), (hi, w_lo), (lo, w_hi)):
                    for k in range(depth):
                        mm = pe.matmul(to, a[:, k * P:(k + 1) * P], w[:, ds(w_columns + k * n, n)],
                                       start=(a is hi and w is w_hi and k == 0),
                                       stop=(a is lo and k == depth - 1))
                return mm

            def load_number(i):
                return pe.value_load(load_of[0:1, ds(i.n, 1)], min_val=1, max_val=LOADS)

            def place(load):
                return (load + 1) % 2 * WEIGHTS

            def up(i, load):
                pe.wait_ge(xsT_ready, i.n + 1)
                wait(pe, h_done, i.n - 1)
                for w, done in ((0, w1_mm), (1, w3_mm)):
                    three_passes(bank[2 + 2 * w + i.slot][:, :], xsT_hi[:, i.slot], xsT_lo[:, i.slot],
                                 place(load) + w * KD * F0, KD).then_inc(done, 1)

            def h_transposes(i):
                pe.wait_ge(h_done, i.n + 1)
                wait(pe, hsT_ready, i.n)
                for k in range(KF):
                    mm = pe.transpose(bank[0][:, k * P:(k + 1) * P], h_sb[:, i.slot, k * P:(k + 1) * P], ident)
                mm.then_inc(hsT_mm, 1)

            def down(i):
                load = load_number(i)
                pe.wait_ge(hsT_ready, i.n + 1)
                wait(pe, y_ready, i.n)
                three_passes(bank[6][:, 0:D], hsT_hi[:, i.slot], hsT_lo[:, i.slot],
                             place(load) + 2 * KD * F0, KF).then_inc(y_mm, 1)

            def stage_f(first, second, third):
                def body(h, par):
                    if second:
                        load = load_number(At(h, par, -1))
                        pe.wait_ge(w_ready, load)
                    if third:
                        h_transposes(At(h, par, -2))
                    if first:
                        rows_transposes(At(h, par))
                    if second:
                        up(At(h, par, -1), load)
                    if third:
                        down(At(h, par, -2))
                return body

            straight(0, 1, stage_f(True, False, False))
            straight(1, 2, stage_f(True, True, False))
            straight(2, 4, stage_f(True, True, True))
            looped(pe, 4, FI - 11, stage_f(True, True, True))
            pe.wait_ge(routed, 2)
            looped(pe, FI - 11, ITEMS, stage_f(True, True, True))
            straight(ITEMS, ITEMS + 1, stage_f(False, True, True))
            straight(ITEMS + 1, ITEMS + 2, stage_f(False, False, True))

            def times_adj(g, layer):
                for pair in range(2):
                    if layer == 0:
                        pe.wait_ge(n2_done, g.n + 1)
                        pe.wait_ge(adjc_in[g.slot], 32 * (g.used + 1))
                        src = n2[:, g.slot]
                        wait(pe, a_ready[2], 2 * (g.n - 1) + pair + 1)
                    else:
                        pe.wait_ge(relu_done[layer - 1], 2 * g.n + pair + 1)
                        src = hrelu
                        pe.wait_ge(a_ready[layer - 1], 2 * g.n + pair + 1)
                    for j in range(2):
                        for k in range(KD):
                            mm = pe.matmul(bank[pair][:, (j * KD + k) * P:(j * KD + k + 1) * P],
                                           src[:, 2 * pair + j, k * P:(k + 1) * P],
                                           adj_sb[:, g.slot, 2 * pair + j], start=True, stop=True)
                    mm.then_inc(a_mm[layer], 1)

            def times_w(g, layer, pairs=(0, 1)):
                for pair in pairs:
                    pe.wait_ge(a_ready[layer], 2 * g.n + pair + 1)
                    if layer == 0:
                        wait(pe, b_added[2], 2 * (g.n - 1) + pair + 1)
                    else:
                        pe.wait_ge(b_added[layer - 1], 2 * g.n + pair + 1)
                    for j in range(2):
                        for k in range(KD):
                            mm = pe.matmul(bank[2 + pair][:, j * D:(j + 1) * D], hT[:, 2 * pair + j, k],
                                           gw_sb[:, layer, k], start=(k == 0), stop=(k == KD - 1))
                    mm.then_inc(b_mm[layer], 1)

            def n3_transposes(g):
                for pair in range(2):
                    pe.wait_ge(n3_done, g.n + 1)
                    wait(pe, n3z_ready, 2 * g.n - 2 + pair + 1)
                    for j in range(2):
                        for k in range(KD):
                            mm = pe.transpose(bank[4 + pair][:, (j * KD + k) * P:(j * KD + k + 1) * P],
                                              n3[:, 2 * pair + j, k * P:(k + 1) * P], ident)
                    mm.then_inc(n3T_mm, 1)

            def graph_logits(g):
                pe.wait_ge(m_done, g.n + 1)
                for k in range(KD):
                    mm = pe.matmul(bank[4][0:2 * GT, 0:E1], m_T[:, k].rearrange("p j g -> p (j g)"), wg1_sb[:, k],
                                   start=(k == 0), stop=(k == KD - 1))
                mm.then_inc(lg_mm, 1)

            def spread_gate(g):
                pe.wait_ge(spread_done, g.n + 1)
                pe.matmul(bank[4][:, E1:E1 + 2 * GT], const_of("half_of", 2 * GT),
                          spread[:, :, :].rearrange("g a j -> g (a j)"), start=True, stop=True
                          ).then_inc(spread_mm, 1)

            def graph_expert(g, pair):
                pe.wait_ge(expert_ready, g.n + 1)
                wait(pe, ysum_done, 2 * (g.n - 1) + pair + 1)
                pe.sem_inc(pe_held, 1)
                for j in range(2):
                    for b in range(2):
                        e = pe.value_load(expert[b * NODES:b * NODES + 1, g.slot, 2 * pair + j:2 * pair + j + 1],
                                          min_val=0, max_val=E1 - 1)
                        for k in range(KD):
                            mm = pe.matmul(bank[6 + pair][:, j * D:(j + 1) * D], n3z[:, 2 * pair + j, k, b],
                                           we_sb[:, ds(e * (KD * D) + k * D, D)],
                                           start=(b == 0 and k == 0), stop=(b == 1 and k == KD - 1))
                mm.then_inc(out_mm, 1)

            def stage_c(cur, prev):
                def body(h, par):
                    g, gp = At(h, par), At(h, par, -1)
                    if cur:
                        times_adj(g, 0)
                        times_w(g, 0)
                    if prev:
                        n3_transposes(gp)
                    if cur:
                        times_adj(g, 1)
                        times_w(g, 1)
                    if prev:
                        graph_logits(gp)
                    if cur:
                        times_adj(g, 2)
                        times_w(g, 2, (0,))
                    if prev:
                        spread_gate(gp)
                    if cur:
                        times_w(g, 2, (1,))
                    if prev:
                        graph_expert(gp, 0)
                        graph_expert(gp, 1)
                return body

            straight(0, 1, stage_c(True, False))
            pe.wait_ge(we_in, 16 * E1)
            pe.wait_ge(y_ready, ITEMS)
            straight(1, 4, stage_c(True, True))
            looped(pe, 4, GROUPS, stage_c(True, True))
            straight(GROUPS, GROUPS + 1, stage_c(False, True))

        @blk.vector
        def _(dve):
            dve.wait_ge(early_in, 16 * EARLY)

            def norm_stats(g, src, st, st_sem, mv, mv_sem, used_sem, per=1):
                wait(dve, mv_sem, g.n)
                for j in range(GT):
                    ins = dve.bn_stats(st[:, j], src[:, j])
                ins.then_inc(st_sem, 1)
                dve.wait_ge(st_sem, g.n + 1)
                wait(dve, used_sem, per * g.n)
                dve.sem_inc(dve_held, 1)
                for j in range(GT):
                    ins = dve.bn_aggr(mv[:, j], st[:, j])
                ins.then_inc(mv_sem, 1)

            def stats_x(g):
                dve.wait_ge(xin_in[g.slot], 16 * (g.used + 1))
                norm_stats(g, xin[:, g.slot], st1, st1_done, mv1, mv1_done, xn_done, GT)

            def dot_w(g, j):
                dve.wait_ge(uv_mm, g.n * GT + j + 1)
                u = bank[2 + j % 2][:, 0:D]
                dve.tensor_tensor_reduce(u, u, xn[:, g.slot, j], ATT_SCALE, 0.0, ALU.mult, ALU.add,
                                         w_col[:, g.slot, j:j + 1]).then_inc(w_dot, 1)

            def mask_w(g):
                dve.wait_ge(w_dot, GT * (g.n + 1))
                dve.tensor_tensor(w_masked[:, :], w_col[:, g.slot], mask[:, ds(g.n * GT, GT)], ALU.mult
                                  ).then_inc(w_masked_done, 1)

            def sub_max(g):
                rows = bank[6][0:GT, 0:P].rearrange("j (g n) -> j g n", g=2)
                dve.wait_ge(w_row, g.n + 1)
                dve.tensor_reduce(w_max[:, :], rows, AX.X, ALU.max).then_inc(w_max_done, 1)
                dve.wait_ge(w_max_done, g.n + 1)
                dve.tensor_tensor(w_sub[:, :, :], rows, w_max[:, :].unsqueeze(2).to_broadcast([GT, 2, NODES]),
                                  ALU.subtract).then_inc(w_sub_done, 1)

            def prob(g):
                dve.wait_ge(w_exp_done, g.n + 1)
                dve.tensor_reduce(w_sum[:, :], w_exp[:, :, :], AX.X, ALU.add).then_inc(w_sum_done, 1)
                dve.wait_ge(w_sum_done, g.n + 1)
                dve.reciprocal(w_rcp[:, :], w_sum[:, :]).then_inc(w_rcp_done, 1)
                dve.wait_ge(w_rcp_done, g.n + 1)
                dve.tensor_tensor(w_prob[:, :, :], w_exp[:, :, :],
                                  w_rcp[:, :].unsqueeze(2).to_broadcast([GT, 2, NODES]), ALU.mult
                                  ).then_inc(w_prob_done, 1)

            def add_x1(g):
                dve.wait_ge(p_mm, g.n + 1)
                wait(dve, x1_done, g.n)
                dve.tensor_copy(p_col[:, :], bank[6][:, P:P + GT]).then_inc(p_col_done, 1)
                dve.wait_ge(p_col_done, g.n + 1)
                dve.wait_ge(v_ready, GT * (g.n + 1))
                dve.wait_ge(x_copied, g.n + 1)
                for j in range(GT):
                    ins = dve.scalar_tensor_tensor(out=x1[:, g.slot, j], in0=v_sb[:, g.slot, j],
                                                   scalar=p_col[:, j:j + 1], in1=x1[:, g.slot, j],
                                                   op0=ALU.mult, op1=ALU.add)
                ins.then_inc(x1_done, 1)

            def stats_x1(g):
                dve.wait_ge(x1_done, g.n + 1)
                norm_stats(g, x1[:, g.slot], st2, st2_done, mv2, mv2_done, n1_done)

            steps = [0]

            def step(ins):
                steps[0] += 1
                ins.then_inc(route_step, 1)
                dve.wait_ge(route_step, steps[0])

            def exp_on_act(turn, k):
                dve.sem_inc(route_exp, 1)
                dve.wait_ge(route_exp, 6 * turn + 2 * k + 2)

            class Route:

                def __init__(self, part, turn=None):
                    self.part, self.turn = part, turn
                    self.t0, at, self.T = (PART_T0[part], 0, PART_T[part]) if turn is None else ROUTE_TURNS[turn]
                    self.at = slice(at, at + self.T)
                    self.a, self.b, self.c, self.p, self.both = (
                        v[:, self.at, :] for v in (r_a, r_b, r_c, r_p, both))
                    self.pick = [pick[:, c, self.at, :] for c in range(2)]
                    self.k = r_k[:, self.at]

                def over_e(self, v):
                    return v.unsqueeze(2).to_broadcast([P, self.T, E0])

                def over_t(self, v):
                    return v.unsqueeze(1).to_broadcast([P, self.T, E0])

                def scores(self):
                    dve.wait_ge(logit_ready, (self.t0 + self.T) // GT)
                    dve.wait_ge(consts_in, 16 * CONSTS)
                    step(dve.tensor_tensor(self.c, logit[:, self.t0:self.t0 + self.T, :],
                                           self.over_t(bg0_sb[:, :]), ALU.add))
                    step(dve.tensor_reduce(self.k, self.c, AX.X, ALU.max))
                    step(dve.tensor_tensor(self.a, self.c, self.over_e(self.k), ALU.subtract))
                    exp_on_act(self.turn, 0)
                    step(dve.tensor_reduce(self.k, self.b, AX.X, ALU.add))
                    step(dve.reciprocal(self.k, self.k))
                    step(dve.tensor_tensor(self.p, self.b, self.over_e(self.k), ALU.mult))

                def choice(self, c):
                    if c == 0:
                        s = self.p
                    else:
                        step(dve.scalar_tensor_tensor(out=self.c, in0=self.pick[0], scalar=-4.0,
                                                      in1=self.p, op0=ALU.mult, op1=ALU.add))
                        s = self.c
                    mx = top[:, c, self.at]
                    step(dve.tensor_reduce(mx, s, AX.X, ALU.max))
                    step(dve.tensor_tensor(self.a, s, self.over_e(mx), ALU.is_ge))
                    step(dve.tensor_tensor(self.a, self.a, self.over_t(const_of("rev0")), ALU.mult))
                    step(dve.tensor_reduce(self.k, self.a, AX.X, ALU.max))
                    step(dve.tensor_tensor(self.pick[c], self.a, self.over_e(self.k), ALU.is_ge))
                    step(dve.tensor_tensor(self.a, self.p, self.over_e(mx), ALU.subtract))
                    exp_on_act(self.turn, 1 + c)
                    step(dve.tensor_tensor(self.both, self.p, self.over_e(mx), ALU.max))
                    step(dve.scalar_tensor_tensor(out=self.c, in0=self.both, scalar=JITTER2,
                                                  in1=self.a, op0=ALU.mult, op1=ALU.add))
                    step(dve.scalar_tensor_tensor(out=self.b, in0=self.c, scalar=0.0,
                                                  in1=self.b, op0=ALU.is_ge, op1=ALU.mult))
                    if c == 1:
                        step(dve.tensor_scalar(self.c, self.pick[0], -1.0, 1.0, ALU.mult, ALU.add))
                        step(dve.tensor_tensor(self.b, self.b, self.c, ALU.mult))
                    step(dve.tensor_reduce(self.k, self.b, AX.X, ALU.add))
                    step(dve.reciprocal(weight[:, self.t0:self.t0 + self.T, c], self.k))
                    if c == 1:
                        step(dve.tensor_tensor(self.both, self.pick[0], self.pick[1], ALU.add))

                def by_e(self, v):
                    return self.flat(v).rearrange("p (e t) -> p e t", e=E0)

                def flat(self, v):
                    return v.rearrange("p t e -> p (t e)")

                def counts(self):
                    n = self.T * E0
                    dve.wait_ge(counts_mm, self.part + 1)
                    step(dve.tensor_copy(self.by_e(self.a), bank[7][:, 0:n].rearrange("p (t e) -> p e t", e=E0)))
                    dve.sem_inc(counts_read, 1)
                    step(dve.tensor_tensor_scan(self.flat(self.b), const_of(f"restart{self.part}"),
                                                self.flat(self.a), 0.0, ALU.mult, ALU.add))
                    count = self.by_e(self.b)[:, :, self.T - 1]
                    step(dve.tensor_scalar(n_f[:, :], count, float(P - 1), None, ALU.add))
                    step(dve.tensor_copy(n_i[:, :], n_f[:, :]))
                    step(dve.tensor_scalar(n_i[:, :], n_i[:, :], 7, 7, ALU.logical_shift_right,
                                           ALU.logical_shift_left))
                    step(dve.tensor_copy(n_f[:, :], n_i[:, :]))
                    step(dve.tensor_tensor_scan(n_end[:, :], const_of("ones")[:, 0:E0], n_f[:, :], 0.0,
                                                ALU.mult, ALU.add))
                    step(dve.tensor_tensor(n_base[:, :], n_end[:, :], n_f[:, :], ALU.subtract))
                    spare = const_of(f"spare{self.part}")
                    step(dve.scalar_tensor_tensor(out=pad_f[:, :], in0=count, scalar=const_of("row"),
                                                  in1=n_base[:, :], op0=ALU.add, op1=ALU.add))
                    step(dve.tensor_tensor(pad_ok[:, :], n_end[:, :], pad_f[:, :], ALU.is_gt))
                    step(dve.tensor_tensor(pad_f[:, :], pad_f[:, :], spare, ALU.subtract))
                    step(dve.tensor_tensor(pad_f[:, :], pad_f[:, :], pad_ok[:, :], ALU.mult))
                    step(dve.tensor_tensor(pad_i[:, self.part], pad_f[:, :], spare, ALU.add))
                    step(dve.tensor_tensor(self.flat(self.b), self.flat(self.b), self.flat(self.a), ALU.subtract))

                def places(self):
                    n, items = self.T * E0, PART_ITEMS[self.part]
                    row = self.by_e(self.b)
                    dve.wait_ge(ranks_mm, self.part + 1)
                    step(dve.tensor_tensor(row, row, bank[7][:, 0:n].rearrange("p (t e) -> p e t", e=E0), ALU.add))
                    dve.sem_inc(rank_read, 1)
                    step(dve.tensor_tensor(row, row, n_base[:, :].unsqueeze(2).to_broadcast([P, E0, self.T]),
                                           ALU.add))
                    for c in range(2):
                        step(dve.tensor_tensor(self.c, self.pick[c], row.rearrange("p e t -> p t e"), ALU.mult))
                        step(dve.tensor_reduce(slot_f[:, 0:self.T], self.c, AX.X, ALU.add))
                        step(dve.tensor_copy(slot_i[:, self.t0:self.t0 + self.T, c], slot_f[:, 0:self.T]))
                    step(dve.tensor_tensor(tile_e[:, 0:items, :],
                                           const_of("tile_start", 1)[:, 0:items].unsqueeze(2)
                                           .to_broadcast([1, items, E0]),
                                           n_end[0:1, :].unsqueeze(1).to_broadcast([1, items, E0]), ALU.is_ge))
                    step(dve.tensor_reduce(tile_ef[:, 0:items], tile_e[:, 0:items, :], AX.X, ALU.add))
                    at = self.part * FI
                    step(dve.tensor_scalar(load_of[:, at:at + items], tile_ef[:, 0:items], float(E0 - 1),
                                           float(self.part * E0 + 1), ALU.min, ALU.add))
                    step(dve.tensor_scalar(n_used[:, :], n_end[0:1, :], 1.0 / P, float(at + 1), ALU.mult, ALU.add))
                    dve.tensor_tensor(used_at[:, self.part * E0:(self.part + 1) * E0], n_used[:, :],
                                      const_of(f"last{self.part}", 1), ALU.max).then_inc(routed, 1)

            route0, early1, late1 = Route(0, 0), Route(1, 1), Route(1, 2)
            all0, all1 = Route(0), Route(1)

            def stage_a(nxt, cur, prev, route=None, early=False):
                def body(h, par):
                    g1, g, gp = (At(h, par, d) for d in (1, 0, -1))
                    if prev:
                        mask_w(gp)
                    if early:
                        early1.scores()
                    if prev:
                        sub_max(gp)
                    if nxt:
                        stats_x(g1)
                    if cur:
                        dot_w(g, 0)
                    if prev:
                        prob(gp)
                    if cur:
                        dot_w(g, 1)
                    if prev:
                        add_x1(gp)
                    if cur:
                        dot_w(g, 2)
                    if route == 0:
                        route0.scores()
                    elif route in (1, 2):
                        route0.choice(route - 1)
                    if route == 2:
                        dve.sem_inc(both_ready, 1)
                    elif route == 3:
                        all0.counts()
                    if prev:
                        stats_x1(gp)
                    if cur:
                        dot_w(g, 3)
                    if route == 3:
                        all0.places()
                return body

            stats_x(At(0, 0))
            straight(0, 1, stage_a(True, True, False))
            straight(1, 4, stage_a(True, True, True))
            looped(dve, 4, ROUTE_STEPS[0], stage_a(True, True, True))
            for k in range(4):
                straight(ROUTE_STEPS[k], ROUTE_STEPS[k] + 1, stage_a(True, True, True, k))
            straight(ROUTE_STEPS[3] + 1, GROUPS - 1, stage_a(True, True, True))
            straight(GROUPS - 1, GROUPS, stage_a(False, True, True))
            straight(GROUPS, GROUPS + 1, stage_a(False, False, True, early=True))
            early1.choice(0)
            early1.choice(1)
            late1.scores()
            late1.choice(0)
            late1.choice(1)
            dve.sem_inc(both_ready, 1)

            for s in range(2):
                dve.wait_ge(x1_out[s], 16 * GROUPS // 2)
                dve.wait_ge(n1_out[s], 16 * GROUPS // 2)
            all1.counts()

            def add_x2(g, c):
                if c == 0:
                    dve.wait_ge(x2_in[g.slot], 16 * (g.used + 1))
                    dve.wait_ge(yg_in[g.slot], 2 * GT * 16 * (g.used + 1))
                else:
                    dve.wait_ge(half_sum, g.n + 1)
                for j in range(GT):
                    ins = dve.scalar_tensor_tensor(
                        out=x2[:, g.slot, j], in0=yg[:, g.slot, j, c],
                        scalar=weight[:, ds(g.n * GT + j, 1), c],
                        in1=x2[:, g.slot, j], op0=ALU.mult, op1=ALU.add)
                ins.then_inc((half_sum, x2_done)[c], 1)

            def stats_x2(g):
                dve.wait_ge(x2_done, g.n + 1)
                norm_stats(g, x2[:, g.slot], st1, st3_done, mv1, mv3_done, n2_done)

            def lo_x(i):
                dve.wait_ge(xsT_hi_ready, i.n + 1)
                dve.tensor_tensor(xsT_lo[:, i.slot], bank[1][:, 0:D], xsT_hi[:, i.slot].bitcast(F32),
                                  ALU.subtract).then_inc(xsT_ready, 1)

            def lo_h(i):
                dve.wait_ge(hsT_hi_ready, i.n + 1)
                dve.tensor_tensor(hsT_lo[:, i.slot], bank[0][:, :], hsT_hi[:, i.slot].bitcast(F32),
                                  ALU.subtract).then_inc(hsT_ready, 1)

            def mul_h(i):
                dve.wait_ge(gelu_done, i.n + 1)
                dve.wait_ge(w3_mm, i.n + 1)
                wait(dve, hsT_mm, i.n - 1)
                dve.tensor_tensor(h_sb[:, i.slot], bank[4 + i.slot][:, :], g_sb[:, i.slot], ALU.mult
                                  ).then_inc(h_done, 1)

            def copy_y(i):
                dve.wait_ge(y_mm, i.n + 2)
                wait(dve, ys_out[i.slot], 16 * i.used)
                dve.tensor_copy(y_sb[:, i.slot], bank[6][:, 0:D]).then_inc(y_ready, 1)

            def stage_f(first, second, third):
                def body(h, par):
                    if third:
                        lo_h(At(h, par, -2))
                    if first:
                        lo_x(At(h, par))
                    if second:
                        mul_h(At(h, par, -1))
                    if third:
                        copy_y(At(h, par, -2))
                return body

            straight(0, 1, stage_f(True, False, False))
            all1.places()
            straight(1, 2, stage_f(True, True, False))
            straight(2, 8, stage_f(True, True, True))
            looped(dve, 8, X2_AT, stage_f(True, True, True))
            add_x2(At(0, 0), 0)
            add_x2(At(0, 0), 1)
            looped(dve, X2_AT, X2_AT + 2, stage_f(True, True, True))
            stats_x2(At(0, 0))
            looped(dve, X2_AT + 2, ITEMS, stage_f(True, True, True))
            straight(ITEMS, ITEMS + 1, stage_f(False, True, True))
            straight(ITEMS + 1, ITEMS + 2, stage_f(False, False, True))

            def add_bias(g, layer):
                for pair in range(2):
                    part = hsum[:, 2 * pair:2 * pair + 2]
                    dve.wait_ge(b_mm[layer], 2 * g.n + pair + 1)
                    if layer:
                        dve.wait_ge(relu_done[layer - 1], 2 * g.n + pair + 1)
                    else:
                        wait(dve, x3_done, g.n)
                    dve.tensor_tensor(part, bank[2 + pair].rearrange("p (j n) -> p j n", j=2),
                                      gb_sb[:, layer].unsqueeze(1).to_broadcast([P, 2, D]), ALU.add
                                      ).then_inc(b_added[layer], 1)

            def add_x3(g):
                dve.wait_ge(b_added[2], 2 * g.n + 2)
                wait(dve, out_done, g.n - 1)
                dve.tensor_tensor(x3[:, g.slot].rearrange("p j n -> p (j n)"),
                                  hsum.rearrange("p j n -> p (j n)"),
                                  x2[:, g.slot].rearrange("p j n -> p (j n)"), ALU.add).then_inc(x3_done, 1)

            def stats_x3(g):
                dve.wait_ge(x3_done, g.n + 1)
                norm_stats(g, x3[:, g.slot], st2, st4_done, mv2, mv4_done, n3_done)

            def graph_sum(g):
                dve.wait_ge(n3z_ready, 2 * g.n + 2)
                wait(dve, lg_mm, g.n)
                for b in range(2):
                    ins = dve.tensor_reduce(
                        m_T[:, :, :, b].rearrange("p k j -> p j k"),
                        n3z[:, :, :, b, b * NODES:(b + 1) * NODES], AX.X, ALU.add)
                ins.then_inc(m_done, 1)

            def graph_gate(g):
                at = [0]

                def link(ins):
                    at[0] += 1
                    ins.then_inc(gate_step, 1)
                    dve.wait_ge(gate_step, GATE_STEPS * g.n + at[0])

                dve.wait_ge(lg_mm, g.n + 1)
                link(dve.scalar_tensor_tensor(out=lg[:, :], in0=bank[4][0:2 * GT, 0:E1], scalar=1.0 / NODES,
                                              in1=bg1_sb[:, :], op0=ALU.mult, op1=ALU.add))
                link(dve.tensor_reduce(lg_s[:, 0:1], lg[:, :], AX.X, ALU.max))
                link(dve.tensor_scalar(lg_k[:, :], lg[:, :], lg_s[:, 0:1], None, ALU.subtract))
                link(dve.tensor_scalar(lg[:, :], lg[:, :], lg_s[:, 0:1], None, ALU.is_ge))
                link(dve.tensor_tensor(lg[:, :], lg[:, :], const_of("rev1", 2 * GT), ALU.mult))
                link(dve.tensor_reduce(lg_s[:, 1:2], lg[:, :], AX.X, ALU.max))
                link(dve.tensor_scalar(lg_s[:, 1:2], lg_s[:, 1:2], -1.0, float(E1), ALU.mult, ALU.add))
                dve.wait_ge(lg_exp, g.n + 1)
                link(dve.reciprocal(lg_s[:, 3:4], lg_s[:, 2:3]))
                link(dve.tensor_scalar(spread[:, 0], const_of("own_tile", 2 * GT), lg_s[:, 3:4], None, ALU.mult))
                link(dve.tensor_scalar(spread[:, 1], const_of("own_tile", 2 * GT), lg_s[:, 1:2], None, ALU.mult))
                assert at[0] == GATE_STEPS
                dve.sem_inc(spread_done, 1)

            def take_gate(g):
                dve.wait_ge(spread_mm, g.n + 1)
                wait(dve, out_done, g.n - 1)
                wait(dve, beg_in[g.slot], GT * 16 * g.used)
                dve.tensor_copy(gate[:, g.slot], bank[4][:, E1:E1 + GT])
                dve.tensor_copy(expert[:, g.slot], bank[4][:, E1 + GT:E1 + 2 * GT]).then_inc(expert_ready, 1)

            def finish(g):
                dve.wait_ge(beg_in[g.slot], GT * 16 * (g.used + 1))
                wait(dve, out_out, 16 * g.n)
                for pair in range(2):
                    dve.wait_ge(out_mm, 2 * g.n + pair + 1)
                    dve.tensor_tensor(outc[:, 2 * pair:2 * pair + 2].rearrange("p j n -> p (j n)"),
                                      bank[6 + pair][:, :],
                                      beg[:, 2 * pair:2 * pair + 2].rearrange("p j n -> p (j n)"),
                                      ALU.add).then_inc(ysum_done, 1)
                dve.wait_ge(ysum_done, 2 * g.n + 2)
                for j in range(GT):
                    ins = dve.scalar_tensor_tensor(out=outc[:, j], in0=outc[:, j],
                                                   scalar=gate[:, g.slot, j:j + 1], in1=x3[:, g.slot, j],
                                                   op0=ALU.mult, op1=ALU.add)
                ins.then_inc(out_done, 1)

            def stage_c(nxt, cur, prev):
                def body(h, par):
                    g1, g, gp = (At(h, par, d) for d in (1, 0, -1))
                    if cur:
                        add_bias(g, 0)
                    if nxt:
                        add_x2(g1, 0)
                    if prev:
                        graph_sum(gp)
                    if cur:
                        add_bias(g, 1)
                    if prev:
                        graph_gate(gp)
                    if nxt:
                        add_x2(g1, 1)
                    if prev:
                        take_gate(gp)
                    elif nxt:
                        stats_x2(g1)
                    if cur:
                        add_bias(g, 2)
                    if nxt and prev:
                        stats_x2(g1)
                    if cur:
                        add_x3(g)
                        stats_x3(g)
                    if prev:
                        finish(gp)
                return body

            dve.wait_ge(w_ready, LOADS)
            for s in range(2):
                dve.wait_ge(ys_out[s], 16 * ITEMS // 2)
                dve.wait_ge(scattered[s], 2 * GT * 16 * GROUPS // 2)
            straight(0, 1, stage_c(True, True, False))
            straight(1, 4, stage_c(True, True, True))
            looped(dve, 4, GROUPS - 2, stage_c(True, True, True))
            straight(GROUPS - 2, GROUPS - 1, stage_c(True, True, True))
            straight(GROUPS - 1, GROUPS, stage_c(False, True, True))
            straight(GROUPS, GROUPS + 1, stage_c(False, False, True))


def shape_constants():
    import numpy as np

    c = np.zeros((P, CONST_COLS), np.float32)
    i = np.arange(P)

    def put(name, value):
        n, at = CONST[name]
        c[:, at:at + n] = value

    put("ident", i[:, None] == i[None, :])
    put("before", i[:, None] < i[None, :])
    put("ones", 1.0)
    put("half_of", (i[:, None] % 2) == (i[None, :] // NODES))
    put("own_tile", (i[:, None] // 2) == np.arange(GT)[None, :])
    put("rev0", E0 - np.arange(E0))
    put("rev1", E1 - np.arange(E1))
    for part in range(2):
        put(f"restart{part}", np.arange(E0 * PART_T[part]) % PART_T[part] != 0)
        put(f"last{part}", (np.arange(E0) == E0 - 1) * (1 + sum(PART_ITEMS[0:part + 1])))
        put(f"spare{part}", P * (PART_ITEMS[part] + np.arange(SPARE))[None, :] + i[:, None])
    put("tile_start", P * np.arange(max(PART_ITEMS)))
    put("row", i[:, None])
    put("eps", EPS)
    put("minus_half", -0.5)
    put("minus_one", -1.0)
    return c


def kernel(x, adj, nodemask, L0_gnn_Wqk, L0_gnn_Wv, L0_ffn_wg, L0_ffn_bg, L0_ffn_w1, L0_ffn_w3, L0_ffn_w2,
           L1_gnn_W1, L1_gnn_b1, L1_gnn_W2, L1_gnn_b2, L1_gnn_W3, L1_gnn_b3, L1_ffn_Wg, L1_ffn_bg, L1_ffn_We,
           L1_ffn_be):
    import numpy as np
    import concourse.bacc as bacc
    from concourse.bass_utils import run_bass_kernel_spmd

    nc = bacc.Bacc("TRN2", target_bir_lowering=False, num_devices=1)
    arrays = {}

    def give(name, a):
        a = np.ascontiguousarray(a)
        arrays[name] = a
        return nc.dram_tensor(name, a.shape, mybir.dt.from_np(a.dtype), kind="ExternalInput").ap()

    def row(a):
        return np.asarray(a)

    args = dict(
        x=give("in_x", np.asarray(x).reshape(TOKENS, D)),
        adjT=give("in_adjT", np.asarray(adj).transpose(0, 2, 1)),
        maskT=give("in_maskT", np.asarray(nodemask).reshape(TILES, P).T),
        wqkT=give("in_wqkT", np.asarray(L0_gnn_Wqk).T),
        wv=give("in_wv", L0_gnn_Wv),
        wg0=give("in_wg0", L0_ffn_wg), bg0=give("in_bg0", row(L0_ffn_bg)),
        w1=give("in_w1", L0_ffn_w1), w3=give("in_w3", L0_ffn_w3), w2=give("in_w2", L0_ffn_w2),
        gw=[give(f"in_gw{i}", w) for i, w in enumerate((L1_gnn_W1, L1_gnn_W2, L1_gnn_W3))],
        gb=[give(f"in_gb{i}", row(b)) for i, b in enumerate((L1_gnn_b1, L1_gnn_b2, L1_gnn_b3))],
        wg1=give("in_wg1", L1_ffn_Wg), bg1=give("in_bg1", row(L1_ffn_bg)),
        we=give("in_we", L1_ffn_We), be=give("in_be", L1_ffn_be),
        const=give("in_const", shape_constants()),
    )
    out = nc.dram_tensor("out", (TOKENS, D), F32, kind="ExternalOutput").ap()
    program(nc, out=out, **args)
    r = run_bass_kernel_spmd(nc, [arrays], core_ids=[0])
    return r.results[0]["out"].reshape(GRAPHS, NODES, D)
```
